# Optimizing a Trainium2 kernel written in Bass

```python
import numpy as np
import jax
import jax.numpy as jnp

def _softmax(x, axis=-1):
    return jax.nn.softmax(x, axis=axis)
def _gelu(x):
    return jax.nn.gelu(x, approximate=True)
def _silu(x):
    return jax.nn.silu(x)
def _sigmoid(x):
    return jax.nn.sigmoid(x)
def _layernorm(x, axis=-1, eps=1e-5):
    m = jnp.mean(x, axis=axis, keepdims=True)
    v = jnp.var(x, axis=axis, keepdims=True)
    return (x - m) / jnp.sqrt(v + eps)
def _scatter_add(tgt, idx, src, axis=0):
    return tgt.at[idx].add(src)
def _segment_sum(src, seg, n):
    return jax.ops.segment_sum(src, seg, n)

kernel_name = 'mk_vit_tower_cls_d1_tok_img256_0c0ded'

def setup_inputs(seed: int = 0):
    np.random.seed(seed)
    _w = jnp.asarray
    def _rec_inputs():
        import jax
        import jax.numpy as jnp
        _rk = jax.random.key(seed)
        x = (-0.000209053 + 0.999977 * jax.random.normal(jax.random.fold_in(_rk, 1), (16, 256, 56, 56), jnp.float32))
        cls_tok = 0.02 * jax.random.normal(jax.random.fold_in(_rk, 5), (1, 1, 256), jnp.float32)
        return x, cls_tok
    x, cls_tok = _rec_inputs()
    def _L0_tok_setup():
        import jax, jax.numpy as jnp
        import numpy as np
        B, EMB, HT, WD = (32, 256, 56, 56)
        NH, WS, SHIFTED = (8, 4, True)

        def _rel_indices(ws):
            coords = np.array([[i, j] for i in range(ws) for j in range(ws)])
            rel = coords[None, :, :] - coords[:, None, :] + ws - 1
            return jnp.asarray(rel)

        def _shift_masks(ws):
            m = np.zeros((ws * ws, ws * ws), np.float32)
            s = ws * (ws // 2)
            m[-s:, :-s] = -np.inf
            m[:-s, -s:] = -np.inf
            col = m.reshape(ws, ws, ws, ws).transpose(1, 0, 3, 2).reshape(ws * ws, ws * ws)
            return (jnp.asarray(m), jnp.asarray(col))
        key = jax.random.key(seed)
        ks = jax.random.split(key, 6)
        x = jax.random.normal(ks[0], (B, EMB, HT, WD), jnp.float32)
        s = 1.0 / np.sqrt(EMB)
        w1 = jax.random.uniform(ks[1], (3 * EMB, EMB), jnp.float32, -s, s)
        b1 = jax.random.uniform(ks[2], (3 * EMB,), jnp.float32, -s, s)
        w2 = jax.random.uniform(ks[3], (EMB, EMB), jnp.float32, -s, s)
        b2 = jax.random.uniform(ks[4], (EMB,), jnp.float32, -s, s)
        pos_emb = jax.random.normal(ks[5], (2 * WS - 1, 2 * WS - 1), jnp.float32)
        return {'x': x, 'w1': w1, 'b1': b1, 'w2': w2, 'b2': b2, 'pos_emb': pos_emb}
    _L0_tok_all = _L0_tok_setup()
    _L0_tok_in = {k: v for k, v in _L0_tok_all.items() if k in ('w1', 'b1', 'w2', 'b2', 'pos_emb', )}
    del _L0_tok_all

    def _L0_attn_setup():
        import jax, jax.numpy as jnp
        import numpy as np
        DIM = 256
        HEADS = 4
        DIM_HEAD = 32
        NUM_MEM = 4
        HIDDEN = HEADS * DIM_HEAD
        SCALE = DIM_HEAD ** (-0.5)

        def rmsnorm(x, g):
            n = jnp.linalg.norm(x, axis=-1, keepdims=True)
            return x / jnp.maximum(n, 1e-12) * g * x.shape[-1] ** 0.5
        key = jax.random.key(seed)
        ks = jax.random.split(key, 8)
        B, N = (4, 16384)
        return {'x': jax.random.normal(ks[0], (B, N, DIM), jnp.float32), 't': jax.random.normal(ks[1], (B,), jnp.float32), 'w_qkv': jax.random.normal(ks[2], (DIM, 3 * HIDDEN), jnp.float32) * 0.02, 'mem_kv': jax.random.normal(ks[3], (2, HEADS, DIM_HEAD, NUM_MEM), jnp.float32), 'w_out': jax.random.normal(ks[4], (HIDDEN, DIM), jnp.float32) * 0.02, 'b_out': jnp.zeros((DIM,), jnp.float32), 'g_out': jnp.ones((DIM,), jnp.float32), 'g_pre': jnp.ones((DIM,), jnp.float32)}
    _L0_attn_all = _L0_attn_setup()
    _L0_attn_in = {k: v for k, v in _L0_attn_all.items() if k in ('t', 'w_qkv', 'mem_kv', 'w_out', 'b_out', 'g_out', 'g_pre', )}
    del _L0_attn_all

    def _L0_ffn_setup():
        import jax, jax.numpy as jnp
        import numpy as np
        B, S, D = (8, 4096, 256)
        H = 4 * D
        CAPACITY = 0.5
        key = jax.random.key(seed)
        ks = jax.random.split(key, 6)
        x = jax.random.normal(ks[0], (B, S, D), dtype=jnp.float32)
        attention_mask = jnp.zeros((B, 1, 1, S), dtype=jnp.float32)
        wr = jax.random.normal(ks[1], (D, 1), dtype=jnp.float32) * 0.02
        br = jnp.zeros((1,), dtype=jnp.float32)
        w1 = jax.random.normal(ks[2], (D, H), dtype=jnp.float32) * 0.02
        b1 = jnp.zeros((H,), dtype=jnp.float32)
        w2 = jax.random.normal(ks[3], (H, D), dtype=jnp.float32) * 0.02
        b2 = jnp.zeros((D,), dtype=jnp.float32)
        return {'x': x, 'attention_mask': attention_mask, 'wr': wr, 'br': br, 'w1': w1, 'b1': b1, 'w2': w2, 'b2': b2}
    _L0_ffn_all = _L0_ffn_setup()
    _L0_ffn_in = {k: v for k, v in _L0_ffn_all.items() if k in ('attention_mask', 'wr', 'br', 'w1', 'b1', 'w2', 'b2', )}
    del _L0_ffn_all

    return {
        "x": x,
        "cls_tok": cls_tok,
        "L0_tok_w1": _L0_tok_in["w1"],
        "L0_tok_b1": _L0_tok_in["b1"],
        "L0_tok_w2": _L0_tok_in["w2"],
        "L0_tok_b2": _L0_tok_in["b2"],
        "L0_tok_pos_emb": _L0_tok_in["pos_emb"],
        "L0_attn_t": _L0_attn_in["t"],
        "L0_attn_w_qkv": _L0_attn_in["w_qkv"],
        "L0_attn_mem_kv": _L0_attn_in["mem_kv"],
        "L0_attn_w_out": _L0_attn_in["w_out"],
        "L0_attn_b_out": _L0_attn_in["b_out"],
        "L0_attn_g_out": _L0_attn_in["g_out"],
        "L0_attn_g_pre": _L0_attn_in["g_pre"],
        "L0_ffn_attention_mask": _L0_ffn_in["attention_mask"],
        "L0_ffn_wr": _L0_ffn_in["wr"],
        "L0_ffn_br": _L0_ffn_in["br"],
        "L0_ffn_w1": _L0_ffn_in["w1"],
        "L0_ffn_b1": _L0_ffn_in["b1"],
        "L0_ffn_w2": _L0_ffn_in["w2"],
        "L0_ffn_b2": _L0_ffn_in["b2"],
    }

def reference(x, cls_tok, L0_tok_w1, L0_tok_b1, L0_tok_w2, L0_tok_b2, L0_tok_pos_emb, L0_attn_t, L0_attn_w_qkv, L0_attn_mem_kv, L0_attn_w_out, L0_attn_b_out, L0_attn_g_out, L0_attn_g_pre, L0_ffn_attention_mask, L0_ffn_wr, L0_ffn_br, L0_ffn_w1, L0_ffn_b1, L0_ffn_w2, L0_ffn_b2):
    import jax
    import jax.numpy as jnp
    def _L0_tok_ref(x, w1, b1, w2, b2, pos_emb):
        import jax, jax.numpy as jnp
        import numpy as np
        B, EMB, HT, WD = (32, 256, 56, 56)
        NH, WS, SHIFTED = (8, 4, True)

        def _rel_indices(ws):
            coords = np.array([[i, j] for i in range(ws) for j in range(ws)])
            rel = coords[None, :, :] - coords[:, None, :] + ws - 1
            return jnp.asarray(rel)

        def _shift_masks(ws):
            m = np.zeros((ws * ws, ws * ws), np.float32)
            s = ws * (ws // 2)
            m[-s:, :-s] = -np.inf
            m[:-s, -s:] = -np.inf
            col = m.reshape(ws, ws, ws, ws).transpose(1, 0, 3, 2).reshape(ws * ws, ws * ws)
            return (jnp.asarray(m), jnp.asarray(col))
        b, c, ht, wd = x.shape
        ws, nh = (WS, NH)
        e = c // nh
        xt = x.reshape(b, c, ht * wd).transpose(0, 2, 1)
        qkv = xt @ w1.T + b1
        qkv = qkv.reshape(b, ht, wd, c, 3)
        if SHIFTED:
            qkv = jnp.roll(qkv, (-ws // 2, -ws // 2), axis=(1, 2))
        Wh, Ww = (ht // ws, wd // ws)
        qkv = qkv.reshape(b, Wh, ws, Ww, ws, e, nh, 3)
        qkv = qkv.transpose(0, 6, 1, 3, 2, 4, 5, 7).reshape(b, nh, Wh, Ww, ws * ws, e, 3)
        Q, K, V = (qkv[..., 0], qkv[..., 1], qkv[..., 2])
        scale = jnp.sqrt(jnp.float32(c / nh))
        wei = jnp.einsum('bhijpe,bhijqe->bhijpq', Q, K) / scale
        rel = _rel_indices(ws)
        wei = wei + pos_emb[rel[..., 0], rel[..., 1]]
        if SHIFTED:
            row_mask, col_mask = _shift_masks(ws)
            wei = wei.at[:, :, -1, :].add(row_mask)
            wei = wei.at[:, :, :, -1].add(col_mask)
        attn = jax.nn.softmax(wei, axis=-1)
        out = jnp.einsum('bhijpq,bhijqe->bhijpe', attn, V)
        out = out.reshape(b, nh, Wh, Ww, ws, ws, e)
        out = out.transpose(0, 2, 4, 3, 5, 1, 6).reshape(b, ht, wd, nh * e)
        out = out.reshape(b, ht * wd, c)
        return out @ w2.T + b2

    def _L0_attn_ref(x, t, w_qkv, mem_kv, w_out, b_out, g_out, g_pre):
        import jax, jax.numpy as jnp
        import numpy as np
        DIM = 256
        HEADS = 4
        DIM_HEAD = 32
        NUM_MEM = 4
        HIDDEN = HEADS * DIM_HEAD
        SCALE = DIM_HEAD ** (-0.5)

        def rmsnorm(x, g):
            n = jnp.linalg.norm(x, axis=-1, keepdims=True)
            return x / jnp.maximum(n, 1e-12) * g * x.shape[-1] ** 0.5
        b, n, c = x.shape
        xn = rmsnorm(x, g_pre)
        qkv = xn @ w_qkv
        q, k, v = jnp.split(qkv, 3, axis=-1)

        def to_heads(z):
            return z.reshape(b, n, HEADS, DIM_HEAD).transpose(0, 2, 3, 1)
        q, k, v = map(to_heads, (q, k, v))
        mk = jnp.broadcast_to(mem_kv[0], (b, HEADS, DIM_HEAD, NUM_MEM))
        mv = jnp.broadcast_to(mem_kv[1], (b, HEADS, DIM_HEAD, NUM_MEM))
        k = jnp.concatenate([mk, k], axis=-1)
        v = jnp.concatenate([mv, v], axis=-1)
        q = jax.nn.softmax(q, axis=-2) * SCALE
        k = jax.nn.softmax(k, axis=-1)
        context = jnp.einsum('bhdn,bhen->bhde', k, v)
        out = jnp.einsum('bhde,bhdn->bhen', context, q)
        out = out.transpose(0, 3, 1, 2).reshape(b, n, HIDDEN)
        out = rmsnorm(out @ w_out + b_out, g_out)
        return out + x

    def _L0_ffn_ref(x, attention_mask, wr, br, w1, b1, w2, b2):
        import jax, jax.numpy as jnp
        import numpy as np
        B, S, D = (8, 4096, 256)
        H = 4 * D
        CAPACITY = 0.5
        b, s, d = x.shape
        weights = (jnp.einsum('bsd,do->bso', x, wr) + br)[..., 0]
        k = max(1, int(CAPACITY * s))
        kk = k - 1 if k > 1 else 1
        _, idx = jax.lax.top_k(weights, k)
        sel_idx = idx[:, :kk]
        sel = jnp.take_along_axis(x, sel_idx[:, :, None], axis=1)
        h = jax.nn.gelu(jnp.einsum('bkd,dh->bkh', sel, w1) + b1)
        y = jnp.einsum('bkh,hd->bkd', h, w2) + b2
        w_sel = jnp.take_along_axis(weights, sel_idx, axis=1)
        y = y * w_sel[..., None]
        batch_idx = jnp.arange(b)[:, None]
        processed = jnp.zeros_like(x).at[batch_idx, sel_idx].set(y)
        return processed + x

    h = _L0_tok_ref(x, L0_tok_w1, L0_tok_b1, L0_tok_w2, L0_tok_b2, L0_tok_pos_emb)
    h = jnp.concatenate([jnp.broadcast_to(cls_tok, (h.shape[0], 1, h.shape[2])), h], axis=1)
    h = h + _L0_attn_ref(_layernorm(h, axis=-1), L0_attn_t, L0_attn_w_qkv, L0_attn_mem_kv, L0_attn_w_out, L0_attn_b_out, L0_attn_g_out, L0_attn_g_pre)
    h = h + _L0_ffn_ref(_layernorm(h, axis=-1), L0_ffn_attention_mask, L0_ffn_wr, L0_ffn_br, L0_ffn_w1, L0_ffn_b1, L0_ffn_w2, L0_ffn_b2)
    return h


_drawn_inputs = setup_inputs


def setup_inputs(seed=0):
    import zlib

    import numpy as np

    out = dict(_drawn_inputs(seed))
    spreads = {'L0_attn_b_out': (0.0, 0.1),
     'L0_attn_g_out': (1.0, 0.2),
     'L0_attn_g_pre': (1.0, 0.6),
     'L0_ffn_b1': (0.0, 0.8),
     'L0_ffn_b2': (0.0, 0.8)}
    factors = {'cls_tok': 4.689,
     'L0_attn_mem_kv': 8.0,
     'L0_ffn_wr': 4.847,
     'L0_ffn_w1': 7.271,
     'L0_ffn_w2': 6.7}
    for name, (base, spread) in spreads.items():
        noise = np.random.default_rng([zlib.crc32(name.encode()), seed]).standard_normal(out[name].shape)
        drawn = base * np.exp(spread * noise) if base else spread * noise
        out[name] = jnp.asarray(drawn.astype(out[name].dtype))
    for name, factor in factors.items():
        out[name] = (out[name] * factor).astype(out[name].dtype)
    return out
```

```python
from contextlib import ExitStack

import concourse.bass as bass
from concourse import mybir
from concourse.bass import ds

ALU = mybir.AluOpType
ACT = mybir.ActivationFunctionType
F32 = mybir.dt.float32
BF16 = mybir.dt.bfloat16
FP16 = mybir.dt.float16
I32 = mybir.dt.int32
AX = mybir.AxisListType.X

NB, C, HT, WD = 16, 256, 56, 56
WS, NH, E = 4, 8, 32
NWR = HT // WS
STEP = WS * WD
NTOK = HT * WD + 1
BLK = 32
NJ = STEP // BLK
TT = STEP // 2
KC = C // 128
NS = NB * NWR
HID, NMEM = 128, 4
KCOL = NTOK + NMEM
FF = 1024
NHB = FF // 128
KK = int(0.5 * NTOK) - 1
NSEL = NB * KK
NPAIR = (NSEL + 255) // 256
SLOTS = NPAIR * 2
SEG = 400
LASTROW = NTOK - 7 * SEG
EPS = 1e-5
TINY2 = 1e-12 ** 2 / C
NEG = -1e30
ISC = float(1.0 / (E ** 0.5))
QSC = float(E ** -0.5)
OUTLAG = 4 + NWR
RING = 20
CR = 4



def link(eng, ins, sem, value):
    ins.then_inc(sem, 1)
    eng.wait_ge(sem, value)


def pool_waits(nc, dot, n):
    nc.gpsimd.tensor_tensor(dot[:, n:n + 1], dot[:, 0:1], dot[:, 0:1], ALU.add)


def schedule(eng, body):
    stages = ("proj", "attn", "mix", "lin", "tq")
    every = set(stages)
    for f in range(6):
        body(f, 0, f, f % 2, {n for lag, n in enumerate(stages) if f >= lag})
    with eng.Fori(6, NWR - 1, 2) as i:
        body(i, 0, i, 0, every)
        body(i + 1, 0, i + 1, 1, every)
    for i in range(4):
        body(NWR + i, 1, i, i % 2, every | ({"ctx"} if i == 3 else set()))
    with eng.Fori(1, NB - 1) as b:
        base = eng.snap(b * NWR)
        with eng.Fori(4, NWR - 1, 2) as i:
            F = eng.snap(base + i)
            body(F, b, i, 0, every | {"out"})
            body(F + 1, b, i + 1, 1, every | {"out"})
        for i in range(4):
            body(base + NWR + i, b + 1, i, i % 2, every | {"out"} | ({"ctx"} if i == 3 else set()))
    with eng.Fori(4, NWR - 1, 2) as i:
        body(i + (NS - NWR), NB - 1, i, 0, every | {"out"})
        body(i + (NS - NWR + 1), NB - 1, i + 1, 1, every | {"out"})
    for i in range(4):
        on = {n for lag, n in enumerate(stages) if i < lag}
        body(NS + i, NB, i, i % 2, on | {"out"} | ({"ctx"} if i == 3 else set()))
    with eng.Fori(4, 3 + NWR, 2) as i:
        body(i + NS, NB, i, 0, {"out"})
        body(i + (NS + 1), NB, i + 1, 1, {"out"})


def ring(F, lag, size):
    return ((F - lag) % RING) * size


def attention_program(nc, A):
    out, x2d, wd, clsd = A["out"], A["x2d"], A["wd"], A["clsd"]
    with ExitStack() as ctx:
        def sb(name, shape, dt=F32):
            return ctx.enter_context(nc.sbuf_tensor(name, shape, dt))

        bank = [ctx.enter_context(nc.psum_tensor(f"bank{n}", [128, 512], F32)) for n in range(8)]
        P_QV, P_K, P_SC, P_PV, P_W2, P_T, P_LIN, P_LK = bank

        w1T = sb("w1T", [128, KC, 6, 128]); b1c = sb("b1c", [128, 6])
        w2T = sb("w2T", [128, KC, C]); b2r = sb("b2r", [128, C])
        tbl = sb("tbl", [128, 2, STEP]); posr = sb("posr", [128, STEP])
        ident = sb("ident", [128, 128])
        gpre = sb("gpre", [128, KC]); wlin = sb("wlin", [128, KC, 3 * HID])
        wout = sb("wout", [128, C]); hmask = sb("hmask", [128, 128])
        bor = sb("bor", [128, C]); gor = sb("gor", [128, C]); wrr = sb("wrr", [128, C]); brr = sb("brr", [128, 1])
        xw = sb("xw", [128, 2, KC, STEP])
        qlin = sb("qlin", [128, 2, STEP]); klin = sb("klin", [128, 2, 2, STEP])
        vlin = sb("vlin", [128, 2, STEP]); vtr = sb("vtr", [128, 2, STEP])
        qblk = sb("qblk", [128, 2, 2 * NJ, 4, BLK]); vblk = sb("vblk", [128, 2, 2 * NJ, 4, BLK])
        sc = sb("sc", [128, 2 * NJ, BLK]); scs = sb("scs", [128, 2 * NJ, BLK])
        pr = sb("pr", [128, 2 * NJ, BLK]); prn = sb("prn", [128, 2 * NJ, BLK])
        smx = sb("smx", [128, 2 * NJ]); ssm = sb("ssm", [128, 2 * NJ]); srec = sb("srec", [128, 2 * NJ])
        pT = sb("pT", [128, 2, 2 * NJ, BLK])
        oT = sb("oT", [128, 2, STEP])
        hh = sb("hh", [TT, 2, 2, C]); bst = sb("bst", [TT, 2, 6]); mv = sb("mv", [TT, 2, 2])
        rcv = sb("rcv", [TT, 2]); pwi = sb("pwi", [TT, 4]); pwo = sb("pwo", [TT, 4])
        mhalf = sb("mhalf", [TT, 4])
        gsc = sb("gsc", [TT, 2]); asc = sb("asc", [TT, 2, 2]); nmr = sb("nmr", [TT, 2, 2])
        xn = sb("xn", [TT, 2, C]); xnT = sb("xnT", [128, KC, STEP])
        s1 = sb("s1", [TT, RING * 2 * C]); qTs = sb("qTs", [128, RING * STEP])
        qraw = sb("qraw", [TT, 8, 32]); qmx = sb("qmx", [TT, 8]); qsh = sb("qsh", [TT, 8, 32])
        qex = sb("qex", [TT, 8, 32]); qsm = sb("qsm", [TT, 8]); qrc = sb("qrc", [TT, 8]); qs = sb("qs", [TT, 8, 32])
        kT = sb("kT", [128, KCOL]); kcst = sb("kcst", [128, 1 + NMEM])
        vst = sb("vst", [TT, 2 * NWR + 1, HID]); kN = sb("kN", [TT, 2, 4 * 128])
        kmx = sb("kmx", [128, 1]); nkmx = sb("nkmx", [128, 1]); ksum = sb("ksum", [128, 1]); krc = sb("krc", [128, 1])
        ctxT = sb("ctxT", [128, 128]); Mw = sb("Mw", [128, C])
        qc = sb("qc", [128, 2, STEP])
        ob = sb("ob", [TT, 2, C]); osq = sb("osq", [TT, 2, C]); oss = sb("oss", [TT, 2])
        onr = sb("onr", [TT, 2]); ors = sb("ors", [TT, 2]); v2 = sb("v2", [TT, 2]); ou = sb("ou", [TT, 2, C])
        h2 = sb("h2", [TT, 2, C]); bst2 = sb("bst2", [TT, 2, 6]); mv2 = sb("mv2", [TT, 2, 2]); r2 = sb("r2", [TT, 2])
        x2 = sb("x2", [TT, 2, 2, C]); bs = sb("bs", [TT, 2, 2, C]); wj = sb("wj", [TT, 2, C])
        ws0 = sb("ws0", [TT, 2]); wsv = sb("wsv", [TT, 2, 2])
        clsq = sb("clsq", [128, 1]); clso = sb("clso", [1, 2, C]); pdot = sb("pdot", [1, 8]); vdot = sb("vdot", [1, 4])
        clss = sb("clss", [TT, C]); clsr = sb("clsr", [TT, C])

        S = {}
        steps = dict(tensor="q_ps k_ps v_ps sc_ps pv_ps w2_ps tx_ps lin_ps lk_ps tq_ps o2_ps".split(),
                     scalar="q_lin k_lin v_lin sm_e o_t xnt q_cp v_cp k_cp qm_e q_t o2_q s1_d".split(),
                     vector="v_tr sm_a sm_s sm_p sm_t h_a ln_v v2_d ln_s xn_d qm_s qm_d o2_a u_d x2_d w_dn".split(),
                     gpsimd="ln_p or_p r2_p qb vb qc_d h2_d bs_d".split())
        for n in sum(steps.values(), []) + ("or_c x_ld0 x_ld1 w_ld ini sm_c ln_c qm_c o2_c st_d0 st_d1 ctx_m ctx_e ctx_t "
                                            "ctx_n ctx_ps ctx_c ctx_x ctx_mp ctx_mw cls_ps cls_c cls_st kc_d "
                                            "set_d set_p set_a set_g tbl_d fin_x fin_p fin_ld fin_d fin_a fin_st").split():
            S[n] = ctx.enter_context(nc.semaphore(n))

        def at(eng, name, s):
            eng.wait_ge(S[name], s + (1 + CR))

        x_ld, st_d = (S["x_ld0"], S["x_ld1"]), (S["st_d0"], S["st_d1"])

        def stored(eng, e, s):
            eng.wait_ge(st_d[e], (s - e) * 24 + 48)

        def credit(eng, who):
            for n in steps[who]:
                eng.sem_inc(S[n], CR)

        loads = [(w1T, "w1T"), (b1c, "b1c"), (w2T, "w2T"), (b2r, "b2r"), (posr, "posr"), (tbl, "mask"),
                 (ident, "ident"), (gpre, "gpre"), (wlin, "wlin"), (wout, "wout"), (hmask, "hmask"),
                 (bor, "bor"), (gor, "gor"), (wrr, "wrr"), (brr, "brr"), (clsr, "clsr")]
        W_ALL = 16 * (len(loads) + 3)

        LN_LINKS = 12

        def layer_norm_1(h, par, lnk, done, powered, free):
            for t in range(2):
                ins = nc.vector.bn_stats(bst[:, t, :], h[:, t, :])
            lnk(ins, 1)
            nc.vector.tensor_copy(vdot[:, 1:2], vdot[:, 0:1])
            for t in range(2):
                ins = nc.vector.bn_aggr(mv[:, t, :], bst[:, t, :])
            lnk(ins, 2)
            mean, var = mv[:, :, 0], mv[:, :, 1]
            lnk(nc.vector.tensor_scalar(pwi[:, 0:2], var, EPS, None, ALU.add), 3)
            lnk(nc.vector.reciprocal(rcv[:], pwi[:, 0:2]), 4)
            nc.vector.scalar_tensor_tensor(out=pwi[:, 2:4], in0=var, scalar=TINY2 * EPS, in1=rcv[:],
                                           op0=ALU.max, op1=ALU.mult).then_inc(*done("ln_v"))
            powered()
            nc.vector.tensor_scalar(asc[:, par, :], pwo[:, 0:2], 1.0, None, ALU.add)
            nc.vector.scalar_tensor_tensor(out=nmr[:, par, :], in0=mean, scalar=-1.0, in1=pwo[:, 0:2],
                                           op0=ALU.mult, op1=ALU.mult).then_inc(*done("ln_s"))
            lnk(nc.vector.tensor_tensor(gsc[:], pwo[:, 0:2], pwo[:, 2:4], ALU.mult), 5)
            free()
            for t in range(2):
                ins = nc.vector.tensor_scalar(xn[:, t, :], h[:, t, :], mv[:, t, 0:1], gsc[:, t:t + 1],
                                              ALU.subtract, ALU.mult)
            ins.then_inc(*done("xn_d"))

        def group(ap):
            return ap[:].rearrange("p (g o) -> p g o", o=1).broadcast_to([ap.shape[0], ap.shape[1], 32])

        def transpose_xn(pe):
            for t in range(2):
                for k in range(KC):
                    ins = nc.tensor.transpose(P_T[:, k * STEP + t * TT:k * STEP + (t + 1) * TT],
                                              xn[:, t, k * 128:(k + 1) * 128], ident[0:TT, 0:TT])
            return ins

        def lin_qv(pe):
            for t in range(2):
                for k in range(KC):
                    ins = nc.tensor.matmul(P_LIN[0:TT, t * 256:(t + 1) * 256], xnT[:, k, t * TT:(t + 1) * TT],
                                           wlin[:, k, 0:256], start=(k == 0), stop=(k == KC - 1))
            return ins

        def lin_k(pe):
            for k in range(KC):
                ins = nc.tensor.matmul(P_LK[:, 0:STEP], wlin[:, k, 256:384], xnT[:, k, :],
                                       start=(k == 0), stop=(k == KC - 1))
            return ins

        def transpose_q(pe):
            for t in range(2):
                ins = nc.tensor.transpose(P_T[:, t * TT:(t + 1) * TT],
                                          qs[:, 4 * t:4 * t + 4, :].rearrange("p g d -> p (g d)"), ident[0:TT, 0:TT])
            return ins

        p_lin3 = P_LIN[0:TT, :].rearrange("p (t n) -> p t n", t=2)

        with nc.Block() as block:
            @block.sync
            def _(sp):
                for dst, name in loads:
                    sp.dma_start(dst[:], A[name]).then_inc(S["w_ld"], 16)
                sp.dma_start(kcst[:, 1:1 + NMEM], A["memk"]).then_inc(S["w_ld"], 16)
                sp.dma_start(vst[1:1 + NMEM, 2 * NWR, :], A["memv"]).then_inc(S["w_ld"], 16)
                sp.dma_start(wd, A["wpad"]).then_inc(S["w_ld"], 16)
                sp.wait_ge(S["w_ld"], W_ALL)

            @block.vector
            def _(dve):
                dve.wait_ge(S["w_ld"], W_ALL)
                n = [0]

                def lnk(ins, k=None):
                    n[0] += 1
                    link(dve, ins, S["set_d"], n[0])

                lnk(nc.vector.memset(vdot[:], 0.0))
                for v in range(2):
                    nc.vector.tensor_tensor(tbl[:, v, :], tbl[:, v, :], posr[:], ALU.add).then_inc(S["tbl_d"], 1)
                for k in range(KC):
                    lnk(nc.vector.tensor_scalar(wlin[:, k, :], wlin[:, k, :], gpre[:, k:k + 1], None, ALU.mult))
                for t in range(2):
                    lnk(nc.vector.tensor_copy(hh[:, 0, t, :], clsr[:]))
                layer_norm_1(hh[:, 0], 0, lnk, lambda name: (S["ini"], 1), lambda: dve.wait_ge(S["set_g"], 5),
                             lambda: None)
                dve.wait_ge(S["ini"], 3)
                lnk(nc.vector.tensor_scalar(clss[:], clsr[:], asc[:, 0, 0:1], nmr[:, 0, 0:1], ALU.mult, ALU.add))
                dve.wait_ge(S["set_p"], 1)
                nc.vector.tensor_copy(xnT[:].rearrange("p k t -> p (k t)"), P_T[:, 0:KC * STEP]).then_inc(S["ini"], 1)
                dve.wait_ge(S["set_p"], 2)
                nc.vector.tensor_copy(vst[0:1, 2 * NWR, :], P_LIN[0:1, 128:256])
                nc.vector.tensor_copy(kcst[:, 0:1], P_LK[:, 0:1])
                lnk(nc.vector.tensor_copy(qraw[:].rearrange("p (t g) d -> p t (g d)", t=2), p_lin3[:, :, 0:128]))
                nc.vector.tensor_copy(kT[:, NTOK - 1:KCOL], kcst[:])
                lnk(nc.vector.tensor_reduce(qmx[:], qraw[:], AX, ALU.max))
                nc.vector.tensor_tensor(qsh[:], qraw[:], group(qmx), ALU.subtract).then_inc(S["ini"], 1)
                dve.wait_ge(S["set_a"], 1)
                lnk(nc.vector.tensor_reduce(qsm[:], qex[:], AX, ALU.add))
                lnk(nc.vector.reciprocal(qrc[:], qsm[:]))
                nc.vector.tensor_tensor(qs[:], qex[:], group(qrc), ALU.mult).then_inc(S["ini"], 1)
                dve.wait_ge(S["set_p"], 3)
                lnk(nc.vector.tensor_copy(clsq[:], P_T[:, 0:1]))
                credit(dve, "vector")

            @block.scalar
            def _(act):
                act.wait_ge(S["ini"], 5)
                nc.scalar.activation(qex[:], qsh[:], ACT.Exp).then_inc(S["set_a"], 1)
                credit(act, "scalar")

            @block.tensor
            def _(pe):
                pe.wait_ge(S["w_ld"], W_ALL)
                pe.wait_ge(S["ini"], 3)
                transpose_xn(pe).then_inc(S["set_p"], 1)
                pe.wait_ge(S["ini"], 4)
                lin_qv(pe)
                lin_k(pe).then_inc(S["set_p"], 1)
                pe.wait_ge(S["ini"], 6)
                transpose_q(pe).then_inc(S["set_p"], 1)
                credit(pe, "tensor")
                pe.sem_inc(S["ctx_ps"], 2)

            @block.gpsimd
            def _(pool):
                nc.gpsimd.memset(qblk[:], 0.0).then_inc(S["set_g"], 1)
                nc.gpsimd.memset(vblk[:], 0.0).then_inc(S["set_g"], 1)
                nc.gpsimd.memset(pdot[:], 0.0).then_inc(S["set_g"], 1)
                nc.gpsimd.memset(mhalf[:], -0.5).then_inc(S["set_g"], 1)
                pool.wait_ge(S["set_g"], 4)
                pool.wait_ge(S["ini"], 1)
                nc.gpsimd.tensor_tensor(pwo[:], pwi[:], mhalf[:], ALU.pow).then_inc(S["set_g"], 1)
                credit(pool, "gpsimd")

        with nc.Block() as block:
            @block.sync
            def _(sp):
                for e in range(2):
                    sp.sem_inc(st_d[e], 48)
                sp.dma_start(xw[:, 0], A["xw"][0]).then_inc(x_ld[0], 16)
                o3, x3, w1d = A["out_rows"], x2d.rearrange("b n c -> (b n) c"), wd.rearrange("b n -> (b n)")

                def body(F, b, i, e, on):
                    if "proj" in on:
                        at(sp, "v_ps", F - 1)
                        sp.dma_start(xw[:, 1 - e:2 - e], A["xw"][ds(F + 1, 1)].rearrange("s p k t -> p s k t"))\
                            .then_inc(x_ld[1 - e], 16)
                    if "ctx" in on:
                        sp.wait_ge(S["cls_c"], b)
                        sp.dma_start(clsd[ds(b - 1, 1), :], clso[0:1, 0, :]).then_inc(S["cls_st"], 16)
                    if "out" in on:
                        s = F - OUTLAG
                        bo = b - 1 if not isinstance(i, int) or i >= 4 else b - 2
                        r0 = s * STEP + bo + 1
                        at(sp, "bs_d", s)
                        sp.dma_start(o3[ds(r0, STEP), :].rearrange("(t p) c -> p t c", p=TT), bs[:, e])\
                            .then_inc(st_d[e], 16)
                        at(sp, "x2_d", s)
                        sp.dma_start(x3[ds(r0, STEP), :].rearrange("(t p) c -> p t c", p=TT), x2[:, e])\
                            .then_inc(st_d[e], 16)
                        at(sp, "w_dn", s)
                        sp.dma_start(w1d[ds(s * STEP + bo * (8 * SEG - NWR * STEP) + 1, STEP)]
                                     .rearrange("(t p) -> p t", p=TT), wsv[:, e, :],
                                     allow_slow_non_contiguous=True).then_inc(st_d[e], 16)
                schedule(sp, body)
                for e in range(2):
                    sp.wait_ge(st_d[e], 48 + 24 * NS)
                sp.wait_ge(S["cls_st"], 16 * NB)
                sp.wait_ge(x_ld[0], 8 * NS + 16)

            @block.gpsimd
            def _(pool):
                def blocks(dst, src, dot):
                    pool_waits(nc, pdot, dot)
                    for h in range(4):
                        r = slice(32 * h, 32 * h + 32)
                        ins = nc.gpsimd.tensor_copy(dst[r, :, h, :], src[r].rearrange("p m (j q) -> p (m j) q", q=BLK))
                    return ins

                def body(F, b, i, e, on):
                    if "out" in on:
                        s = F - OUTLAG
                        if "proj" in on:
                            at(pool, "vb", F - 1)
                        at(pool, "q_t", s)
                        at(pool, "o2_ps", s - 2)
                        pool_waits(nc, pdot, 2)
                        nc.gpsimd.tensor_copy(qc[:, e, :], qTs[:, ds(ring(F, OUTLAG, STEP), STEP)])\
                            .then_inc(S["qc_d"], 1)
                    if "proj" in on:
                        at(pool, "q_lin", F)
                        at(pool, "sc_ps", F - 2)
                        if "out" in on:
                            at(pool, "qc_d", F - OUTLAG)
                            at(pool, "bs_d", F - OUTLAG - 1)
                        else:
                            at(pool, "vb", F - 1)
                        blocks(qblk[:, e], qlin, 1).then_inc(S["qb"], 1)
                    if "mix" in on:
                        s = F - 2
                        at(pool, "ln_v", s)
                        if "proj" in on:
                            at(pool, "qb", F)
                        nc.gpsimd.tensor_tensor(pwo[:], pwi[:], mhalf[:], ALU.pow).then_inc(S["ln_p"], 1)
                    if "proj" in on:
                        at(pool, "v_tr", F)
                        at(pool, "pv_ps", F - 2)
                        if "mix" in on:
                            at(pool, "ln_p", F - 2)
                        else:
                            at(pool, "qb", F)
                        blocks(vblk[:, e], vtr, 4).then_inc(S["vb"], 1)
                    if "out" in on:
                        s = F - OUTLAG
                        if "proj" in on:
                            at(pool, "vb", F)
                        at(pool, "o2_q", s)
                        pool_waits(nc, pdot, 3)
                        nc.gpsimd.tensor_scalar(onr[:], oss[:], TINY2, None, ALU.max).then_inc(S["or_c"], 1)
                        pool.wait_ge(S["or_c"], s + 1)
                        nc.gpsimd.tensor_tensor(ors[:], onr[:], mhalf[:, 0:2], ALU.pow).then_inc(S["or_p"], 1)
                        at(pool, "u_d", s)
                        at(pool, "s1_d", s)
                        at(pool, "x2_d", s - 1)
                        nc.gpsimd.tensor_tensor(h2[:].rearrange("p t c -> p (t c)"), ou[:].rearrange("p t c -> p (t c)"),
                                                s1[:, ds(ring(F, OUTLAG, 2 * C), 2 * C)], ALU.add).then_inc(S["h2_d"], 1)
                        at(pool, "v2_d", s)
                        nc.gpsimd.tensor_tensor(r2[:], v2[:], mhalf[:, 0:2], ALU.pow).then_inc(S["r2_p"], 1)
                        at(pool, "x2_d", s)
                        at(pool, "h2_d", s)
                        stored(pool, e, s)
                        nc.gpsimd.tensor_tensor(bs[:, e], h2[:], x2[:, e], ALU.add).then_inc(S["bs_d"], 1)
                schedule(pool, body)

            @block.scalar
            def _(act):
                def body(F, b, i, e, on):
                    if "mix" in on:
                        s = F - 2
                        at(act, "pv_ps", s)
                        at(act, "w2_ps", s - 1)
                        for m in range(2):
                            ins = nc.scalar.activation(
                                oT[:, m, :].rearrange("p (r w c) -> p r w c", r=WS, c=WS),
                                P_PV[:, m * STEP:(m + 1) * STEP].rearrange("p (w r c) -> p r w c", r=WS, c=WS), ACT.Copy)
                        ins.then_inc(S["o_t"], 1)
                    if "proj" in on:
                        at(act, "q_ps", F)
                        at(act, "qb", F - 1)
                        for m in range(2):
                            ins = nc.scalar.activation(qlin[:, m, :], P_QV[:, m * STEP:(m + 1) * STEP], ACT.Identity,
                                                       bias=b1c[:, m:m + 1])
                        ins.then_inc(S["q_lin"], 1)
                        at(act, "k_ps", F)
                        at(act, "sc_ps", F - 2)
                        for m in range(2):
                            ins = nc.scalar.activation(klin[:, e, m, :], P_K[:, m * STEP:(m + 1) * STEP], ACT.Identity,
                                                       bias=b1c[:, 2 + m:3 + m])
                        ins.then_inc(S["k_lin"], 1)
                    if "attn" in on:
                        s = F - 1
                        at(act, "sm_s", s)
                        at(act, "sm_p", s - 1)
                        nc.scalar.activation(pr[:], scs[:], ACT.Exp).then_inc(S["sm_e"], 1)
                    if "ctx" in on:
                        act.wait_ge(S["ctx_m"], b)
                        nc.scalar.activation(kT[:], kT[:], ACT.Exp, bias=nkmx[:, 0:1], accum_out=ksum[:, 0:1])\
                            .then_inc(S["ctx_e"], 1)
                    if "lin" in on:
                        s = F - 3
                        at(act, "tx_ps", s)
                        at(act, "lk_ps", s - 1)
                        nc.scalar.activation(xnT[:].rearrange("p k t -> p (k t)"), P_T[:, 0:KC * STEP], ACT.Copy)\
                            .then_inc(S["xnt"], 1)
                    if "proj" in on:
                        at(act, "v_ps", F)
                        at(act, "v_tr", F - 1)
                        for m in range(2):
                            ins = nc.scalar.activation(vlin[:, m, :], P_QV[:, m * STEP:(m + 1) * STEP], ACT.Identity,
                                                       bias=b1c[:, 4 + m:5 + m])
                        ins.then_inc(S["v_lin"], 1)
                    if "mix" in on:
                        s = F - 2
                        at(act, "ln_s", s)
                        for t in range(2):
                            ins = nc.scalar.activation(s1[:, ds(ring(F, 2, 2 * C) + t * C, C)], hh[:, e, t, :],
                                                       ACT.Identity, bias=nmr[:, e, t:t + 1], scale=asc[:, e, t:t + 1])
                        ins.then_inc(S["s1_d"], 1)
                    if "out" in on:
                        s = F - OUTLAG
                        at(act, "o2_a", s)
                        at(act, "u_d", s - 1)
                        for t in range(2):
                            ins = nc.scalar.activation(osq[:, t, :], ob[:, t, :], ACT.Square, scale=float(C) ** -0.5,
                                                       accum_out=oss[:, t:t + 1])
                        ins.then_inc(S["o2_q"], 1)
                    if "ctx" in on:
                        for g in range(8):
                            act.wait_ge(S["ctx_t"], b * 8 - 8 + g + 1)
                            act.wait_ge(S["ctx_ps"], b * 8 - 8 + g + 1)
                            src = P_LK if g % 2 else P_K
                            if g < 7:
                                ins = nc.scalar.activation(kN[:, g % 2, :], src[0:TT, :], ACT.Copy)
                            else:
                                ins = nc.scalar.activation(kN[0:1 + NMEM, g % 2, 0:128], src[0:1 + NMEM, 0:128], ACT.Copy)
                            ins.then_inc(S["ctx_n"], 1)
                        nc.scalar.activation(kT[:, NTOK - 1:KCOL], kcst[:], ACT.Copy).then_inc(S["kc_d"], 1)
                    if "lin" in on:
                        s = F - 3
                        at(act, "lin_ps", s)
                        at(act, "qm_s", s - 1)
                        nc.scalar.activation(qraw[:].rearrange("p (t g) d -> p t (g d)", t=2), p_lin3[:, :, 0:128],
                                             ACT.Copy).then_inc(S["q_cp"], 1)
                        i3 = i - 3 if not isinstance(i, int) or i >= 3 else i - 3 + NWR
                        nc.scalar.activation(vst[:, ds(i3 * 2, 2), :], p_lin3[:, :, 128:256], ACT.Copy)\
                            .then_inc(S["v_cp"], 1)
                        at(act, "lk_ps", s)
                        nc.scalar.activation(kT[:, ds(i3 * STEP, STEP)], P_LK[:, 0:STEP], ACT.Copy)\
                            .then_inc(S["k_cp"], 1)
                    if "tq" in on:
                        s = F - 4
                        at(act, "tq_ps", s)
                        nc.scalar.activation(qTs[:, ds(ring(F, 4, STEP), STEP)], P_T[:, 0:STEP], ACT.Copy)\
                            .then_inc(S["q_t"], 1)
                    if "lin" in on:
                        s = F - 3
                        at(act, "qm_s", s)
                        at(act, "qm_d", s - 1)
                        nc.scalar.activation(qex[:], qsh[:], ACT.Exp).then_inc(S["qm_e"], 1)
                schedule(act, body)

            @block.tensor
            def _(pe):
                def project(e, f, P, name):
                    for m in range(2):
                        for k in range(KC):
                            ins = nc.tensor.matmul(P[:, m * STEP:(m + 1) * STEP], w1T[:, k, f + m, :],
                                                   xw[:, e, k, :],
                                                   start=(k == 0), stop=(k == KC - 1))
                    ins.then_inc(S[name], 1)

                def body(F, b, i, e, on):
                    if "attn" in on:
                        s, p = F - 1, 1 - e
                        at(pe, "qb", s)
                        at(pe, "k_lin", s)
                        at(pe, "sm_a", s - 1)
                        for n in range(2 * NJ):
                            m, j = n // NJ, n % NJ
                            ins = nc.tensor.matmul(P_SC[:, n * BLK:(n + 1) * BLK],
                                                   qblk[:, p, n, :, :].rearrange("p h q -> p (h q)"),
                                                   klin[:, p, m, j * BLK:(j + 1) * BLK], start=True, stop=True)
                        ins.then_inc(S["sc_ps"], 1)
                    if "mix" in on:
                        s = F - 2
                        at(pe, "sm_t", s)
                        at(pe, "vb", s)
                        at(pe, "o_t", s - 1)
                        for n in range(2 * NJ):
                            ins = nc.tensor.matmul(P_PV[:, n * BLK:(n + 1) * BLK],
                                                   vblk[:, e, n, :, :].rearrange("p h q -> p (h q)"),
                                                   pT[:, e, n, :], start=True, stop=True)
                        ins.then_inc(S["pv_ps"], 1)
                    if "proj" in on:
                        pe.wait_ge(x_ld[e], (F - e) * 8 + 16)
                        at(pe, "v_lin", F - 1)
                        project(e, 0, P_QV, "q_ps")
                        at(pe, "k_lin", F - 1)
                        if "out" in on:
                            at(pe, "o2_a", F - OUTLAG - 1)
                        project(e, 2, P_K, "k_ps")
                    if "mix" in on:
                        s = F - 2
                        at(pe, "o_t", s)
                        at(pe, "h_a", s - 1)
                        for t in range(2):
                            for m in range(2):
                                ins = nc.tensor.matmul(P_W2[0:TT, t * C:(t + 1) * C], oT[:, m, t * TT:(t + 1) * TT],
                                                       w2T[:, m, :], start=(m == 0), stop=(m == 1))
                        ins.then_inc(S["w2_ps"], 1)
                    if "lin" in on:
                        s = F - 3
                        at(pe, "xn_d", s)
                        at(pe, "q_t", s - 2)
                        transpose_xn(pe).then_inc(S["tx_ps"], 1)
                    if "proj" in on:
                        at(pe, "q_lin", F)
                        project(e, 4, P_QV, "v_ps")
                    if "out" in on:
                        s = F - OUTLAG
                        at(pe, "qc_d", s)
                        bo = b - 1 if not isinstance(i, int) or i >= 4 else b - 2
                        pe.wait_ge(S["ctx_mw"], bo + 1)
                        at(pe, "o2_a", s - 1)
                        if "proj" in on:
                            at(pe, "k_lin", F)
                        pe.wait_ge(S["ctx_n"], (bo + 1) * 8)
                        for t in range(2):
                            ins = nc.tensor.matmul(P_K[0:TT, t * C:(t + 1) * C], qc[:, e, t * TT:(t + 1) * TT], Mw[:],
                                                   start=True, stop=True)
                        ins.then_inc(S["o2_ps"], 1)
                    if "ctx" in on:
                        pe.wait_ge(S["ctx_e"], b)
                        at(pe, "k_cp", F - 4)
                        at(pe, "k_lin", F) if "proj" in on else None
                        if "out" in on:
                            at(pe, "o2_a", F - OUTLAG)
                        at(pe, "q_cp", F - 4)
                        at(pe, "v_cp", F - 4)

                        def turn(g):
                            if g >= 2:
                                pe.wait_ge(S["ctx_n"], b * 8 - 8 + g - 1)
                            P = P_LK if g % 2 else P_K
                            if g < 7:
                                for q in range(4):
                                    c0 = (4 * g + q) * TT
                                    ins = nc.tensor.transpose(P[0:TT, q * 128:(q + 1) * 128], kT[:, c0:c0 + TT], ident[:])
                            else:
                                ins = nc.tensor.transpose(P[0:1 + NMEM, 0:128], kT[:, NTOK - 1:KCOL], ident[:])
                            ins.then_inc(S["ctx_t"], 1)

                        def sum_up(g):
                            pe.wait_ge(S["ctx_n"], b * 8 - 8 + g + 1)
                            for q in range(4 if g < 7 else 1):
                                r = TT if g < 7 else 1 + NMEM
                                ins = nc.tensor.matmul(P_LIN[:, 0:128], vst[0:r, 4 * g + q, :],
                                                       kN[0:r, g % 2, q * 128:(q + 1) * 128],
                                                       start=(g == 0 and q == 0), stop=(g == 7))
                            ins.then_inc(S["ctx_ps"], 1)

                        turn(0)
                        turn(1)
                        for g in range(8):
                            sum_up(g)
                            if g + 2 < 8:
                                turn(g + 2)
                        pe.wait_ge(S["ctx_x"], b)
                        nc.tensor.matmul(P_LIN[:, 256:512], ctxT[:], wout[:], start=True, stop=True).then_inc(S["ctx_mp"], 1)
                        pe.wait_ge(S["ctx_mw"], b)
                        nc.tensor.matmul(P_LIN[0:1, 0:C], clsq[:], Mw[:], start=True, stop=True).then_inc(S["cls_ps"], 1)
                        pe.wait_ge(S["cls_c"], b)
                    if "lin" in on:
                        s = F - 3
                        at(pe, "xnt", s)
                        at(pe, "q_cp", s - 1)
                        at(pe, "v_cp", s - 1)
                        lin_qv(pe).then_inc(S["lin_ps"], 1)
                        at(pe, "k_cp", s - 1)
                        if "ctx" in on:
                            pe.wait_ge(S["kc_d"], b)
                        lin_k(pe).then_inc(S["lk_ps"], 1)
                    if "tq" in on:
                        s = F - 4
                        at(pe, "qm_d", s)
                        at(pe, "xnt", s + 1) if "lin" in on else None
                        transpose_q(pe).then_inc(S["tq_ps"], 1)
                schedule(pe, body)

            @block.vector
            def _(dve):
                def body(F, b, i, e, on):
                    if "ctx" in on:
                        at(dve, "k_cp", F - 4)
                        if not isinstance(b, int) or b > 1:
                            dve.wait_ge(S["kc_d"], b - 1)
                            dve.wait_ge(S["ctx_e"], b - 1)
                        link(dve, nc.vector.tensor_reduce(kmx[:], kT[:], AX, ALU.max), S["ctx_c"], b * 2 - 1)
                        nc.vector.tensor_scalar(nkmx[:], kmx[:], -1.0, None, ALU.mult).then_inc(S["ctx_m"], 1)
                    if "attn" in on:
                        s, p = F - 1, 1 - e
                        last_row = isinstance(i, int) and i == 0
                        at(dve, "sc_ps", s)
                        for m in range(2):
                            ins = nc.vector.scalar_tensor_tensor(
                                out=sc[:, m * NJ:(m + 1) * NJ, :].rearrange("p j q -> p (j q)"),
                                in0=P_SC[:, m * STEP:(m + 1) * STEP], scalar=ISC, in1=tbl[:, int(last_row), :],
                                op0=ALU.mult, op1=ALU.add)
                        ins.then_inc(S["sm_a"], 1)
                        at(dve, "sm_a", s)
                        link(dve, nc.vector.tensor_reduce(smx[:], sc[:], AX, ALU.max), S["sm_c"], s * 3 + 1)
                        at(dve, "sm_e", s - 1)
                        nc.vector.tensor_tensor(scs[:], sc[:], group(smx), ALU.subtract).then_inc(S["sm_s"], 1)
                    if "mix" in on:
                        s = F - 2
                        at(dve, "w2_ps", s)
                        at(dve, "s1_d", s - 2)
                        ins = nc.vector.tensor_tensor(
                            hh[:, e], P_W2[0:TT, :].rearrange("p (t c) -> p t c", t=2),
                            b2r[0:TT, :].rearrange("p (o c) -> p o c", o=1).broadcast_to([TT, 2, C]), ALU.add)
                        ins.then_inc(S["h_a"], 1)
                        at(dve, "h_a", s)
                        layer_norm_1(hh[:, e], e, lambda ins, k: link(dve, ins, S["ln_c"], s * 5 + k),
                                     lambda name: (S[name], 1), lambda: at(dve, "ln_p", s), lambda: at(dve, "tx_ps", s - 1))
                    if "attn" in on:
                        s, p = F - 1, 1 - e
                        at(dve, "sm_e", s)
                        link(dve, nc.vector.tensor_reduce(ssm[:], pr[:], AX, ALU.add), S["sm_c"], s * 3 + 2)
                        link(dve, nc.vector.reciprocal(srec[:], ssm[:]), S["sm_c"], s * 3 + 3)
                        nc.vector.tensor_tensor(prn[:], pr[:], group(srec), ALU.mult).then_inc(S["sm_p"], 1)
                    if "attn" in on:
                        at(dve, "sm_p", s)
                        at(dve, "pv_ps", s - 2)
                        nc.vector.transpose(pT[:, p].rearrange("p n q -> p (n q)"),
                                            prn[:].rearrange("p n q -> p (n q)")).then_inc(S["sm_t"], 1)
                    if "proj" in on:
                        at(dve, "v_lin", F)
                        at(dve, "vb", F - 1)
                        nc.vector.transpose(vtr[:].rearrange("p m q -> p (m q)"),
                                            vlin[:].rearrange("p m q -> p (m q)")).then_inc(S["v_tr"], 1)
                    if "out" in on:
                        s = F - OUTLAG
                        at(dve, "o2_ps", s)
                        at(dve, "o2_q", s - 1)
                        nc.vector.tensor_tensor(
                            ob[:], P_K[0:TT, :].rearrange("p (t c) -> p t c", t=2),
                            bor[0:TT, :].rearrange("p (o c) -> p o c", o=1).broadcast_to([TT, 2, C]), ALU.add)\
                            .then_inc(S["o2_a"], 1)
                        at(dve, "or_p", s)
                        at(dve, "h2_d", s - 1)
                        for t in range(2):
                            ins = nc.vector.scalar_tensor_tensor(out=ou[:, t, :], in0=ob[:, t, :], scalar=ors[:, t:t + 1],
                                                                 in1=gor[0:TT, :], op0=ALU.mult, op1=ALU.mult)
                        ins.then_inc(S["u_d"], 1)
                        at(dve, "h2_d", s)
                        for t in range(2):
                            ins = nc.vector.bn_stats(bst2[:, t, :], h2[:, t, :])
                        link(dve, ins, S["o2_c"], s * 3 + 1)
                        nc.vector.tensor_copy(vdot[:, 2:3], vdot[:, 0:1])
                        for t in range(2):
                            ins = nc.vector.bn_aggr(mv2[:, t, :], bst2[:, t, :])
                        link(dve, ins, S["o2_c"], s * 3 + 2)
                        nc.vector.tensor_scalar(v2[:], mv2[:, :, 1], EPS, None, ALU.add).then_inc(S["v2_d"], 1)
                        at(dve, "r2_p", s)
                        at(dve, "bs_d", s - 2)
                        stored(dve, e, s)
                        for t in range(2):
                            ins = nc.vector.tensor_scalar(x2[:, e, t, :], h2[:, t, :], mv2[:, t, 0:1], r2[:, t:t + 1],
                                                          ALU.subtract, ALU.mult)
                        ins.then_inc(S["x2_d"], 1)
                        at(dve, "x2_d", s)
                        for t in range(2):
                            ins = nc.vector.tensor_tensor_reduce(wj[:, t, :], x2[:, e, t, :], wrr[0:TT, :], 1.0, 0.0, ALU.mult,
                                                                 ALU.add, ws0[:, t:t + 1])
                        link(dve, ins, S["o2_c"], s * 3 + 3)
                        nc.vector.tensor_scalar(wsv[:, e, :], ws0[:], brr[0:TT, 0:1], None, ALU.add).then_inc(S["w_dn"], 1)
                    if "ctx" in on:
                        dve.wait_ge(S["ctx_e"], b)
                        if not isinstance(b, int) or b > 1:
                            dve.wait_ge(S["ctx_mw"], b - 1)
                        link(dve, nc.vector.reciprocal(krc[:], ksum[:]), S["ctx_c"], b * 2)
                        dve.wait_ge(S["ctx_ps"], b * 8 + 2)
                        nc.vector.tensor_tensor(ctxT[:], P_LIN[:, 0:128], hmask[:], ALU.mult).then_inc(S["ctx_x"], 1)
                        dve.wait_ge(S["ctx_mp"], b)
                        if "out" in on:
                            at(dve, "o2_ps", F - OUTLAG)
                        nc.vector.tensor_scalar(Mw[:], P_LIN[:, 256:512], krc[:, 0:1], QSC, ALU.mult, ALU.mult).then_inc(S["ctx_mw"], 1)
                        dve.wait_ge(S["cls_ps"], b)
                        if not isinstance(b, int) or b > 1:
                            dve.wait_ge(S["cls_st"], b * 16 - 16)
                        nc.vector.tensor_copy(clso[0:1, 0, :], P_LIN[0:1, 0:C]).then_inc(S["cls_c"], 1)
                    if "lin" in on:
                        s = F - 3
                        at(dve, "q_cp", s)
                        link(dve, nc.vector.tensor_reduce(qmx[:], qraw[:], AX, ALU.max), S["qm_c"], s * 3 + 1)
                        at(dve, "qm_e", s - 1)
                        nc.vector.tensor_tensor(qsh[:], qraw[:], group(qmx), ALU.subtract).then_inc(S["qm_s"], 1)
                        at(dve, "qm_e", s)
                        link(dve, nc.vector.tensor_reduce(qsm[:], qex[:], AX, ALU.add), S["qm_c"], s * 3 + 2)
                        link(dve, nc.vector.reciprocal(qrc[:], qsm[:]), S["qm_c"], s * 3 + 3)
                        at(dve, "tq_ps", s - 1)
                        nc.vector.tensor_tensor(qs[:], qex[:], group(qrc), ALU.mult).then_inc(S["qm_d"], 1)
                schedule(dve, body)

        G = NB
        with nc.Block() as block:
            @block.sync
            def _(sp):
                sp.dma_start(ob[0:G, 0, :], clsd).then_inc(S["fin_ld"], 16)
                sp.wait_ge(S["fin_d"], 8)
                sp.dma_start(out[:, 0, :], bs[0:G, 0, 0, :]).then_inc(S["fin_st"], 16)
                sp.dma_start(x2d[:, 0, :], x2[0:G, 0, 0, :]).then_inc(S["fin_st"], 16)
                sp.dma_start(wd[:, 0:1], wsv[0:G, 0, 0:1], allow_slow_non_contiguous=True)\
                    .then_inc(S["fin_st"], 16)
                sp.wait_ge(S["fin_st"], 48)

            @block.gpsimd
            def _(pool):
                pool.wait_ge(S["fin_d"], 2)
                nc.gpsimd.tensor_tensor(ors[0:G, 0:1], onr[0:G, 0:1], mhalf[0:G, 0:1], ALU.pow).then_inc(S["fin_p"], 1)
                pool.wait_ge(S["fin_d"], 7)
                nc.gpsimd.tensor_tensor(r2[0:G, 0:1], v2[0:G, 0:1], mhalf[0:G, 0:1], ALU.pow).then_inc(S["fin_p"], 1)

            @block.scalar
            def _(act):
                act.wait_ge(S["fin_d"], 1)
                nc.scalar.activation(osq[0:G, 0, :], ob[0:G, 1, :], ACT.Square, scale=float(C) ** -0.5,
                                     accum_out=oss[0:G, 0:1]).then_inc(S["fin_a"], 1)

            @block.vector
            def _(dve):
                n = [0]

                def lnk(ins):
                    n[0] += 1
                    link(dve, ins, S["fin_d"], n[0])

                dve.wait_ge(S["fin_ld"], 16)
                lnk(nc.vector.tensor_tensor(ob[0:G, 1, :], ob[0:G, 0, :], bor[0:G], ALU.add))
                dve.wait_ge(S["fin_a"], 1)
                lnk(nc.vector.tensor_scalar(onr[0:G, 0:1], oss[0:G, 0:1], TINY2, None, ALU.max))
                dve.wait_ge(S["fin_p"], 1)
                lnk(nc.vector.scalar_tensor_tensor(out=ou[0:G, 0, :], in0=ob[0:G, 1, :], scalar=ors[0:G, 0:1],
                                                   in1=gor[0:G], op0=ALU.mult, op1=ALU.mult))
                lnk(nc.vector.tensor_tensor(h2[0:G, 0, :], ou[0:G, 0, :], clss[0:G], ALU.add))
                lnk(nc.vector.bn_stats(bst2[0:G, 0, :], h2[0:G, 0, :]))
                lnk(nc.vector.bn_aggr(mv2[0:G, 0, :], bst2[0:G, 0, :]))
                lnk(nc.vector.tensor_scalar(v2[0:G, 0:1], mv2[0:G, 0, 1:2], EPS, None, ALU.add))
                dve.wait_ge(S["fin_p"], 2)
                nc.vector.tensor_scalar(x2[0:G, 0, 0, :], h2[0:G, 0, :], mv2[0:G, 0, 0:1], r2[0:G, 0:1],
                                        ALU.subtract, ALU.mult).then_inc(S["fin_x"], 1)
                dve.wait_ge(S["fin_x"], 1)
                nc.vector.tensor_tensor(bs[0:G, 0, 0, :], h2[0:G, 0, :], x2[0:G, 0, 0, :], ALU.add)
                nc.vector.tensor_tensor_reduce(wj[0:G, 0, :], x2[0:G, 0, 0, :], wrr[0:G, :], 1.0, 0.0, ALU.mult,
                                               ALU.add, ws0[0:G, 0:1]).then_inc(S["fin_x"], 1)
                dve.wait_ge(S["fin_x"], 2)
                nc.vector.tensor_scalar(wsv[0:G, 0, 0:1], ws0[0:G, 0:1], brr[0:G, 0:1], None, ALU.add)\
                    .then_inc(S["fin_d"], 1)


def select_program(nc, A, ctx):
    wd = A["wd"]

    def sb(name, shape, dt=F32):
        return ctx.enter_context(nc.sbuf_tensor(name, shape, dt))

    ids = sb("ids", [128, SLOTS], I32)
    with ExitStack() as tmp:
        def tb(name, shape, dt=F32):
            return tmp.enter_context(nc.sbuf_tensor(name, shape, dt))

        wt = tb("wt", [128, SEG]); same = tb("same", [128, 128]); before = tb("before", [128, 128])
        allb = tb("allb", [128, 128]); iot = tb("iot", [128, SLOTS]); iotb = tb("iotb", [128, SLOTS], FP16)
        idhi = tb("idhi", [128, SEG]); idlo = tb("idlo", [128, SEG])
        bit = tb("bit", [128, 2], I32); u = tb("u", [128, 1], I32); cand = tb("cand", [128, 1], I32)
        msk = tb("msk", [128, 1], I32); thr = tb("thr", [128, 1], I32); okm = tb("okm", [128, 1], I32)
        cnt = tb("cnt", [128, 1]); junk = tb("junk", [128, SEG]); ones = tb("ones", [128, SEG]); zer = tb("zer", [128, SEG])
        gt = tb("gt", [128, SEG]); eq = tb("eq", [128, SEG]); esc = tb("esc", [128, SEG]); seleq = tb("seleq", [128, SEG])
        sel = tb("sel", [128, SEG]); psc = tb("psc", [128, SEG]); pos = tb("pos", [128, SEG]); poi = tb("poi", [128, SEG], I32)
        pdi = tb("pdi", [128, SEG], I32); pmi = tb("pmi", [128, SEG], I32); pdf = tb("pdf", [128, SEG]); pmf = tb("pmf", [128, SEG])
        room = tb("room", [128, 1]); room1 = tb("room1", [128, 1])
        UN = 4
        onL = tb("onL", [128, UN, 128], FP16); onR = tb("onR", [128, UN, 2, SLOTS], FP16)
        lstf = tb("lstf", [128, SLOTS])
        P_C = tmp.enter_context(nc.psum_tensor("p_cnt", [128, 512], F32))
        P_L = tmp.enter_context(nc.psum_tensor("p_list", [128, 512], F32))
        S = {n: tmp.enter_context(nc.semaphore("sel_" + n)) for n in "ld c cn cp n r rd pr prd l0 l mm lst".split()}
        loads = [(wt, wd.rearrange("b (s f) -> (b s) f", s=8)), (same, A["same"]), (before, A["before"]), (allb, A["allb"]),
                 (iot, A["iota"]), (idhi, A["idhi"]), (idlo, A["idlo"]), (bit[:, 0:1], A["bit"])]
        thf = thr[:].bitcast(F32)
        with nc.Block() as block:
            @block.sync
            def _(sp):
                for dst, src in loads:
                    sp.dma_start(dst if dst is loads[-1][0] else dst[:], src).then_inc(S["ld"], 16)
                sp.wait_ge(S["ld"], 16 * len(loads))

            @block.vector
            def _(dve):
                dve.wait_ge(S["ld"], 16 * len(loads))
                PER = 7

                def lnk(ins, v):
                    link(dve, ins, S["c"], v)

                def threshold(key, v):
                    lnk(nc.vector.tensor_scalar(msk[:], key[:], 31, -1, ALU.arith_shift_right, ALU.bitwise_xor), v + 1)
                    lnk(nc.vector.scalar_tensor_tensor(out=thr[:], in0=msk[:], scalar=-2147483648, in1=key[:],
                                                       op0=ALU.bitwise_or, op1=ALU.bitwise_xor), v + 2)

                nc.vector.memset(u[:], 0)
                nc.vector.memset(ones[:], 1.0)
                nc.vector.memset(zer[:], 0.0)
                lnk(nc.vector.tensor_copy(iotb[:], iot[:]), 1)
                with dve.Fori(0, 32) as r:
                    v = r * PER + 1
                    lnk(nc.vector.tensor_tensor(cand[:], u[:], bit[:, 0:1], ALU.bitwise_or), v + 1)
                    threshold(cand, v + 1)
                    nc.vector.scalar_tensor_tensor(out=junk[:], in0=wt[:], scalar=thf[:, 0:1], in1=ones[:], op0=ALU.is_ge,
                                                   op1=ALU.mult, accum_out=cnt[:]).then_inc(S["cn"], 1)
                    dve.wait_ge(S["cp"], r + 1)
                    lnk(nc.vector.tensor_scalar(okm[:], P_C[:, 0:1], float(KK), -1.0, ALU.is_ge, ALU.mult), v + 4)
                    lnk(nc.vector.scalar_tensor_tensor(out=u[:], in0=okm[:], scalar=bit[:, 0:1], in1=u[:],
                                                       op0=ALU.bitwise_and, op1=ALU.bitwise_or), v + 5)
                    lnk(nc.vector.tensor_scalar(bit[:, 1:2], bit[:, 0:1], 1, None, ALU.logical_shift_right), v + 6)
                    lnk(nc.vector.tensor_copy(bit[:, 0:1], bit[:, 1:2]), v + 7)
                v = 32 * PER + 1
                threshold(u, v)
                nc.vector.scalar_tensor_tensor(out=gt[:], in0=wt[:], scalar=thf[:, 0:1], in1=ones[:], op0=ALU.is_gt,
                                               op1=ALU.mult, accum_out=cnt[:]).then_inc(S["cn"], 1)
                lnk(nc.vector.tensor_scalar(eq[:], wt[:], thf[:, 0:1], None, ALU.is_equal), v + 3)
                nc.vector.tensor_tensor_scan(esc[:], eq[:], zer[:], 0.0, ALU.add, ALU.add).then_inc(S["cn"], 1)
                dve.wait_ge(S["cp"], 34)
                lnk(nc.vector.tensor_scalar(room[:], P_C[:, 0:1], -1.0, float(KK), ALU.mult, ALU.add), v + 4)
                lnk(nc.vector.tensor_tensor(room1[:], room[:], P_C[:, 1:2], ALU.subtract), v + 5)
                lnk(nc.vector.scalar_tensor_tensor(out=seleq[:], in0=esc[:], scalar=room1[:, 0:1], in1=eq[:],
                                                   op0=ALU.is_le, op1=ALU.mult), v + 6)
                lnk(nc.vector.tensor_tensor(sel[:], gt[:], seleq[:], ALU.add), v + 7)
                nc.vector.tensor_tensor_scan(psc[:], sel[:], zer[:], 0.0, ALU.add, ALU.add).then_inc(S["cn"], 1)
                dve.wait_ge(S["cp"], 35)
                lnk(nc.vector.tensor_copy(room[:], P_C[:, 2:3]), v + 8)
                lnk(nc.vector.scalar_tensor_tensor(out=pos[:], in0=psc[:], scalar=room[:, 0:1], in1=sel[:],
                                                   op0=ALU.add, op1=ALU.mult), v + 9)
                lnk(nc.vector.tensor_scalar(poi[:], pos[:], -1.0, None, ALU.add), v + 10)
                nc.vector.tensor_scalar(pdi[:], poi[:], 7, None, ALU.arith_shift_right)
                lnk(nc.vector.tensor_scalar(pmi[:], poi[:], 127, None, ALU.bitwise_and), v + 11)
                nc.vector.tensor_copy(pdf[:], pdi[:])
                lnk(nc.vector.tensor_copy(pmf[:], pmi[:]), v + 12)
                with dve.Fori(0, SEG - UN + 1, UN) as f:
                    for q in range(UN):
                        dve.wait_ge(S["mm"], f + q + 1)
                        nc.vector.tensor_scalar(onL[:, q, :], iotb[:, 0:128], pmf[:, ds(f + q, 1)], None, ALU.is_equal)
                        for n, part in enumerate((idhi, idlo)):
                            ins = nc.vector.tensor_scalar(onR[:, q, n, :], iotb[:], pdf[:, ds(f + q, 1)],
                                                          part[:, ds(f + q, 1)], ALU.is_equal, ALU.mult)
                        ins.then_inc(S["l"], 1)
                dve.wait_ge(S["mm"], SEG + UN)
                lnk(nc.vector.tensor_scalar(lstf[:], P_L[:, 0:SLOTS], 256.0, None, ALU.mult), v + 13)
                lnk(nc.vector.tensor_tensor(ids[:], lstf[:], P_L[:, SLOTS:2 * SLOTS], ALU.add), v + 14)

            @block.tensor
            def _(pe):
                pe.wait_ge(S["ld"], 16 * len(loads))
                pe.sem_inc(S["mm"], UN)
                with pe.Fori(0, 32) as r:
                    pe.wait_ge(S["cn"], r + 1)
                    nc.tensor.matmul(P_C[:, 0:1], same[:], cnt[:], start=True, stop=True).then_inc(S["cp"], 1)
                pe.wait_ge(S["cn"], 33)
                nc.tensor.matmul(P_C[:, 0:1], same[:], cnt[:], start=True, stop=True).then_inc(S["cp"], 1)
                pe.wait_ge(S["cn"], 34)
                nc.tensor.matmul(P_C[:, 1:2], before[:], esc[:, SEG - 1:SEG], start=True, stop=True).then_inc(S["cp"], 1)
                pe.wait_ge(S["cn"], 35)
                nc.tensor.matmul(P_C[:, 2:3], allb[:], psc[:, SEG - 1:SEG], start=True, stop=True).then_inc(S["cp"], 1)

                def add(q, v, start, stop):
                    pe.wait_ge(S["l"], v)
                    return nc.tensor.matmul(P_L[:, 0:2 * SLOTS], onL[:, q, :], onR[:, q].rearrange("p n a -> p (n a)"),
                                            start=start, stop=stop).then_inc(S["mm"], 1)
                add(0, 1, True, False)
                for q in range(1, UN):
                    add(q, q + 1, False, False)
                with pe.Fori(UN, SEG - 2 * UN + 1, UN) as f:
                    for q in range(UN):
                        add(q, f + q + 1, False, False)
                for q in range(UN):
                    add(q, SEG - UN + q + 1, False, q == UN - 1)
    return ids


def feed_forward_program(nc, A, ids):
    with ExitStack() as ctx:
        def sb(name, shape, dt=F32):
            return ctx.enter_context(nc.sbuf_tensor(name, shape, dt))

        w1 = sb("w1", [128, KC, FF]); b1 = sb("b1", [128, NHB]); w2 = sb("w2", [128, NHB, C])
        b2 = sb("b2", [128, C]); wr = sb("wr", [128, C]); br = sb("br", [128, 1]); idn = sb("idn", [128, 128])
        ix = sb("ix", [128, 4, 2], I32); pdot = sb("pdot3", [1, 16])
        xg = sb("xg", [128, 2, 2, C]); xgT = sb("xgT", [128, 2, KC, 256])
        wsj = sb("wsj", [128, 2, C]); wg = sb("wg", [128, 2]); wgb = sb("wgb", [128, 2, 2])
        hT = sb("hT", [128, 2, NHB, 256]); yb = sb("yb", [128, 2, 2, C]); ym = sb("ym", [128, 2, 2, C])
        P_X = ctx.enter_context(nc.psum_tensor("p_x", [128, 512], F32))
        P_H = [ctx.enter_context(nc.psum_tensor(f"p_h{n}", [128, 512], F32)) for n in range(4)]
        P_Y = [ctx.enter_context(nc.psum_tensor(f"p_y{n}", [128, 512], F32)) for n in range(2)]
        S = {n: ctx.enter_context(nc.semaphore("ff_" + n)) for n in
             "dot ld ix g0 g1 xt xc h0 h1 h2 h3 e y ya ym wc w s0 s1".split()}
        g, st = (S["g0"], S["g1"]), (S["s0"], S["s1"])
        loads = [(w1, "fw1"), (b1, "fb1"), (w2, "fw2"), (b2, "fb2"), (wr, "wrr"), (br, "brr"), (idn, "ident")]
        LAST = NSEL - (NPAIR * 256 - 128)
        out_rows, x2_rows = A["out_rows"], A["x2d"].rearrange("b n c -> (b n) c")

        def pairs(eng, body):
            for p in range(2):
                body(p, p, False)
            with eng.Fori(2, NPAIR - 3, 2) as p:
                body(p, 0, False)
                body(p + 1, 1, False)
            body(NPAIR - 2, 0, False)
            body(NPAIR - 1, 1, True)

        with nc.Block() as block:
            @block.sync
            def _(sp):
                for dst, name in loads:
                    sp.dma_start(dst[:], A[name]).then_inc(S["ld"], 16)
                sp.wait_ge(S["ld"], 16 * len(loads))

            @block.gpsimd
            def _(pool):
                def index(p, q):
                    pool_waits(nc, pdot, 4)
                    nc.gpsimd.tensor_copy(ix[:, q, :], ids[:, ds(p * 2, 2)]).then_inc(S["ix"], 1)

                def rows(last, t):
                    return LAST if last and t == 1 else 128

                def gather(p, e, q, last):
                    pool.wait_ge(S["ix"], p + 1)
                    pool.wait_ge(S["xt"], p + 1)
                    pool.wait_ge(S["w"], p + 1)
                    pool_waits(nc, pdot, 5)
                    for t in range(2):
                        r = rows(last, t)
                        nc.gpsimd.indirect_dma_start(
                            out=xg[0:r, e, t, :], out_offset=None, in_=x2_rows,
                            in_offset=bass.IndirectOffsetOnAxis(ap=ix[0:r, q, t:t + 1], axis=0)).then_inc(g[e], 16)

                def scatter(p, e, q, last):
                    pool.wait_ge(S["ym"], p + 1)
                    pool_waits(nc, pdot, 6 + q)
                    for t in range(2):
                        r = rows(last, t)
                        nc.gpsimd.indirect_dma_start(
                            out=out_rows, out_offset=bass.IndirectOffsetOnAxis(ap=ix[0:r, q, t:t + 1], axis=0),
                            in_=ym[0:r, e, t, :], in_offset=None, compute_op=ALU.add).then_inc(st[e], 16)

                nc.gpsimd.memset(pdot[:], 0.0).then_inc(S["dot"], 1)
                pool.wait_ge(S["dot"], 1)
                for p in range(2):
                    index(p, p)
                    gather(p, p, p, False)
                with pool.Fori(2, NPAIR - 7, 4) as p:
                    for k in range(4):
                        e, q = k % 2, (2 + k) % 4
                        pool.wait_ge(st[e], (p + k - e) * 16 - 32)
                        index(p + k, q)
                        gather(p + k, e, q, False)
                        scatter(p + k - 2, e, k % 4, False)
                for p in range(NPAIR - 4, NPAIR):
                    e, q = p % 2, (p % 4)
                    pool.wait_ge(st[e], (p - e) * 16 - 32)
                    index(p, q)
                    gather(p, e, q, p == NPAIR - 1)
                    scatter(p - 2, e, (q + 2) % 4, False)
                for p in (NPAIR - 2, NPAIR - 1):
                    scatter(p, p % 2, p % 4, p == NPAIR - 1)
                for e in range(2):
                    pool.wait_ge(st[e], 32 * (NPAIR // 2))

            @block.tensor
            def _(pe):
                def turn(p, e):
                    pe.wait_ge(g[e], (p - e) * 16 + 32)
                    pe.wait_ge(S["xc"], p + 2)
                    for t in range(2):
                        for k in range(KC):
                            ins = nc.tensor.transpose(P_X[:, k * 256 + t * 128:k * 256 + (t + 1) * 128],
                                                      xg[:, e, t, k * 128:(k + 1) * 128], idn[:])
                    ins.then_inc(S["xt"], 1)

                def up(p, e):
                    pe.wait_ge(S["xc"], p + 3)
                    for n in range(4):
                        pe.wait_ge(S["e"], (p + 1) * 4 + n + 1)
                        for m in range(2):
                            for k in range(KC):
                                hb = 2 * n + m
                                ins = nc.tensor.matmul(P_H[n][:, m * 256:(m + 1) * 256], w1[:, k, hb * 128:(hb + 1) * 128],
                                                       xgT[:, e, k, :], start=(k == 0), stop=(k == KC - 1))
                        ins.then_inc(S[f"h{n}"], 1)

                def down(p, e):
                    pe.wait_ge(S["ya"], p + 1)
                    pe.wait_ge(S["e"], (p + 2) * 4 + 4)
                    for t in range(2):
                        for hb in range(NHB):
                            ins = nc.tensor.matmul(P_Y[e][:, t * C:(t + 1) * C], hT[:, e, hb, t * 128:(t + 1) * 128],
                                                   w2[:, hb, :], start=(hb == 0), stop=(hb == NHB - 1))
                    ins.then_inc(S["y"], 1)

                pe.wait_ge(S["ld"], 16 * len(loads))
                pe.sem_inc(S["xt"], 2)
                pe.sem_inc(S["y"], 2)
                turn(0, 0)
                up(0, 0)
                turn(1, 1)
                up(1, 1)
                down(0, 0)
                with pe.Fori(2, NPAIR - 1, 2) as p:
                    for e in range(2):
                        turn(p + e, e)
                        up(p + e, e)
                        down(p + e - 1, 1 - e)
                down(NPAIR - 1, 1)

            @block.scalar
            def _(act):
                act.wait_ge(S["ld"], 16 * len(loads))
                act.sem_inc(S["e"], 8)

                def body(p, e, last):
                    act.wait_ge(S["y"], p + 1)
                    for n in range(4):
                        act.wait_ge(S[f"h{n}"], p + 1)
                        for m in range(2):
                            hb = 2 * n + m
                            ins = nc.scalar.activation(hT[:, e, hb, :], P_H[n][:, m * 256:(m + 1) * 256],
                                                       ACT.Gelu_apprx_tanh, bias=b1[:, hb:hb + 1])
                        ins.then_inc(S["e"], 1)
                pairs(act, body)

            @block.vector
            def _(dve):
                dve.wait_ge(S["ld"], 16 * len(loads))
                dve.sem_inc(S["xc"], 2)
                dve.sem_inc(S["ya"], 2)
                dve.sem_inc(S["w"], 2)
                dve.sem_inc(S["wc"], 2)

                def first(p, e, last):
                    dve.wait_ge(S["xt"], p + 3)
                    dve.wait_ge(S["h3"], p - 1) if not isinstance(p, int) or p >= 2 else None
                    nc.vector.tensor_copy(xgT[:, e].rearrange("p k t -> p (k t)"), P_X[:]).then_inc(S["xc"], 1)
                    dve.wait_ge(g[e], (p - e) * 16 + 32)
                    dve.wait_ge(S["wc"], p + 2)
                    for t in range(2):
                        ins = nc.vector.tensor_tensor_reduce(wsj[:, t, :], xg[:, e, t, :], wr[:], 1.0, 0.0, ALU.mult,
                                                             ALU.add, wg[:, t:t + 1])
                    ins.then_inc(S["w"], 1)
                    dve.wait_ge(S["w"], p + 3)
                    nc.vector.tensor_scalar(wgb[:, e, :], wg[:], br[:, 0:1], None, ALU.add).then_inc(S["wc"], 1)

                def second(p, e, last):
                    dve.wait_ge(S["y"], p + 3)
                    nc.vector.tensor_tensor(yb[:, e], P_Y[e][:].rearrange("p (t c) -> p t c", t=2),
                                            b2[:].rearrange("p (o c) -> p o c", o=1).broadcast_to([128, 2, C]), ALU.add)\
                        .then_inc(S["ya"], 1)
                    dve.wait_ge(S["ya"], p + 3)
                    dve.wait_ge(S["wc"], p + 3)
                    dve.wait_ge(st[e], (p - e) * 16 + 0) if not isinstance(p, int) or p >= 2 else None
                    for t in range(2):
                        ins = nc.vector.tensor_scalar(ym[:, e, t, :], yb[:, e, t, :], wgb[:, e, t:t + 1], None, ALU.mult)
                    ins.then_inc(S["ym"], 1)

                first(0, 0, False)
                first(1, 1, False)
                second(0, 0, False)
                with dve.Fori(2, NPAIR - 1, 2) as p:
                    for e in range(2):
                        first(p + e, e, False)
                        second(p + e - 1, 1 - e, False)
                second(NPAIR - 1, 1, True)


def lay_out(inputs):
    import numpy as np
    f = {n: np.asarray(a) for n, a in inputs.items()}
    x = np.concatenate([f["x"][:, :, WS // 2:], f["x"][:, :, :WS // 2]], axis=2)
    x = np.concatenate([x[:, :, :, WS // 2:], x[:, :, :, :WS // 2]], axis=3)
    x = x.reshape(NB, KC, 128, NWR, WS, NWR, WS).transpose(0, 3, 2, 1, 5, 4, 6).reshape(NS, 128, KC, STEP)
    xw = np.concatenate([x, x[:1]], axis=0)
    w1 = f["L0_tok_w1"].reshape(E, NH, 3, C).transpose(2, 1, 0, 3).reshape(6, 128, C)
    b1 = f["L0_tok_b1"].reshape(E, NH, 3).transpose(2, 1, 0).reshape(6, 128)
    tok = np.arange(BLK)
    win, row, col = tok // 16, tok % 16 // WS, tok % WS
    pos = f["L0_tok_pos_emb"][row[None, :] - row[:, None] + WS - 1, col[None, :] - col[:, None] + WS - 1]
    other = win[:, None] != win[None, :]
    half = WS // 2
    rows = (row[:, None] >= half) != (row[None, :] >= half)
    cols = (col[:, None] >= half) != (col[None, :] >= half)
    mask = np.zeros((2, NJ, BLK, BLK), np.float32)
    mask[:, :, other] = NEG
    mask[1, :, rows] = NEG
    edge = cols & (win[:, None] == 1) & (win[None, :] == 1)
    mask[:, NJ - 1, edge] = NEG
    mask = np.broadcast_to(mask.transpose(2, 0, 1, 3)[None], (4, BLK, 2, NJ, BLK)).reshape(128, 2, STEP)
    posr = np.broadcast_to(pos[None, :, None, :], (4, BLK, NJ, BLK)).reshape(128, STEP)
    q, k, v = np.split(f["L0_attn_w_qkv"], 3, axis=1)
    wlin = np.concatenate([q, v, k], axis=1).reshape(KC, 128, 3 * HID).transpose(1, 0, 2)

    def rep(a, n=128):
        return np.broadcast_to(a.reshape(1, -1), (n, a.size))
    part = np.arange(128)
    mk, mvv = f["L0_attn_mem_kv"]
    tokid = (part // 8 * NTOK + part % 8 * SEG)[:, None] + np.arange(SEG)[None, :]
    tokid = np.where(np.arange(SEG)[None, :] + (part % 8 * SEG)[:, None] < NTOK, tokid, 0)
    return {
        "xw": xw, "w1T": w1.transpose(2, 0, 1).reshape(KC, 128, 6, 128).transpose(1, 0, 2, 3), "b1c": b1.T,
        "w2T": f["L0_tok_w2"].T.reshape(KC, 128, C).transpose(1, 0, 2), "b2r": rep(f["L0_tok_b2"]),
        "posr": posr, "mask": mask, "ident": np.eye(128, dtype=np.float32),
        "gpre": f["L0_attn_g_pre"].reshape(KC, 128).T, "wlin": wlin, "wout": f["L0_attn_w_out"],
        "hmask": (part[:, None] // 32 == part[None, :] // 32).astype(np.float32),
        "bor": rep(f["L0_attn_b_out"]), "gor": rep(f["L0_attn_g_out"]), "wrr": rep(f["L0_ffn_wr"]),
        "brr": rep(f["L0_ffn_br"]), "clsr": rep(f["cls_tok"], TT),
        "memk": mk.reshape(HID, NMEM), "memv": mvv.reshape(HID, NMEM).T,
        "wpad": np.full((NB, 8 * SEG), -3e38, np.float32),
        "same": (part[:, None] // 8 == part[None, :] // 8).astype(np.float32),
        "before": ((part[:, None] // 8 == part[None, :] // 8) & (part[:, None] < part[None, :])).astype(np.float32),
        "allb": (part[:, None] < part[None, :]).astype(np.float32),
        "iota": rep(np.arange(SLOTS, dtype=np.float32)),
        "idhi": (tokid // 256).astype(np.float32), "idlo": (tokid % 256).astype(np.float32),
        "bit": np.full((128, 1), -2 ** 31, np.int32),
        "fw1": f["L0_ffn_w1"].reshape(KC, 128, FF).transpose(1, 0, 2), "fb1": f["L0_ffn_b1"].reshape(NHB, 128).T,
        "fw2": f["L0_ffn_w2"].reshape(NHB, 128, C).transpose(1, 0, 2), "fb2": rep(f["L0_ffn_b2"]),
    }


def kernel(**inputs):
    import numpy as np
    import concourse.bacc as bacc
    from concourse.bass_utils import run_bass_kernel_spmd

    nc = bacc.Bacc("TRN2", target_bir_lowering=False, num_devices=1)
    arrays, A = {}, {}
    for name, a in lay_out(inputs).items():
        a = np.ascontiguousarray(a)
        arrays[f"in_{name}"] = a
        A[name] = nc.dram_tensor(f"in_{name}", a.shape, mybir.dt.from_np(a.dtype), kind="ExternalInput").ap()
    A["out"] = nc.dram_tensor("out_h", (NB, NTOK, C), F32, kind="ExternalOutput").ap()
    A["out_rows"] = A["out"].rearrange("b n c -> (b n) c")
    A["x2d"] = nc.dram_tensor("x2_scratch", (NB, NTOK, C), F32).ap()
    A["wd"] = nc.dram_tensor("w_scratch", (NB, 8 * SEG), F32).ap()
    A["clsd"] = nc.dram_tensor("cls_scratch", (NB, C), F32).ap()
    attention_program(nc, A)
    with ExitStack() as ctx:
        ids = select_program(nc, A, ctx)
        feed_forward_program(nc, A, ids)
    r = run_bass_kernel_spmd(nc, [arrays], core_ids=[0])
    return r.results[0]["out_h"]
```

```python
from contextlib import ExitStack

import concourse.bass as bass
from concourse import mybir
from concourse.bass import ds

ALU = mybir.AluOpType
ACT = mybir.ActivationFunctionType
F32 = mybir.dt.float32
BF16 = mybir.dt.bfloat16
FP16 = mybir.dt.float16
I32 = mybir.dt.int32
AX = mybir.AxisListType.X

NB, C, HT, WD = 16, 256, 56, 56
WS, NH, E = 4, 8, 32
NWR = HT // WS
STEP = WS * WD
NTOK = HT * WD + 1
BLK = 32
NJ = STEP // BLK
TT = STEP // 2
KC = C // 128
NS = NB * NWR
HID, NMEM = 128, 4
KCOL = NTOK + NMEM
FF = 1024
NHB = FF // 128
KK = int(0.5 * NTOK) - 1
NSEL = NB * KK
NPAIR = (NSEL + 255) // 256
SLOTS = NPAIR * 2
SEG = 400
LASTROW = NTOK - 7 * SEG
EPS = 1e-5
TINY2 = 1e-12 ** 2 / C
NEG = -1e30
ISC = float(1.0 / (E ** 0.5))
QSC = float(E ** -0.5)
OUTLAG = 3 + NWR
RING = 20
CR = 4



def link(eng, ins, sem, value):
    ins.then_inc(sem, 1)
    eng.wait_ge(sem, value)


def pool_waits(nc, dot, n):
    nc.gpsimd.tensor_tensor(dot[:, n:n + 1], dot[:, 0:1], dot[:, 0:1], ALU.add)


def schedule(eng, body):
    stages = ("proj", "attn", "mix", "lin", "tq")
    every = set(stages)

    def ctx(i):
        return {"ctx"} if i == 3 else set()

    for f in range(6):
        body(f, 0, f, f % 2, {n for lag, n in enumerate(stages) if f >= lag})
    with eng.Fori(6, NWR - 1, 2) as i:
        body(i, 0, i, 0, every)
        body(i + 1, 0, i + 1, 1, every)
    for i in range(6):
        body(NWR + i, 1, i, i % 2, every | {n for n, k in (("out", 3), ("fin", 4)) if i >= k} | ctx(i))
    every = every | {"out", "fin"}
    with eng.Fori(6, NWR - 1, 2) as i:
        body(i + NWR, 1, i, 0, every)
        body(i + (NWR + 1), 1, i + 1, 1, every)
    for i in range(6):
        body(2 * NWR + i, 2, i, i % 2, every | ctx(i))
    with eng.Fori(2, NB - 1) as b:
        base = eng.snap(b * NWR)
        with eng.Fori(6, NWR - 1, 2) as i:
            F = eng.snap(base + i)
            body(F, b, i, 0, every)
            body(F + 1, b, i + 1, 1, every)
        for i in range(6):
            body(base + NWR + i, b + 1, i, i % 2, every | ctx(i))
    with eng.Fori(6, NWR - 1, 2) as i:
        body(i + (NS - NWR), NB - 1, i, 0, every)
        body(i + (NS - NWR + 1), NB - 1, i + 1, 1, every)
    for i in range(6):
        body(NS + i, NB, i, i % 2, {n for lag, n in enumerate(stages) if i < lag} | {"out", "fin"} | ctx(i))
    with eng.Fori(6, NWR + 1, 2) as i:
        body(i + NS, NB, i, 0, {"out", "fin"})
        body(i + (NS + 1), NB, i + 1, 1, {"out", "fin"})
    body(NS + OUTLAG - 1, NB, OUTLAG - 1, 0, {"out", "fin"})
    body(NS + OUTLAG, NB, OUTLAG, 1, {"fin"})


def ring(F, lag, size):
    return ((F - lag) % RING) * size


def attention_program(nc, A):
    out, x2d, wd, clsd = A["out"], A["x2d"], A["wd"], A["clsd"]
    with ExitStack() as ctx:
        def sb(name, shape, dt=F32):
            return ctx.enter_context(nc.sbuf_tensor(name, shape, dt))

        bank = [ctx.enter_context(nc.psum_tensor(f"bank{n}", [128, 512], F32)) for n in range(8)]
        P_QV, P_K, P_SC, P_PV, P_W2, P_T, P_LIN, P_LK = bank

        w1T = sb("w1T", [128, KC, 6, 128]); b1c = sb("b1c", [128, 6])
        w2T = sb("w2T", [128, KC, C]); b2r = sb("b2r", [128, C])
        tbl = sb("tbl", [128, 2, STEP]); posr = sb("posr", [128, STEP])
        ident = sb("ident", [128, 128])
        gpre = sb("gpre", [128, KC]); wlin = sb("wlin", [128, KC, 3 * HID])
        wout = sb("wout", [128, C]); hmask = sb("hmask", [128, 128])
        bor = sb("bor", [128, C]); gor = sb("gor", [128, C]); wrr = sb("wrr", [128, C]); brr = sb("brr", [128, 1])
        bvr = sb("bvr", [128, 2, TT])
        xw = sb("xw", [128, 2, KC, STEP])
        klin = sb("klin", [128, 2, 2, STEP])
        qblk = sb("qblk", [128, 2, 2 * NJ, 4, BLK]); vblk = sb("vblk", [128, 2, 2 * NJ, 4, BLK])
        sc = sb("sc", [128, 2 * NJ, BLK]); scs = sb("scs", [128, 2 * NJ, BLK])
        pr = sb("pr", [128, 2 * NJ, BLK]); prn = sb("prn", [128, 2 * NJ, BLK])
        smx = sb("smx", [128, 2 * NJ]); ssm = sb("ssm", [128, 2 * NJ]); srec = sb("srec", [128, 2 * NJ])
        pT = sb("pT", [128, 2, 2 * NJ, BLK])
        oT = sb("oT", [128, 2, STEP])
        hh = sb("hh", [TT, 2, 2, C]); bst = sb("bst", [TT, 2, 6]); mv = sb("mv", [TT, 2, 2])
        rcv = sb("rcv", [TT, 2]); pwi = sb("pwi", [TT, 4]); pwo = sb("pwo", [TT, 4])
        mhalf = sb("mhalf", [TT, 4])
        gsc = sb("gsc", [TT, 2]); asc = sb("asc", [TT, 2, 2]); nmr = sb("nmr", [TT, 2, 2])
        xn = sb("xn", [TT, 2, C]); xnT = sb("xnT", [128, KC, STEP])
        s1 = sb("s1", [TT, RING * 2 * C]); qTs = sb("qTs", [128, RING * STEP])
        qraw = sb("qraw", [TT, 8, 32]); qmx = sb("qmx", [TT, 8]); qsh = sb("qsh", [TT, 8, 32])
        qex = sb("qex", [TT, 8, 32]); qsm = sb("qsm", [TT, 8]); qrc = sb("qrc", [TT, 8]); qs = sb("qs", [TT, 8, 32])
        kT = sb("kT", [128, KCOL]); kcst = sb("kcst", [128, 1 + NMEM])
        vst = sb("vst", [TT, 2 * NWR + 1, HID]); kN = sb("kN", [TT, 2, 4 * 128])
        kmx = sb("kmx", [128, 1]); nkmx = sb("nkmx", [128, 1]); ksum = sb("ksum", [128, 1]); krc = sb("krc", [128, 1])
        ctxT = sb("ctxT", [128, 128]); Mw = sb("Mw", [128, C]); Mq = sb("Mq", [128, C]); boq = sb("boq", [128, C])
        qc = sb("qc", [128, 2, STEP])
        ob = sb("ob", [TT, 2, C]); osq = sb("osq", [TT, 2, C]); oss = sb("oss", [TT, 2])
        onr = sb("onr", [TT, 2]); ors = sb("ors", [TT, 2]); v2 = sb("v2", [TT, 2]); ou = sb("ou", [TT, 2, C])
        h2 = sb("h2", [TT, 2, C]); bst2 = sb("bst2", [TT, 2, 6]); mv2 = sb("mv2", [TT, 2, 2]); r2 = sb("r2", [TT, 2])
        x2 = sb("x2", [TT, 2, 2, C]); bs = sb("bs", [TT, 2, 2, C]); wj = sb("wj", [TT, 2, C])
        ws0 = sb("ws0", [TT, 2]); wsv = sb("wsv", [TT, 2, 2])
        clsq = sb("clsq", [128, 1]); clso = sb("clso", [1, 2, C]); pdot = sb("pdot", [1, 8]); vdot = sb("vdot", [1, 4])
        clss = sb("clss", [TT, C]); clsr = sb("clsr", [TT, C])

        S = {}
        steps = dict(tensor="q_ps k_ps v_ps sc_ps pv_ps w2_ps tx_ps lin_ps lk_ps tq_ps o2_ps".split(),
                     scalar="qb k_lin sm_e o_t xnt q_cp v_cp k_cp qm_e q_t o2_q s1_d".split(),
                     vector="vb sm_a sm_s sm_p sm_t h_a ln_v v2_d ln_s xn_d qm_s qm_d u_d x2_d w_dn".split(),
                     gpsimd="ln_p or_p r2_p qc_d h2_d bs_d".split())
        for n in sum(steps.values(), []) + ("or_c x_ld0 x_ld1 w_ld ini sm_c ln_c qm_c o2_c st_d0 st_d1 ctx_m ctx_e ctx_t "
                                            "ctx_n ctx_ps ctx_c ctx_x ctx_mp ctx_mw cls_ps cls_c cls_st kc_d "
                                            "bv_d bv_p set_d set_p set_a set_g tbl_d fin_x fin_p fin_ld fin_d fin_a fin_st").split():
            S[n] = ctx.enter_context(nc.semaphore(n))

        def at(eng, name, s):
            eng.wait_ge(S[name], s + (1 + CR))

        x_ld, st_d = (S["x_ld0"], S["x_ld1"]), (S["st_d0"], S["st_d1"])

        def stored(eng, e, s):
            eng.wait_ge(st_d[e], (s - e) * 24 + 48)

        def credit(eng, who):
            for n in steps[who]:
                eng.sem_inc(S[n], CR)

        loads = [(w1T, "w1T"), (b1c, "b1c"), (w2T, "w2T"), (b2r, "b2r"), (posr, "posr"), (tbl, "mask"),
                 (ident, "ident"), (gpre, "gpre"), (wlin, "wlin"), (wout, "wout"), (hmask, "hmask"),
                 (bor, "bor"), (gor, "gor"), (wrr, "wrr"), (brr, "brr"), (clsr, "clsr")]
        W_ALL = 16 * (len(loads) + 3)

        LN_LINKS = 12

        def layer_norm_1(h, par, lnk, done, powered, free):
            for t in range(2):
                ins = nc.vector.bn_stats(bst[:, t, :], h[:, t, :])
            lnk(ins, 1)
            nc.vector.tensor_copy(vdot[:, 1:2], vdot[:, 0:1])
            for t in range(2):
                ins = nc.vector.bn_aggr(mv[:, t, :], bst[:, t, :])
            lnk(ins, 2)
            mean, var = mv[:, :, 0], mv[:, :, 1]
            lnk(nc.vector.tensor_scalar(pwi[:, 0:2], var, EPS, None, ALU.add), 3)
            lnk(nc.vector.reciprocal(rcv[:], pwi[:, 0:2]), 4)
            nc.vector.scalar_tensor_tensor(out=pwi[:, 2:4], in0=var, scalar=TINY2 * EPS, in1=rcv[:],
                                           op0=ALU.max, op1=ALU.mult).then_inc(*done("ln_v"))
            powered()
            nc.vector.tensor_scalar(asc[:, par, :], pwo[:, 0:2], 1.0, None, ALU.add)
            nc.vector.scalar_tensor_tensor(out=nmr[:, par, :], in0=mean, scalar=-1.0, in1=pwo[:, 0:2],
                                           op0=ALU.mult, op1=ALU.mult).then_inc(*done("ln_s"))
            lnk(nc.vector.tensor_tensor(gsc[:], pwo[:, 0:2], pwo[:, 2:4], ALU.mult), 5)
            free()
            for t in range(2):
                ins = nc.vector.tensor_scalar(xn[:, t, :], h[:, t, :], mv[:, t, 0:1], gsc[:, t:t + 1],
                                              ALU.subtract, ALU.mult)
            ins.then_inc(*done("xn_d"))

        def group(ap):
            return ap[:].rearrange("p (g o) -> p g o", o=1).broadcast_to([ap.shape[0], ap.shape[1], 32])

        def transpose_xn(pe):
            for t in range(2):
                for k in range(KC):
                    ins = nc.tensor.transpose(P_T[:, k * STEP + t * TT:k * STEP + (t + 1) * TT],
                                              xn[:, t, k * 128:(k + 1) * 128], ident[0:TT, 0:TT])
            return ins

        def lin_qv(pe):
            for t in range(2):
                for k in range(KC):
                    ins = nc.tensor.matmul(P_LIN[0:TT, t * 256:(t + 1) * 256], xnT[:, k, t * TT:(t + 1) * TT],
                                           wlin[:, k, 0:256], start=(k == 0), stop=(k == KC - 1))
            return ins

        def lin_k(pe):
            for k in range(KC):
                ins = nc.tensor.matmul(P_LK[:, 0:STEP], wlin[:, k, 256:384], xnT[:, k, :],
                                       start=(k == 0), stop=(k == KC - 1))
            return ins

        def transpose_q(pe):
            for t in range(2):
                ins = nc.tensor.transpose(P_T[:, t * TT:(t + 1) * TT],
                                          qs[:, 4 * t:4 * t + 4, :].rearrange("p g d -> p (g d)"), ident[0:TT, 0:TT])
            return ins

        p_lin3 = P_LIN[0:TT, :].rearrange("p (t n) -> p t n", t=2)

        with nc.Block() as block:
            @block.sync
            def _(sp):
                for dst, name in loads:
                    sp.dma_start(dst[:], A[name]).then_inc(S["w_ld"], 16)
                sp.dma_start(kcst[:, 1:1 + NMEM], A["memk"]).then_inc(S["w_ld"], 16)
                sp.dma_start(vst[1:1 + NMEM, 2 * NWR, :], A["memv"]).then_inc(S["w_ld"], 16)
                sp.dma_start(wd, A["wpad"]).then_inc(S["w_ld"], 16)
                sp.wait_ge(S["w_ld"], W_ALL)

            @block.vector
            def _(dve):
                dve.wait_ge(S["w_ld"], W_ALL)
                n = [0]

                def lnk(ins, k=None):
                    n[0] += 1
                    link(dve, ins, S["set_d"], n[0])

                lnk(nc.vector.memset(vdot[:], 0.0))
                for m in range(2):
                    ins = nc.vector.tensor_copy(bvr[:, m, :], b1c[:, 4 + m:5 + m].broadcast_to([128, TT]))
                ins.then_inc(S["bv_d"], 1)
                dve.wait_ge(S["bv_p"], 1)
                lnk(nc.vector.tensor_tensor(b2r[0:TT], b2r[0:TT], P_W2[0:TT, 0:C], ALU.add))
                for v in range(2):
                    nc.vector.tensor_tensor(tbl[:, v, :], tbl[:, v, :], posr[:], ALU.add).then_inc(S["tbl_d"], 1)
                lnk(nc.vector.tensor_scalar(boq[:], bor[:], 1.0 / (HID // 32), None, ALU.mult))
                for k in range(KC):
                    lnk(nc.vector.tensor_scalar(wlin[:, k, :], wlin[:, k, :], gpre[:, k:k + 1], None, ALU.mult))
                for t in range(2):
                    lnk(nc.vector.tensor_copy(hh[:, 0, t, :], clsr[:]))
                layer_norm_1(hh[:, 0], 0, lnk, lambda name: (S["ini"], 1), lambda: dve.wait_ge(S["set_g"], 5),
                             lambda: None)
                dve.wait_ge(S["ini"], 3)
                lnk(nc.vector.tensor_scalar(clss[:], clsr[:], asc[:, 0, 0:1], nmr[:, 0, 0:1], ALU.mult, ALU.add))
                dve.wait_ge(S["set_p"], 1)
                nc.vector.tensor_copy(xnT[:].rearrange("p k t -> p (k t)"), P_T[:, 0:KC * STEP]).then_inc(S["ini"], 1)
                dve.wait_ge(S["set_p"], 2)
                nc.vector.tensor_copy(vst[0:1, 2 * NWR, :], P_LIN[0:1, 128:256])
                nc.vector.tensor_copy(kcst[:, 0:1], P_LK[:, 0:1])
                lnk(nc.vector.tensor_copy(qraw[:].rearrange("p (t g) d -> p t (g d)", t=2), p_lin3[:, :, 0:128]))
                nc.vector.tensor_copy(kT[:, NTOK - 1:KCOL], kcst[:])
                lnk(nc.vector.tensor_reduce(qmx[:], qraw[:], AX, ALU.max))
                nc.vector.tensor_tensor(qsh[:], qraw[:], group(qmx), ALU.subtract).then_inc(S["ini"], 1)
                dve.wait_ge(S["set_a"], 1)
                lnk(nc.vector.tensor_reduce(qsm[:], qex[:], AX, ALU.add))
                lnk(nc.vector.reciprocal(qrc[:], qsm[:]))
                nc.vector.tensor_tensor(qs[:], qex[:], group(qrc), ALU.mult).then_inc(S["ini"], 1)
                dve.wait_ge(S["set_p"], 3)
                lnk(nc.vector.tensor_copy(clsq[:], P_T[:, 0:1]))
                credit(dve, "vector")

            @block.scalar
            def _(act):
                act.wait_ge(S["ini"], 5)
                nc.scalar.activation(qex[:], qsh[:], ACT.Exp).then_inc(S["set_a"], 1)
                credit(act, "scalar")

            @block.tensor
            def _(pe):
                pe.wait_ge(S["w_ld"], W_ALL)
                pe.wait_ge(S["bv_d"], 1)
                for m in range(2):
                    ins = nc.tensor.matmul(P_W2[0:TT, 0:C], bvr[:, m, :], w2T[:, m, :], start=(m == 0), stop=(m == 1))
                ins.then_inc(S["bv_p"], 1)
                pe.wait_ge(S["ini"], 3)
                transpose_xn(pe).then_inc(S["set_p"], 1)
                pe.wait_ge(S["ini"], 4)
                lin_qv(pe)
                lin_k(pe).then_inc(S["set_p"], 1)
                pe.wait_ge(S["ini"], 6)
                transpose_q(pe).then_inc(S["set_p"], 1)
                credit(pe, "tensor")
                pe.sem_inc(S["ctx_ps"], 2)

            @block.gpsimd
            def _(pool):
                nc.gpsimd.memset(qblk[:], 0.0).then_inc(S["set_g"], 1)
                nc.gpsimd.memset(vblk[:], 0.0).then_inc(S["set_g"], 1)
                nc.gpsimd.memset(pdot[:], 0.0).then_inc(S["set_g"], 1)
                nc.gpsimd.memset(mhalf[:], -0.5).then_inc(S["set_g"], 1)
                pool.wait_ge(S["set_g"], 4)
                pool.wait_ge(S["ini"], 1)
                nc.gpsimd.tensor_tensor(pwo[:], pwi[:], mhalf[:], ALU.pow).then_inc(S["set_g"], 1)
                credit(pool, "gpsimd")

        with nc.Block() as block:
            @block.sync
            def _(sp):
                for e in range(2):
                    sp.sem_inc(st_d[e], 48)
                sp.dma_start(xw[:, 0], A["xw"][0]).then_inc(x_ld[0], 16)
                o3, x3, w1d = A["out_rows"], x2d.rearrange("b n c -> (b n) c"), wd.rearrange("b n -> (b n)")

                def body(F, b, i, e, on):
                    if "fin" in on:
                        s = F - OUTLAG - 1
                        bo = b - 1 if not isinstance(i, int) or i > OUTLAG - NWR else b - 2
                        r0 = s * STEP + bo + 1
                        w0 = s * STEP + bo * (8 * SEG - NWR * STEP) + 1
                    if "proj" in on:
                        at(sp, "v_ps", F - 1)
                        sp.dma_start(xw[:, 1 - e:2 - e], A["xw"][ds(F + 1, 1)].rearrange("s p k t -> p s k t"))\
                            .then_inc(x_ld[1 - e], 16)
                    if "ctx" in on:
                        sp.wait_ge(S["cls_c"], b)
                        sp.dma_start(clsd[ds(b - 1, 1), :], clso[0:1, 0, :]).then_inc(S["cls_st"], 16)
                    if "fin" in on:
                        at(sp, "bs_d", s)
                        sp.dma_start(o3[ds(r0, STEP), :].rearrange("(t p) c -> p t c", p=TT), bs[:, e])\
                            .then_inc(st_d[e], 16)
                        at(sp, "w_dn", s)
                        sp.dma_start(x3[ds(r0, STEP), :].rearrange("(t p) c -> p t c", p=TT), x2[:, e])\
                            .then_inc(st_d[e], 16)
                        sp.dma_start(w1d[ds(w0, STEP)]
                                     .rearrange("(t p) -> p t", p=TT), wsv[:, e, :],
                                     allow_slow_non_contiguous=True).then_inc(st_d[e], 16)
                schedule(sp, body)
                for e in range(2):
                    sp.wait_ge(st_d[e], 48 + 24 * NS)
                sp.wait_ge(S["cls_st"], 16 * NB)
                sp.wait_ge(x_ld[0], 8 * NS + 16)

            @block.gpsimd
            def _(pool):
                def body(F, b, i, e, on):
                    if "fin" in on:
                        s = F - OUTLAG - 1
                        at(pool, "u_d", s)
                        at(pool, "s1_d", s)
                        at(pool, "x2_d", s - 1)
                        at(pool, "bs_d", s - 1)
                        nc.gpsimd.tensor_tensor(h2[:].rearrange("p t c -> p (t c)"), ou[:].rearrange("p t c -> p (t c)"),
                                                s1[:, ds(ring(F, OUTLAG + 1, 2 * C), 2 * C)], ALU.add)\
                            .then_inc(S["h2_d"], 1)
                    if "out" in on:
                        s = F - OUTLAG
                        at(pool, "q_t", s)
                        at(pool, "o2_ps", s - 2)
                        pool_waits(nc, pdot, 1)
                        nc.gpsimd.tensor_copy(qc[:, e, :], qTs[:, ds(ring(F, OUTLAG, STEP), STEP)])\
                            .then_inc(S["qc_d"], 1)
                    if "fin" in on:
                        at(pool, "v2_d", F - OUTLAG - 1)
                        nc.gpsimd.tensor_tensor(r2[:], v2[:], mhalf[:, 0:2], ALU.pow).then_inc(S["r2_p"], 1)
                    if "out" in on:
                        s = F - OUTLAG
                        at(pool, "o2_q", s)
                        pool_waits(nc, pdot, 2)
                        nc.gpsimd.tensor_scalar(onr[:], oss[:], TINY2, None, ALU.max).then_inc(S["or_c"], 1)
                        pool.wait_ge(S["or_c"], s + 1)
                        nc.gpsimd.tensor_tensor(ors[:], onr[:], mhalf[:, 0:2], ALU.pow).then_inc(S["or_p"], 1)
                    if "mix" in on:
                        at(pool, "ln_v", F - 2)
                        nc.gpsimd.tensor_tensor(pwo[:], pwi[:], mhalf[:], ALU.pow).then_inc(S["ln_p"], 1)
                    if "fin" in on:
                        s = F - OUTLAG - 1
                        at(pool, "x2_d", s)
                        at(pool, "h2_d", s)
                        stored(pool, e, s)
                        nc.gpsimd.tensor_tensor(bs[:, e], h2[:], x2[:, e], ALU.add).then_inc(S["bs_d"], 1)
                schedule(pool, body)

            @block.scalar
            def _(act):
                def body(F, b, i, e, on):
                    if "tq" in on:
                        s = F - 4
                        at(act, "qm_s", s)
                        at(act, "qm_d", s - 1)
                        nc.scalar.activation(qex[:], qsh[:], ACT.Exp).then_inc(S["qm_e"], 1)
                    if "lin" in on:
                        s = F - 3
                        at(act, "ln_s", s)
                        for t in range(2):
                            ins = nc.scalar.activation(s1[:, ds(ring(F, 3, 2 * C) + t * C, C)], hh[:, 1 - e, t, :],
                                                       ACT.Identity, bias=nmr[:, 1 - e, t:t + 1], scale=asc[:, 1 - e, t:t + 1])
                        ins.then_inc(S["s1_d"], 1)
                    if "proj" in on:
                        at(act, "q_ps", F)
                        at(act, "sc_ps", F - 2)
                        for h in range(4):
                            r = slice(32 * h, 32 * h + 32)
                            for m in range(2):
                                ins = nc.scalar.activation(
                                    qblk[r, e, m * NJ:(m + 1) * NJ, h, :],
                                    P_QV[r, m * STEP:(m + 1) * STEP].rearrange("p (j q) -> p j q", q=BLK),
                                    ACT.Identity, bias=b1c[r, m:m + 1])
                        ins.then_inc(S["qb"], 1)
                    if "ctx" in on:
                        act.wait_ge(S["ctx_m"], b)
                        nc.scalar.activation(kT[:], kT[:], ACT.Exp, bias=nkmx[:, 0:1], accum_out=ksum[:, 0:1])\
                            .then_inc(S["ctx_e"], 1)
                        for g in range(8):
                            act.wait_ge(S["ctx_t"], b * 8 - 8 + g + 1)
                            act.wait_ge(S["ctx_ps"], b * 8 - 8 + g + 1)
                            src = P_LK if g % 2 else P_K
                            if g < 7:
                                ins = nc.scalar.activation(kN[:, g % 2, :], src[0:TT, :], ACT.Copy)
                            else:
                                ins = nc.scalar.activation(kN[0:1 + NMEM, g % 2, 0:128], src[0:1 + NMEM, 0:128], ACT.Copy)
                            ins.then_inc(S["ctx_n"], 1)
                        nc.scalar.activation(kT[:, NTOK - 1:KCOL], kcst[:], ACT.Copy).then_inc(S["kc_d"], 1)
                    if "proj" in on:
                        at(act, "k_ps", F)
                        at(act, "sc_ps", F - 2)
                        for m in range(2):
                            ins = nc.scalar.activation(klin[:, e, m, :], P_K[:, m * STEP:(m + 1) * STEP], ACT.Identity,
                                                       bias=b1c[:, 2 + m:3 + m])
                        ins.then_inc(S["k_lin"], 1)
                    if "lin" in on:
                        s = F - 3
                        at(act, "tx_ps", s)
                        at(act, "lk_ps", s - 1)
                        nc.scalar.activation(xnT[:].rearrange("p k t -> p (k t)"), P_T[:, 0:KC * STEP], ACT.Copy)\
                            .then_inc(S["xnt"], 1)
                    if "attn" in on:
                        s = F - 1
                        at(act, "sm_s", s)
                        at(act, "sm_p", s - 1)
                        nc.scalar.activation(pr[:], scs[:], ACT.Exp).then_inc(S["sm_e"], 1)
                    if "lin" in on:
                        s = F - 3
                        at(act, "lin_ps", s)
                        at(act, "qm_s", s - 1)
                        nc.scalar.activation(qraw[:].rearrange("p (t g) d -> p t (g d)", t=2), p_lin3[:, :, 0:128],
                                             ACT.Copy).then_inc(S["q_cp"], 1)
                        i3 = i - 3 if not isinstance(i, int) or i >= 3 else i - 3 + NWR
                        nc.scalar.activation(vst[:, ds(i3 * 2, 2), :], p_lin3[:, :, 128:256], ACT.Copy)\
                            .then_inc(S["v_cp"], 1)
                    if "mix" in on:
                        s = F - 2
                        at(act, "pv_ps", s)
                        at(act, "w2_ps", s - 1)
                        for m in range(2):
                            ins = nc.scalar.activation(
                                oT[:, m, :].rearrange("p (r w c) -> p r w c", r=WS, c=WS),
                                P_PV[:, m * STEP:(m + 1) * STEP].rearrange("p (w r c) -> p r w c", r=WS, c=WS), ACT.Copy)
                        ins.then_inc(S["o_t"], 1)
                    if "out" in on:
                        s = F - OUTLAG
                        at(act, "o2_ps", s)
                        at(act, "u_d", s - 1)
                        for t in range(2):
                            ins = nc.scalar.activation(osq[:, t, :], P_K[0:TT, t * C:(t + 1) * C], ACT.Square, scale=float(C) ** -0.5,
                                                       accum_out=oss[:, t:t + 1])
                        ins.then_inc(S["o2_q"], 1)
                    if "lin" in on:
                        s = F - 3
                        at(act, "lk_ps", s)
                        nc.scalar.activation(kT[:, ds(i3 * STEP, STEP)], P_LK[:, 0:STEP], ACT.Copy)\
                            .then_inc(S["k_cp"], 1)
                    if "tq" in on:
                        s = F - 4
                        at(act, "tq_ps", s)
                        nc.scalar.activation(qTs[:, ds(ring(F, 4, STEP), STEP)], P_T[:, 0:STEP], ACT.Copy)\
                            .then_inc(S["q_t"], 1)
                schedule(act, body)

            @block.tensor
            def _(pe):
                def project(e, f, P, name):
                    for m in range(2):
                        for k in range(KC):
                            ins = nc.tensor.matmul(P[:, m * STEP:(m + 1) * STEP], w1T[:, k, f + m, :],
                                                   xw[:, e, k, :],
                                                   start=(k == 0), stop=(k == KC - 1))
                    ins.then_inc(S[name], 1)

                def scores(e, m):
                    for n in range(m * NJ, (m + 1) * NJ):
                        ins = nc.tensor.matmul(P_SC[:, n * BLK:(n + 1) * BLK],
                                               qblk[:, e, n, :, :].rearrange("p h q -> p (h q)"),
                                               klin[:, e, m, (n - m * NJ) * BLK:(n - m * NJ + 1) * BLK],
                                               start=True, stop=True)
                    return ins

                def attend(e, m):
                    for n in range(m * NJ, (m + 1) * NJ):
                        ins = nc.tensor.matmul(P_PV[:, n * BLK:(n + 1) * BLK],
                                               vblk[:, e, n, :, :].rearrange("p h q -> p (h q)"),
                                               pT[:, e, n, :], start=True, stop=True)
                    return ins

                def body(F, b, i, e, on):
                    if "attn" in on:
                        s = F - 1
                        at(pe, "qb", s)
                        at(pe, "k_lin", s)
                        at(pe, "sm_a", s - 1)
                        scores(1 - e, 0)
                    if "proj" in on:
                        pe.wait_ge(x_ld[e], (F - e) * 8 + 16)
                        at(pe, "vb", F - 1)
                        project(e, 0, P_QV, "q_ps")
                    if "attn" in on:
                        scores(1 - e, 1).then_inc(S["sc_ps"], 1)
                    if "fin" in on:
                        at(pe, "u_d", F - OUTLAG - 1)
                    if "ctx" in on:
                        pe.wait_ge(S["ctx_e"], b)
                        at(pe, "k_cp", F - 4)
                        at(pe, "q_cp", F - 4)
                        at(pe, "v_cp", F - 4)

                        def turn(g):
                            if g >= 2:
                                pe.wait_ge(S["ctx_n"], b * 8 - 8 + g - 1)
                            P = P_LK if g % 2 else P_K
                            if g < 7:
                                for q in range(4):
                                    c0 = (4 * g + q) * TT
                                    ins = nc.tensor.transpose(P[0:TT, q * 128:(q + 1) * 128], kT[:, c0:c0 + TT], ident[:])
                            else:
                                ins = nc.tensor.transpose(P[0:1 + NMEM, 0:128], kT[:, NTOK - 1:KCOL], ident[:])
                            ins.then_inc(S["ctx_t"], 1)

                        def sum_up(g):
                            pe.wait_ge(S["ctx_n"], b * 8 - 8 + g + 1)
                            for q in range(4 if g < 7 else 1):
                                r = TT if g < 7 else 1 + NMEM
                                ins = nc.tensor.matmul(P_LIN[:, 0:128], vst[0:r, 4 * g + q, :],
                                                       kN[0:r, g % 2, q * 128:(q + 1) * 128],
                                                       start=(g == 0 and q == 0), stop=(g == 7))
                            ins.then_inc(S["ctx_ps"], 1)

                        turn(0)
                        turn(1)
                        for g in range(8):
                            sum_up(g)
                            if g + 2 < 8:
                                turn(g + 2)
                        pe.wait_ge(S["ctx_x"], b)
                        nc.tensor.matmul(P_LIN[:, 256:512], ctxT[:], wout[:], start=True, stop=True).then_inc(S["ctx_mp"], 1)
                        pe.wait_ge(S["ctx_mw"], b)
                        nc.tensor.matmul(P_LIN[0:1, 0:C], clsq[:], Mw[:], start=True, stop=True).then_inc(S["cls_ps"], 1)
                        pe.wait_ge(S["cls_c"], b)
                    if "proj" in on:
                        at(pe, "k_lin", F - 1)
                        project(e, 2, P_K, "k_ps")
                    if "lin" in on:
                        s = F - 3
                        at(pe, "xn_d", s)
                        at(pe, "q_t", s - 2)
                        transpose_xn(pe).then_inc(S["tx_ps"], 1)
                    if "mix" in on:
                        s = F - 2
                        at(pe, "sm_t", s)
                        at(pe, "vb", s)
                        at(pe, "o_t", s - 1)
                        attend(e, 0)
                    if "lin" in on:
                        s = F - 3
                        at(pe, "xnt", s)
                        at(pe, "q_cp", s - 1)
                        at(pe, "v_cp", s - 1)
                        lin_qv(pe).then_inc(S["lin_ps"], 1)
                    if "mix" in on:
                        attend(e, 1).then_inc(S["pv_ps"], 1)
                    if "proj" in on:
                        at(pe, "qb", F)
                        project(e, 4, P_QV, "v_ps")
                    if "mix" in on:
                        s = F - 2
                        at(pe, "o_t", s)
                        at(pe, "h_a", s - 1)
                        for t in range(2):
                            for m in range(2):
                                ins = nc.tensor.matmul(P_W2[0:TT, t * C:(t + 1) * C], oT[:, m, t * TT:(t + 1) * TT],
                                                       w2T[:, m, :], start=(m == 0), stop=(m == 1))
                        ins.then_inc(S["w2_ps"], 1)
                    if "out" in on:
                        s = F - OUTLAG
                        at(pe, "qc_d", s)
                        bo = b - 1 if not isinstance(i, int) or i >= OUTLAG - NWR else b - 2
                        pe.wait_ge(S["ctx_mw"], bo + 1)
                        if "proj" in on:
                            at(pe, "k_lin", F)
                        for t in range(2):
                            ins = nc.tensor.matmul(P_K[0:TT, t * C:(t + 1) * C], qc[:, e, t * TT:(t + 1) * TT], Mw[:],
                                                   start=True, stop=True)
                        ins.then_inc(S["o2_ps"], 1)
                    if "lin" in on:
                        s = F - 3
                        at(pe, "k_cp", s - 1)
                        lin_k(pe).then_inc(S["lk_ps"], 1)
                    if "tq" in on:
                        s = F - 4
                        at(pe, "qm_d", s)
                        at(pe, "xnt", s + 1) if "lin" in on else None
                        transpose_q(pe).then_inc(S["tq_ps"], 1)
                schedule(pe, body)

            @block.vector
            def _(dve):
                def finish_rows(F, e, on):
                    if "fin" in on:
                        s, o = F - OUTLAG - 1, e
                        at(dve, "r2_p", s)
                        at(dve, "bs_d", s - 2)
                        stored(dve, o, s)
                        for t in range(2):
                            ins = nc.vector.tensor_scalar(x2[:, o, t, :], h2[:, t, :], mv2[:, t, 0:1], r2[:, t:t + 1],
                                                          ALU.subtract, ALU.mult)
                        ins.then_inc(S["x2_d"], 1)
                        at(dve, "x2_d", s)
                        for t in range(2):
                            ins = nc.vector.tensor_tensor_reduce(wj[:, t, :], x2[:, o, t, :], wrr[0:TT, :], 1.0, 0.0, ALU.mult,
                                                                 ALU.add, ws0[:, t:t + 1])
                        link(dve, ins, S["o2_c"], s * 3 + 3)
                        nc.vector.tensor_scalar(wsv[:, o, :], ws0[:], brr[0:TT, 0:1], None, ALU.add).then_inc(S["w_dn"], 1)

                def body(F, b, i, e, on):
                    if "ctx" in on:
                        at(dve, "k_cp", F - 4)
                        if not isinstance(b, int) or b > 1:
                            dve.wait_ge(S["kc_d"], b - 1)
                            dve.wait_ge(S["ctx_e"], b - 1)
                        link(dve, nc.vector.tensor_reduce(kmx[:], kT[:], AX, ALU.max), S["ctx_c"], b * 3 - 2)
                        nc.vector.tensor_scalar(nkmx[:], kmx[:], -1.0, None, ALU.mult).then_inc(S["ctx_m"], 1)
                    if "fin" in on:
                        s = F - OUTLAG - 1
                        at(dve, "or_p", s)
                        at(dve, "h2_d", s - 1)
                        for t in range(2):
                            ins = nc.vector.scalar_tensor_tensor(out=ou[:, t, :], in0=P_K[0:TT, t * C:(t + 1) * C], scalar=ors[:, t:t + 1],
                                                                 in1=gor[0:TT, :], op0=ALU.mult, op1=ALU.mult)
                        ins.then_inc(S["u_d"], 1)
                    if "tq" in on:
                        s = F - 4
                        at(dve, "qm_e", s)
                        link(dve, nc.vector.tensor_reduce(qsm[:], qex[:], AX, ALU.add), S["qm_c"], s * 3 + 2)
                        link(dve, nc.vector.reciprocal(qrc[:], qsm[:]), S["qm_c"], s * 3 + 3)
                        at(dve, "tq_ps", s - 1)
                        nc.vector.tensor_tensor(qs[:], qex[:], group(qrc), ALU.mult).then_inc(S["qm_d"], 1)
                    if "attn" in on:
                        s, p = F - 1, 1 - e
                        last_row = isinstance(i, int) and i == 0
                        at(dve, "sc_ps", s)
                        for m in range(2):
                            ins = nc.vector.scalar_tensor_tensor(
                                out=sc[:, m * NJ:(m + 1) * NJ, :].rearrange("p j q -> p (j q)"),
                                in0=P_SC[:, m * STEP:(m + 1) * STEP], scalar=ISC, in1=tbl[:, int(last_row), :],
                                op0=ALU.mult, op1=ALU.add)
                        ins.then_inc(S["sm_a"], 1)
                        at(dve, "sm_a", s)
                        link(dve, nc.vector.tensor_reduce(smx[:], sc[:], AX, ALU.max), S["sm_c"], s * 3 + 1)
                        at(dve, "sm_e", s - 1)
                        nc.vector.tensor_tensor(scs[:], sc[:], group(smx), ALU.subtract).then_inc(S["sm_s"], 1)
                    if "fin" in on:
                        s = F - OUTLAG - 1
                        at(dve, "h2_d", s)
                        for t in range(2):
                            ins = nc.vector.bn_stats(bst2[:, t, :], h2[:, t, :])
                        link(dve, ins, S["o2_c"], s * 3 + 1)
                        nc.vector.tensor_copy(vdot[:, 2:3], vdot[:, 0:1])
                        for t in range(2):
                            ins = nc.vector.bn_aggr(mv2[:, t, :], bst2[:, t, :])
                        link(dve, ins, S["o2_c"], s * 3 + 2)
                        nc.vector.tensor_scalar(v2[:], mv2[:, :, 1], EPS, None, ALU.add).then_inc(S["v2_d"], 1)
                    if "ctx" in on:
                        dve.wait_ge(S["ctx_e"], b)
                        if not isinstance(b, int) or b > 1:
                            dve.wait_ge(S["ctx_mw"], b - 1)
                        link(dve, nc.vector.reciprocal(krc[:], ksum[:]), S["ctx_c"], b * 3 - 1)
                        dve.wait_ge(S["ctx_ps"], b * 8 + 2)
                        nc.vector.tensor_tensor(ctxT[:], P_LIN[:, 0:128], hmask[:], ALU.mult).then_inc(S["ctx_x"], 1)
                        dve.wait_ge(S["ctx_mp"], b)
                        if "fin" in on:
                            at(dve, "o2_ps", F - OUTLAG - 1)
                        link(dve, nc.vector.tensor_scalar(Mq[:], P_LIN[:, 256:512], krc[:, 0:1], QSC, ALU.mult, ALU.mult),
                             S["ctx_c"], b * 3)
                        nc.vector.tensor_tensor(Mw[:], Mq[:], boq[:], ALU.add).then_inc(S["ctx_mw"], 1)
                        dve.wait_ge(S["cls_ps"], b)
                        if not isinstance(b, int) or b > 1:
                            dve.wait_ge(S["cls_st"], b * 16 - 16)
                        nc.vector.tensor_copy(clso[0:1, 0, :], P_LIN[0:1, 0:C]).then_inc(S["cls_c"], 1)
                    if "attn" in on:
                        s, p = F - 1, 1 - e
                        at(dve, "sm_e", s)
                        link(dve, nc.vector.tensor_reduce(ssm[:], pr[:], AX, ALU.add), S["sm_c"], s * 3 + 2)
                        link(dve, nc.vector.reciprocal(srec[:], ssm[:]), S["sm_c"], s * 3 + 3)
                        nc.vector.tensor_tensor(prn[:], pr[:], group(srec), ALU.mult).then_inc(S["sm_p"], 1)
                        at(dve, "sm_p", s)
                        at(dve, "pv_ps", s - 2)
                        nc.vector.transpose(pT[:, p].rearrange("p n q -> p (n q)"),
                                            prn[:].rearrange("p n q -> p (n q)")).then_inc(S["sm_t"], 1)
                    if "lin" in on:
                        s = F - 3
                        at(dve, "q_cp", s)
                        link(dve, nc.vector.tensor_reduce(qmx[:], qraw[:], AX, ALU.max), S["qm_c"], s * 3 + 1)
                        at(dve, "qm_e", s - 1)
                        nc.vector.tensor_tensor(qsh[:], qraw[:], group(qmx), ALU.subtract).then_inc(S["qm_s"], 1)
                    if "proj" in on:
                        at(dve, "v_ps", F)
                        at(dve, "pv_ps", F - 2)
                        for h in range(4):
                            r = slice(32 * h, 32 * h + 32)
                            ins = nc.vector.transpose(vblk[r, e, :, h, :],
                                                      P_QV[r, 0:2 * STEP].rearrange("p (n q) -> p n q", q=BLK))
                        ins.then_inc(S["vb"], 1)
                    if "mix" in on:
                        s = F - 2
                        at(dve, "w2_ps", s)
                        at(dve, "s1_d", s - 2)
                        ins = nc.vector.tensor_tensor(
                            hh[:, e], P_W2[0:TT, :].rearrange("p (t c) -> p t c", t=2),
                            b2r[0:TT, :].rearrange("p (o c) -> p o c", o=1).broadcast_to([TT, 2, C]), ALU.add)
                        ins.then_inc(S["h_a"], 1)
                        at(dve, "h_a", s)

                        def powered():
                            finish_rows(F, e, on)
                            at(dve, "ln_p", s)
                        layer_norm_1(hh[:, e], e, lambda ins, k: link(dve, ins, S["ln_c"], s * 5 + k),
                                     lambda name: (S[name], 1), powered, lambda: at(dve, "tx_ps", s - 1))
                    else:
                        finish_rows(F, e, on)
                schedule(dve, body)

        G = NB
        with nc.Block() as block:
            @block.sync
            def _(sp):
                sp.dma_start(ob[0:G, 0, :], clsd).then_inc(S["fin_ld"], 16)
                sp.wait_ge(S["fin_d"], 8)
                sp.dma_start(out[:, 0, :], bs[0:G, 0, 0, :]).then_inc(S["fin_st"], 16)
                sp.dma_start(x2d[:, 0, :], x2[0:G, 0, 0, :]).then_inc(S["fin_st"], 16)
                sp.dma_start(wd[:, 0:1], wsv[0:G, 0, 0:1], allow_slow_non_contiguous=True)\
                    .then_inc(S["fin_st"], 16)
                sp.wait_ge(S["fin_st"], 48)

            @block.gpsimd
            def _(pool):
                pool.wait_ge(S["fin_d"], 2)
                nc.gpsimd.tensor_tensor(ors[0:G, 0:1], onr[0:G, 0:1], mhalf[0:G, 0:1], ALU.pow).then_inc(S["fin_p"], 1)
                pool.wait_ge(S["fin_d"], 7)
                nc.gpsimd.tensor_tensor(r2[0:G, 0:1], v2[0:G, 0:1], mhalf[0:G, 0:1], ALU.pow).then_inc(S["fin_p"], 1)

            @block.scalar
            def _(act):
                act.wait_ge(S["fin_d"], 1)
                nc.scalar.activation(osq[0:G, 0, :], ob[0:G, 1, :], ACT.Square, scale=float(C) ** -0.5,
                                     accum_out=oss[0:G, 0:1]).then_inc(S["fin_a"], 1)

            @block.vector
            def _(dve):
                n = [0]

                def lnk(ins):
                    n[0] += 1
                    link(dve, ins, S["fin_d"], n[0])

                dve.wait_ge(S["fin_ld"], 16)
                lnk(nc.vector.tensor_copy(ob[0:G, 1, :], ob[0:G, 0, :]))
                dve.wait_ge(S["fin_a"], 1)
                lnk(nc.vector.tensor_scalar(onr[0:G, 0:1], oss[0:G, 0:1], TINY2, None, ALU.max))
                dve.wait_ge(S["fin_p"], 1)
                lnk(nc.vector.scalar_tensor_tensor(out=ou[0:G, 0, :], in0=ob[0:G, 1, :], scalar=ors[0:G, 0:1],
                                                   in1=gor[0:G], op0=ALU.mult, op1=ALU.mult))
                lnk(nc.vector.tensor_tensor(h2[0:G, 0, :], ou[0:G, 0, :], clss[0:G], ALU.add))
                lnk(nc.vector.bn_stats(bst2[0:G, 0, :], h2[0:G, 0, :]))
                lnk(nc.vector.bn_aggr(mv2[0:G, 0, :], bst2[0:G, 0, :]))
                lnk(nc.vector.tensor_scalar(v2[0:G, 0:1], mv2[0:G, 0, 1:2], EPS, None, ALU.add))
                dve.wait_ge(S["fin_p"], 2)
                nc.vector.tensor_scalar(x2[0:G, 0, 0, :], h2[0:G, 0, :], mv2[0:G, 0, 0:1], r2[0:G, 0:1],
                                        ALU.subtract, ALU.mult).then_inc(S["fin_x"], 1)
                dve.wait_ge(S["fin_x"], 1)
                nc.vector.tensor_tensor(bs[0:G, 0, 0, :], h2[0:G, 0, :], x2[0:G, 0, 0, :], ALU.add)
                nc.vector.tensor_tensor_reduce(wj[0:G, 0, :], x2[0:G, 0, 0, :], wrr[0:G, :], 1.0, 0.0, ALU.mult,
                                               ALU.add, ws0[0:G, 0:1]).then_inc(S["fin_x"], 1)
                dve.wait_ge(S["fin_x"], 2)
                nc.vector.tensor_scalar(wsv[0:G, 0, 0:1], ws0[0:G, 0:1], brr[0:G, 0:1], None, ALU.add)\
                    .then_inc(S["fin_d"], 1)


def select_program(nc, A, ctx):
    wd = A["wd"]

    def sb(name, shape, dt=F32):
        return ctx.enter_context(nc.sbuf_tensor(name, shape, dt))

    ids = sb("ids", [128, SLOTS], I32)
    with ExitStack() as tmp:
        def tb(name, shape, dt=F32):
            return tmp.enter_context(nc.sbuf_tensor(name, shape, dt))

        wt = tb("wt", [128, SEG]); same = tb("same", [128, 128]); before = tb("before", [128, 128])
        allb = tb("allb", [128, 128]); iot = tb("iot", [128, SLOTS]); iotb = tb("iotb", [128, SLOTS], FP16)
        idhi = tb("idhi", [128, SEG]); idlo = tb("idlo", [128, SEG])
        bit = tb("bit", [128, 2], I32); u = tb("u", [128, 1], I32); cand = tb("cand", [128, 1], I32)
        msk = tb("msk", [128, 1], I32); thr = tb("thr", [128, 1], I32); okm = tb("okm", [128, 1], I32)
        cnt = tb("cnt", [128, 1]); junk = tb("junk", [128, SEG]); ones = tb("ones", [128, SEG]); zer = tb("zer", [128, SEG])
        gt = tb("gt", [128, SEG]); eq = tb("eq", [128, SEG]); esc = tb("esc", [128, SEG]); seleq = tb("seleq", [128, SEG])
        sel = tb("sel", [128, SEG]); psc = tb("psc", [128, SEG]); pos = tb("pos", [128, SEG]); poi = tb("poi", [128, SEG], I32)
        pdi = tb("pdi", [128, SEG], I32); pmi = tb("pmi", [128, SEG], I32); pdf = tb("pdf", [128, SEG]); pmf = tb("pmf", [128, SEG])
        room = tb("room", [128, 1]); room1 = tb("room1", [128, 1])
        UN = 4
        onL = tb("onL", [128, UN, 128], FP16); onR = tb("onR", [128, UN, 2, SLOTS], FP16)
        lstf = tb("lstf", [128, SLOTS])
        P_C = tmp.enter_context(nc.psum_tensor("p_cnt", [128, 512], F32))
        P_L = tmp.enter_context(nc.psum_tensor("p_list", [128, 512], F32))
        S = {n: tmp.enter_context(nc.semaphore("sel_" + n)) for n in "ld c cn cp n r rd pr prd l0 l mm lst".split()}
        loads = [(wt, wd.rearrange("b (s f) -> (b s) f", s=8)), (same, A["same"]), (before, A["before"]), (allb, A["allb"]),
                 (iot, A["iota"]), (idhi, A["idhi"]), (idlo, A["idlo"]), (bit[:, 0:1], A["bit"])]
        thf = thr[:].bitcast(F32)
        with nc.Block() as block:
            @block.sync
            def _(sp):
                for dst, src in loads:
                    sp.dma_start(dst if dst is loads[-1][0] else dst[:], src).then_inc(S["ld"], 16)
                sp.wait_ge(S["ld"], 16 * len(loads))

            @block.vector
            def _(dve):
                dve.wait_ge(S["ld"], 16 * len(loads))
                PER = 7

                def lnk(ins, v):
                    link(dve, ins, S["c"], v)

                def threshold(key, v):
                    lnk(nc.vector.tensor_scalar(msk[:], key[:], 31, -1, ALU.arith_shift_right, ALU.bitwise_xor), v + 1)
                    lnk(nc.vector.scalar_tensor_tensor(out=thr[:], in0=msk[:], scalar=-2147483648, in1=key[:],
                                                       op0=ALU.bitwise_or, op1=ALU.bitwise_xor), v + 2)

                nc.vector.memset(u[:], 0)
                nc.vector.memset(ones[:], 1.0)
                nc.vector.memset(zer[:], 0.0)
                lnk(nc.vector.tensor_copy(iotb[:], iot[:]), 1)
                with dve.Fori(0, 32) as r:
                    v = r * PER + 1
                    lnk(nc.vector.tensor_tensor(cand[:], u[:], bit[:, 0:1], ALU.bitwise_or), v + 1)
                    threshold(cand, v + 1)
                    nc.vector.scalar_tensor_tensor(out=junk[:], in0=wt[:], scalar=thf[:, 0:1], in1=ones[:], op0=ALU.is_ge,
                                                   op1=ALU.mult, accum_out=cnt[:]).then_inc(S["cn"], 1)
                    dve.wait_ge(S["cp"], r + 1)
                    lnk(nc.vector.tensor_scalar(okm[:], P_C[:, 0:1], float(KK), -1.0, ALU.is_ge, ALU.mult), v + 4)
                    lnk(nc.vector.scalar_tensor_tensor(out=u[:], in0=okm[:], scalar=bit[:, 0:1], in1=u[:],
                                                       op0=ALU.bitwise_and, op1=ALU.bitwise_or), v + 5)
                    lnk(nc.vector.tensor_scalar(bit[:, 1:2], bit[:, 0:1], 1, None, ALU.logical_shift_right), v + 6)
                    lnk(nc.vector.tensor_copy(bit[:, 0:1], bit[:, 1:2]), v + 7)
                v = 32 * PER + 1
                threshold(u, v)
                nc.vector.scalar_tensor_tensor(out=gt[:], in0=wt[:], scalar=thf[:, 0:1], in1=ones[:], op0=ALU.is_gt,
                                               op1=ALU.mult, accum_out=cnt[:]).then_inc(S["cn"], 1)
                lnk(nc.vector.tensor_scalar(eq[:], wt[:], thf[:, 0:1], None, ALU.is_equal), v + 3)
                nc.vector.tensor_tensor_scan(esc[:], eq[:], zer[:], 0.0, ALU.add, ALU.add).then_inc(S["cn"], 1)
                dve.wait_ge(S["cp"], 34)
                lnk(nc.vector.tensor_scalar(room[:], P_C[:, 0:1], -1.0, float(KK), ALU.mult, ALU.add), v + 4)
                lnk(nc.vector.tensor_tensor(room1[:], room[:], P_C[:, 1:2], ALU.subtract), v + 5)
                lnk(nc.vector.scalar_tensor_tensor(out=seleq[:], in0=esc[:], scalar=room1[:, 0:1], in1=eq[:],
                                                   op0=ALU.is_le, op1=ALU.mult), v + 6)
                lnk(nc.vector.tensor_tensor(sel[:], gt[:], seleq[:], ALU.add), v + 7)
                nc.vector.tensor_tensor_scan(psc[:], sel[:], zer[:], 0.0, ALU.add, ALU.add).then_inc(S["cn"], 1)
                dve.wait_ge(S["cp"], 35)
                lnk(nc.vector.tensor_copy(room[:], P_C[:, 2:3]), v + 8)
                lnk(nc.vector.scalar_tensor_tensor(out=pos[:], in0=psc[:], scalar=room[:, 0:1], in1=sel[:],
                                                   op0=ALU.add, op1=ALU.mult), v + 9)
                lnk(nc.vector.tensor_scalar(poi[:], pos[:], -1.0, None, ALU.add), v + 10)
                nc.vector.tensor_scalar(pdi[:], poi[:], 7, None, ALU.arith_shift_right)
                lnk(nc.vector.tensor_scalar(pmi[:], poi[:], 127, None, ALU.bitwise_and), v + 11)
                nc.vector.tensor_copy(pdf[:], pdi[:])
                lnk(nc.vector.tensor_copy(pmf[:], pmi[:]), v + 12)
                with dve.Fori(0, SEG - UN + 1, UN) as f:
                    for q in range(UN):
                        dve.wait_ge(S["mm"], f + q + 1)
                        nc.vector.tensor_scalar(onL[:, q, :], iotb[:, 0:128], pmf[:, ds(f + q, 1)], None, ALU.is_equal)
                        for n, part in enumerate((idhi, idlo)):
                            ins = nc.vector.tensor_scalar(onR[:, q, n, :], iotb[:], pdf[:, ds(f + q, 1)],
                                                          part[:, ds(f + q, 1)], ALU.is_equal, ALU.mult)
                        ins.then_inc(S["l"], 1)
                dve.wait_ge(S["mm"], SEG + UN)
                lnk(nc.vector.tensor_scalar(lstf[:], P_L[:, 0:SLOTS], 256.0, None, ALU.mult), v + 13)
                lnk(nc.vector.tensor_tensor(ids[:], lstf[:], P_L[:, SLOTS:2 * SLOTS], ALU.add), v + 14)

            @block.tensor
            def _(pe):
                pe.wait_ge(S["ld"], 16 * len(loads))
                pe.sem_inc(S["mm"], UN)
                with pe.Fori(0, 32) as r:
                    pe.wait_ge(S["cn"], r + 1)
                    nc.tensor.matmul(P_C[:, 0:1], same[:], cnt[:], start=True, stop=True).then_inc(S["cp"], 1)
                pe.wait_ge(S["cn"], 33)
                nc.tensor.matmul(P_C[:, 0:1], same[:], cnt[:], start=True, stop=True).then_inc(S["cp"], 1)
                pe.wait_ge(S["cn"], 34)
                nc.tensor.matmul(P_C[:, 1:2], before[:], esc[:, SEG - 1:SEG], start=True, stop=True).then_inc(S["cp"], 1)
                pe.wait_ge(S["cn"], 35)
                nc.tensor.matmul(P_C[:, 2:3], allb[:], psc[:, SEG - 1:SEG], start=True, stop=True).then_inc(S["cp"], 1)

                def add(q, v, start, stop):
                    pe.wait_ge(S["l"], v)
                    return nc.tensor.matmul(P_L[:, 0:2 * SLOTS], onL[:, q, :], onR[:, q].rearrange("p n a -> p (n a)"),
                                            start=start, stop=stop).then_inc(S["mm"], 1)
                add(0, 1, True, False)
                for q in range(1, UN):
                    add(q, q + 1, False, False)
                with pe.Fori(UN, SEG - 2 * UN + 1, UN) as f:
                    for q in range(UN):
                        add(q, f + q + 1, False, False)
                for q in range(UN):
                    add(q, SEG - UN + q + 1, False, q == UN - 1)
    return ids


def feed_forward_program(nc, A, ids):
    with ExitStack() as ctx:
        def sb(name, shape, dt=F32):
            return ctx.enter_context(nc.sbuf_tensor(name, shape, dt))

        w1 = sb("w1", [128, KC, FF]); b1 = sb("b1", [128, NHB]); w2 = sb("w2", [128, NHB, C])
        b2 = sb("b2", [128, C]); wr = sb("wr", [128, C]); br = sb("br", [128, 1]); idn = sb("idn", [128, 128])
        ix = sb("ix", [128, 4, 2], I32); pdot = sb("pdot3", [1, 16])
        xg = sb("xg", [128, 2, 2, C]); xgT = sb("xgT", [128, 2, KC, 256])
        wsj = sb("wsj", [128, 2, C]); wg = sb("wg", [128, 2]); wgb = sb("wgb", [128, 2, 2])
        hT = sb("hT", [128, 2, NHB, 256]); yb = sb("yb", [128, 2, 2, C]); ym = sb("ym", [128, 2, 2, C])
        P_X = ctx.enter_context(nc.psum_tensor("p_x", [128, 512], F32))
        P_H = [ctx.enter_context(nc.psum_tensor(f"p_h{n}", [128, 512], F32)) for n in range(4)]
        P_Y = [ctx.enter_context(nc.psum_tensor(f"p_y{n}", [128, 512], F32)) for n in range(2)]
        S = {n: ctx.enter_context(nc.semaphore("ff_" + n)) for n in
             "dot ld ix g0 g1 xt xc h0 h1 h2 h3 e y ya ym wc w s0 s1".split()}
        g, st = (S["g0"], S["g1"]), (S["s0"], S["s1"])
        loads = [(w1, "fw1"), (b1, "fb1"), (w2, "fw2"), (b2, "fb2"), (wr, "wrr"), (br, "brr"), (idn, "ident")]
        LAST = NSEL - (NPAIR * 256 - 128)
        out_rows, x2_rows = A["out_rows"], A["x2d"].rearrange("b n c -> (b n) c")

        def pairs(eng, body):
            for p in range(2):
                body(p, p, False)
            with eng.Fori(2, NPAIR - 3, 2) as p:
                body(p, 0, False)
                body(p + 1, 1, False)
            body(NPAIR - 2, 0, False)
            body(NPAIR - 1, 1, True)

        with nc.Block() as block:
            @block.sync
            def _(sp):
                for dst, name in loads:
                    sp.dma_start(dst[:], A[name]).then_inc(S["ld"], 16)
                sp.wait_ge(S["ld"], 16 * len(loads))

            @block.gpsimd
            def _(pool):
                def index(p, q):
                    pool_waits(nc, pdot, 4)
                    nc.gpsimd.tensor_copy(ix[:, q, :], ids[:, ds(p * 2, 2)]).then_inc(S["ix"], 1)

                def rows(last, t):
                    return LAST if last and t == 1 else 128

                def gather(p, e, q, last):
                    pool.wait_ge(S["ix"], p + 1)
                    pool.wait_ge(S["xt"], p + 1)
                    pool.wait_ge(S["w"], p + 1)
                    pool_waits(nc, pdot, 5)
                    for t in range(2):
                        r = rows(last, t)
                        nc.gpsimd.indirect_dma_start(
                            out=xg[0:r, e, t, :], out_offset=None, in_=x2_rows,
                            in_offset=bass.IndirectOffsetOnAxis(ap=ix[0:r, q, t:t + 1], axis=0)).then_inc(g[e], 16)

                def scatter(p, e, q, last):
                    pool.wait_ge(S["ym"], p + 1)
                    pool_waits(nc, pdot, 6 + q)
                    for t in range(2):
                        r = rows(last, t)
                        nc.gpsimd.indirect_dma_start(
                            out=out_rows, out_offset=bass.IndirectOffsetOnAxis(ap=ix[0:r, q, t:t + 1], axis=0),
                            in_=ym[0:r, e, t, :], in_offset=None, compute_op=ALU.add).then_inc(st[e], 16)

                nc.gpsimd.memset(pdot[:], 0.0).then_inc(S["dot"], 1)
                pool.wait_ge(S["dot"], 1)
                for p in range(2):
                    index(p, p)
                    gather(p, p, p, False)
                with pool.Fori(2, NPAIR - 7, 4) as p:
                    for k in range(4):
                        e, q = k % 2, (2 + k) % 4
                        pool.wait_ge(st[e], (p + k - e) * 16 - 32)
                        index(p + k, q)
                        gather(p + k, e, q, False)
                        scatter(p + k - 2, e, k % 4, False)
                for p in range(NPAIR - 4, NPAIR):
                    e, q = p % 2, (p % 4)
                    pool.wait_ge(st[e], (p - e) * 16 - 32)
                    index(p, q)
                    gather(p, e, q, p == NPAIR - 1)
                    scatter(p - 2, e, (q + 2) % 4, False)
                for p in (NPAIR - 2, NPAIR - 1):
                    scatter(p, p % 2, p % 4, p == NPAIR - 1)
                for e in range(2):
                    pool.wait_ge(st[e], 32 * (NPAIR // 2))

            @block.tensor
            def _(pe):
                def turn(p, e):
                    pe.wait_ge(g[e], (p - e) * 16 + 32)
                    pe.wait_ge(S["xc"], p + 2)
                    for t in range(2):
                        for k in range(KC):
                            ins = nc.tensor.transpose(P_X[:, k * 256 + t * 128:k * 256 + (t + 1) * 128],
                                                      xg[:, e, t, k * 128:(k + 1) * 128], idn[:])
                    ins.then_inc(S["xt"], 1)

                def up(p, e):
                    pe.wait_ge(S["xc"], p + 3)
                    for n in range(4):
                        pe.wait_ge(S["e"], (p + 1) * 4 + n + 1)
                        for m in range(2):
                            for k in range(KC):
                                hb = 2 * n + m
                                ins = nc.tensor.matmul(P_H[n][:, m * 256:(m + 1) * 256], w1[:, k, hb * 128:(hb + 1) * 128],
                                                       xgT[:, e, k, :], start=(k == 0), stop=(k == KC - 1))
                        ins.then_inc(S[f"h{n}"], 1)

                def down(p, e):
                    pe.wait_ge(S["ya"], p + 1)
                    pe.wait_ge(S["e"], (p + 2) * 4 + 4)
                    for t in range(2):
                        for hb in range(NHB):
                            ins = nc.tensor.matmul(P_Y[e][:, t * C:(t + 1) * C], hT[:, e, hb, t * 128:(t + 1) * 128],
                                                   w2[:, hb, :], start=(hb == 0), stop=(hb == NHB - 1))
                    ins.then_inc(S["y"], 1)

                pe.wait_ge(S["ld"], 16 * len(loads))
                pe.sem_inc(S["xt"], 2)
                pe.sem_inc(S["y"], 2)
                turn(0, 0)
                up(0, 0)
                turn(1, 1)
                up(1, 1)
                turn(2, 0)
                down(0, 0)
                with pe.Fori(2, NPAIR - 3, 2) as p:
                    for e in range(2):
                        up(p + e, e)
                        turn(p + e + 1, 1 - e)
                        down(p + e - 1, 1 - e)
                up(NPAIR - 2, 0)
                turn(NPAIR - 1, 1)
                down(NPAIR - 3, 1)
                up(NPAIR - 1, 1)
                down(NPAIR - 2, 0)
                down(NPAIR - 1, 1)

            @block.scalar
            def _(act):
                act.wait_ge(S["ld"], 16 * len(loads))
                act.sem_inc(S["e"], 8)

                def body(p, e, last):
                    act.wait_ge(S["y"], p + 1)
                    for n in range(4):
                        act.wait_ge(S[f"h{n}"], p + 1)
                        for m in range(2):
                            hb = 2 * n + m
                            ins = nc.scalar.activation(hT[:, e, hb, :], P_H[n][:, m * 256:(m + 1) * 256],
                                                       ACT.Gelu_apprx_tanh, bias=b1[:, hb:hb + 1])
                        ins.then_inc(S["e"], 1)
                pairs(act, body)

            @block.vector
            def _(dve):
                dve.wait_ge(S["ld"], 16 * len(loads))
                dve.sem_inc(S["xc"], 2)
                dve.sem_inc(S["ya"], 2)
                dve.sem_inc(S["w"], 2)
                dve.sem_inc(S["wc"], 2)

                def turned(p, e):
                    dve.wait_ge(S["xt"], p + 3)
                    dve.wait_ge(S["h3"], p - 1) if not isinstance(p, int) or p >= 2 else None
                    nc.vector.tensor_copy(xgT[:, e].rearrange("p k t -> p (k t)"), P_X[:]).then_inc(S["xc"], 1)

                def weigh(p, e):
                    dve.wait_ge(g[e], (p - e) * 16 + 32)
                    dve.wait_ge(S["wc"], p + 2)
                    for t in range(2):
                        ins = nc.vector.tensor_tensor_reduce(wsj[:, t, :], xg[:, e, t, :], wr[:], 1.0, 0.0, ALU.mult,
                                                             ALU.add, wg[:, t:t + 1])
                    ins.then_inc(S["w"], 1)
                    dve.wait_ge(S["w"], p + 3)
                    nc.vector.tensor_scalar(wgb[:, e, :], wg[:], br[:, 0:1], None, ALU.add).then_inc(S["wc"], 1)

                def second(p, e, last):
                    dve.wait_ge(S["y"], p + 3)
                    nc.vector.tensor_tensor(yb[:, e], P_Y[e][:].rearrange("p (t c) -> p t c", t=2),
                                            b2[:].rearrange("p (o c) -> p o c", o=1).broadcast_to([128, 2, C]), ALU.add)\
                        .then_inc(S["ya"], 1)
                    dve.wait_ge(S["ya"], p + 3)
                    dve.wait_ge(S["wc"], p + 3)
                    dve.wait_ge(st[e], (p - e) * 16 + 0) if not isinstance(p, int) or p >= 2 else None
                    for t in range(2):
                        ins = nc.vector.tensor_scalar(ym[:, e, t, :], yb[:, e, t, :], wgb[:, e, t:t + 1], None, ALU.mult)
                    ins.then_inc(S["ym"], 1)

                turned(0, 0)
                weigh(0, 0)
                turned(1, 1)
                weigh(1, 1)
                turned(2, 0)
                second(0, 0, False)
                weigh(2, 0)
                with dve.Fori(2, NPAIR - 3, 2) as p:
                    for e in range(2):
                        turned(p + e + 1, 1 - e)
                        second(p + e - 1, 1 - e, False)
                        weigh(p + e + 1, 1 - e)
                turned(NPAIR - 1, 1)
                second(NPAIR - 3, 1, False)
                weigh(NPAIR - 1, 1)
                second(NPAIR - 2, 0, False)
                second(NPAIR - 1, 1, True)


def lay_out(inputs):
    import numpy as np
    f = {n: np.asarray(a) for n, a in inputs.items()}
    x = np.concatenate([f["x"][:, :, WS // 2:], f["x"][:, :, :WS // 2]], axis=2)
    x = np.concatenate([x[:, :, :, WS // 2:], x[:, :, :, :WS // 2]], axis=3)
    x = x.reshape(NB, KC, 128, NWR, WS, NWR, WS).transpose(0, 3, 2, 1, 5, 4, 6).reshape(NS, 128, KC, STEP)
    xw = np.concatenate([x, x[:1]], axis=0)
    w1 = f["L0_tok_w1"].reshape(E, NH, 3, C).transpose(2, 1, 0, 3).reshape(6, 128, C)
    b1 = f["L0_tok_b1"].reshape(E, NH, 3).transpose(2, 1, 0).reshape(6, 128)
    tok = np.arange(BLK)
    win, row, col = tok // 16, tok % 16 // WS, tok % WS
    pos = f["L0_tok_pos_emb"][row[None, :] - row[:, None] + WS - 1, col[None, :] - col[:, None] + WS - 1]
    other = win[:, None] != win[None, :]
    half = WS // 2
    rows = (row[:, None] >= half) != (row[None, :] >= half)
    cols = (col[:, None] >= half) != (col[None, :] >= half)
    mask = np.zeros((2, NJ, BLK, BLK), np.float32)
    mask[:, :, other] = NEG
    mask[1, :, rows] = NEG
    edge = cols & (win[:, None] == 1) & (win[None, :] == 1)
    mask[:, NJ - 1, edge] = NEG
    mask = np.broadcast_to(mask.transpose(2, 0, 1, 3)[None], (4, BLK, 2, NJ, BLK)).reshape(128, 2, STEP)
    posr = np.broadcast_to(pos[None, :, None, :], (4, BLK, NJ, BLK)).reshape(128, STEP)
    q, k, v = np.split(f["L0_attn_w_qkv"], 3, axis=1)
    wlin = np.concatenate([q, v, k], axis=1).reshape(KC, 128, 3 * HID).transpose(1, 0, 2)

    def rep(a, n=128):
        return np.broadcast_to(a.reshape(1, -1), (n, a.size))
    part = np.arange(128)
    mk, mvv = f["L0_attn_mem_kv"]
    tokid = (part // 8 * NTOK + part % 8 * SEG)[:, None] + np.arange(SEG)[None, :]
    tokid = np.where(np.arange(SEG)[None, :] + (part % 8 * SEG)[:, None] < NTOK, tokid, 0)
    return {
        "xw": xw, "w1T": w1.transpose(2, 0, 1).reshape(KC, 128, 6, 128).transpose(1, 0, 2, 3), "b1c": b1.T,
        "w2T": f["L0_tok_w2"].T.reshape(KC, 128, C).transpose(1, 0, 2), "b2r": rep(f["L0_tok_b2"]),
        "posr": posr, "mask": mask, "ident": np.eye(128, dtype=np.float32),
        "gpre": f["L0_attn_g_pre"].reshape(KC, 128).T, "wlin": wlin, "wout": f["L0_attn_w_out"],
        "hmask": (part[:, None] // 32 == part[None, :] // 32).astype(np.float32),
        "bor": rep(f["L0_attn_b_out"]), "gor": rep(f["L0_attn_g_out"]), "wrr": rep(f["L0_ffn_wr"]),
        "brr": rep(f["L0_ffn_br"]), "clsr": rep(f["cls_tok"], TT),
        "memk": mk.reshape(HID, NMEM), "memv": mvv.reshape(HID, NMEM).T,
        "wpad": np.full((NB, 8 * SEG), -3e38, np.float32),
        "same": (part[:, None] // 8 == part[None, :] // 8).astype(np.float32),
        "before": ((part[:, None] // 8 == part[None, :] // 8) & (part[:, None] < part[None, :])).astype(np.float32),
        "allb": (part[:, None] < part[None, :]).astype(np.float32),
        "iota": rep(np.arange(SLOTS, dtype=np.float32)),
        "idhi": (tokid // 256).astype(np.float32), "idlo": (tokid % 256).astype(np.float32),
        "bit": np.full((128, 1), -2 ** 31, np.int32),
        "fw1": f["L0_ffn_w1"].reshape(KC, 128, FF).transpose(1, 0, 2), "fb1": f["L0_ffn_b1"].reshape(NHB, 128).T,
        "fw2": f["L0_ffn_w2"].reshape(NHB, 128, C).transpose(1, 0, 2), "fb2": rep(f["L0_ffn_b2"]),
    }


def kernel(**inputs):
    import numpy as np
    import concourse.bacc as bacc
    from concourse.bass_utils import run_bass_kernel_spmd

    nc = bacc.Bacc("TRN2", target_bir_lowering=False, num_devices=1)
    arrays, A = {}, {}
    for name, a in lay_out(inputs).items():
        a = np.ascontiguousarray(a)
        arrays[f"in_{name}"] = a
        A[name] = nc.dram_tensor(f"in_{name}", a.shape, mybir.dt.from_np(a.dtype), kind="ExternalInput").ap()
    A["out"] = nc.dram_tensor("out_h", (NB, NTOK, C), F32, kind="ExternalOutput").ap()
    A["out_rows"] = A["out"].rearrange("b n c -> (b n) c")
    A["x2d"] = nc.dram_tensor("x2_scratch", (NB, NTOK, C), F32).ap()
    A["wd"] = nc.dram_tensor("w_scratch", (NB, 8 * SEG), F32).ap()
    A["clsd"] = nc.dram_tensor("cls_scratch", (NB, C), F32).ap()
    attention_program(nc, A)
    with ExitStack() as ctx:
        ids = select_program(nc, A, ctx)
        feed_forward_program(nc, A, ids)
    r = run_bass_kernel_spmd(nc, [arrays], core_ids=[0])
    return r.results[0]["out_h"]
```

```python
from contextlib import ExitStack

import concourse.bass as bass
from concourse import mybir
from concourse.bass import ds

ALU = mybir.AluOpType
ACT = mybir.ActivationFunctionType
F32 = mybir.dt.float32
F32R = mybir.dt.float32r
I32 = mybir.dt.int32
AX = mybir.AxisListType.X

NB, C, HT, WD = 16, 256, 56, 56
WS, NH, E = 4, 8, 32
NWR = HT // WS
STEP = WS * WD
NTOK = HT * WD + 1
BLK = 32
NJ = STEP // BLK
TT = STEP // 2
KC = C // 128
NS = NB * NWR
HID, NMEM = 128, 4
KCOL = NTOK + NMEM
FF = 1024
NHB = FF // 128
KK = int(0.5 * NTOK) - 1
NSEL = NB * KK
NPAIR = (NSEL + 255) // 256
SLOTS = NPAIR * 2
SEG = 400
EPS = 1e-5
TINY2 = 1e-12 ** 2 / C
NEG = -1e30
ISC = float(1.0 / (E ** 0.5))
QSC = float(E ** -0.5)
OUTLAG = 3 + NWR
RING = 17
CR = 4


def link(eng, ins, sem, value):
    ins.then_inc(sem, 1)
    eng.wait_ge(sem, value)


def pool_waits(nc, dot, n):
    nc.gpsimd.tensor_tensor(dot[:, n:n + 1], dot[:, 0:1], dot[:, 0:1], ALU.add)


def upper_part(nc, high, x):
    return nc.vector.tensor_copy(high, x)


def lower_part(nc, low, x, high):
    return nc.vector.tensor_tensor(low, x, high.bitcast(F32), ALU.subtract)


def split_matmul(nc, out, stationary, moving, start, stop):
    (sh, sl), (mh, ml) = stationary, moving
    nc.tensor.matmul(out, sh, mh, start=start, stop=False)
    nc.tensor.matmul(out, sh, ml, start=False, stop=False)
    return nc.tensor.matmul(out, sl, mh, start=False, stop=stop)


def schedule(eng, body):
    stages = ("proj", "attn", "mix", "lin", "tq")
    every = set(stages)

    def ctx(i):
        return {2: {"kmax"}, 3: {"ctx"}}.get(i, set())

    for f in range(6):
        body(f, 0, f, f % 2, {n for lag, n in enumerate(stages) if f >= lag})
    with eng.Fori(6, NWR - 1, 2) as i:
        body(i, 0, i, 0, every)
        body(i + 1, 0, i + 1, 1, every)
    for i in range(6):
        body(NWR + i, 1, i, i % 2, every | {n for n, k in (("out", 3), ("fin", 4)) if i >= k} | ctx(i))
    every = every | {"out", "fin"}
    with eng.Fori(6, NWR - 1, 2) as i:
        body(i + NWR, 1, i, 0, every)
        body(i + (NWR + 1), 1, i + 1, 1, every)
    for i in range(6):
        body(2 * NWR + i, 2, i, i % 2, every | ctx(i))
    with eng.Fori(2, NB - 1) as b:
        base = eng.snap(b * NWR)
        with eng.Fori(6, NWR - 1, 2) as i:
            F = eng.snap(base + i)
            body(F, b, i, 0, every)
            body(F + 1, b, i + 1, 1, every)
        for i in range(6):
            body(base + NWR + i, b + 1, i, i % 2, every | ctx(i))
    with eng.Fori(6, NWR - 1, 2) as i:
        body(i + (NS - NWR), NB - 1, i, 0, every)
        body(i + (NS - NWR + 1), NB - 1, i + 1, 1, every)
    for i in range(6):
        body(NS + i, NB, i, i % 2, {n for lag, n in enumerate(stages) if i < lag} | {"out", "fin"} | ctx(i))
    with eng.Fori(6, NWR + 1, 2) as i:
        body(i + NS, NB, i, 0, {"out", "fin"})
        body(i + (NS + 1), NB, i + 1, 1, {"out", "fin"})
    body(NS + OUTLAG - 1, NB, OUTLAG - 1, 0, {"out", "fin"})
    body(NS + OUTLAG, NB, OUTLAG, 1, {"fin"})


def ring(F, lag, size):
    return ((F - lag) % RING) * size


def attention_program(nc, A):
    out, x2d, wd, clsd = A["out"], A["x2d"], A["wd"], A["clsd"]
    with ExitStack() as ctx:
        def sb(name, shape, dt=F32):
            return ctx.enter_context(nc.sbuf_tensor(name, shape, dt))

        bank = [ctx.enter_context(nc.psum_tensor(f"bank{n}", [128, 512], F32)) for n in range(8)]
        P_QV, P_K, P_SC, P_PV, P_W2, P_T, P_LIN, P_LK = bank

        w1T = sb("w1T", [128, KC, 6, 128]); b1c = sb("b1c", [128, 6])
        w2T = sb("w2T", [128, KC, C]); b2r = sb("b2r", [128, C])
        tbl = sb("tbl", [128, 2, STEP]); posr = sb("posr", [128, STEP])
        ident = sb("ident", [128, 128])
        gpre = sb("gpre", [128, KC]); wlin = sb("wlin", [128, KC, 3 * HID])
        wout = sb("wout", [128, C]); hmask = sb("hmask", [128, 128])
        bor = sb("bor", [128, C]); gor = sb("gor", [128, C]); wrr = sb("wrr", [128, C]); brr = sb("brr", [128, 1])
        bvr = sb("bvr", [128, 2, TT])
        xw = sb("xw", [128, 2, KC, STEP])
        klin = sb("klin", [128, 2, 2, STEP])
        qblk = sb("qblk", [128, 2, 2 * NJ, 4, BLK]); vblk = sb("vblk", [128, 2, 2 * NJ, 4, BLK])
        sc = sb("sc", [128, 2 * NJ, BLK]); scs = sb("scs", [128, 2 * NJ, BLK])
        pr = sb("pr", [128, 2 * NJ, BLK]); prn = sb("prn", [128, 2 * NJ, BLK])
        smx = sb("smx", [128, 2 * NJ]); ssm = sb("ssm", [128, 2 * NJ]); srec = sb("srec", [128, 2 * NJ])
        pT = sb("pT", [128, 2, 2 * NJ, BLK])
        oT = sb("oT", [128, 2, STEP])
        hh = sb("hh", [TT, 2, 2, C]); bst = sb("bst", [TT, 2, 6]); mv = sb("mv", [TT, 2, 2])
        rcv = sb("rcv", [TT, 2]); pwi = sb("pwi", [TT, 4]); pwo = sb("pwo", [TT, 4])
        mhalf = sb("mhalf", [TT, 4])
        gsc = sb("gsc", [TT, 2]); asc = sb("asc", [TT, 2, 2]); nmr = sb("nmr", [TT, 2, 2])
        xn = sb("xn", [TT, 2, C]); xnT = sb("xnT", [128, KC, STEP])
        s1 = sb("s1", [TT, RING * 2 * C]); qTs = sb("qTs", [128, RING * STEP])
        qraw = sb("qraw", [TT, 8, 32]); qmx = sb("qmx", [TT, 8]); qsh = sb("qsh", [TT, 8, 32])
        qex = sb("qex", [TT, 8, 32]); qsm = sb("qsm", [TT, 8]); qrc = sb("qrc", [TT, 8]); qs = sb("qs", [TT, 8, 32])
        kT = sb("kT", [128, KCOL]); kcst = sb("kcst", [128, 1 + NMEM])
        vst = sb("vst", [TT, 2 * NWR + 1, HID]); kN = sb("kN", [TT, 2, 4 * 128])
        kmx = sb("kmx", [128, 2]); nkmx = sb("nkmx", [128, 1]); ksum = sb("ksum", [128, 1]); krc = sb("krc", [128, 1])
        ctxT = sb("ctxT", [128, 128]); Mw = sb("Mw", [128, C]); Mq = sb("Mq", [128, C]); boq = sb("boq", [128, C])
        qch = sb("qch", [128, 2, STEP], F32R); qcl = sb("qcl", [128, 2, STEP], F32R)
        w2h = sb("tw2h", [128, KC, C], F32R); w2l = sb("tw2l", [128, KC, C], F32R)
        wlh = sb("wlh", [128, KC, 256], F32R); wll = sb("wll", [128, KC, 256], F32R)
        xnh = sb("xnh", [128, KC, STEP], F32R); xnl = sb("xnl", [128, KC, STEP], F32R)
        oh = sb("oh", [128, 2, STEP], F32R); ol = sb("ol", [128, 2, STEP], F32R)
        Mh = sb("Mh", [128, C], F32R); Ml = sb("Ml", [128, C], F32R)
        ob = sb("ob", [TT, 2, C]); osq = sb("osq", [TT, 2, C]); oss = sb("oss", [TT, 2])
        onr = sb("onr", [TT, 2]); ors = sb("ors", [TT, 2]); v2 = sb("v2", [TT, 2]); ou = sb("ou", [TT, 2, C])
        h2 = sb("h2", [TT, 2, C]); bst2 = sb("bst2", [TT, 2, 6]); mv2 = sb("mv2", [TT, 2, 2]); r2 = sb("r2", [TT, 2])
        x2 = sb("x2", [TT, 2, 2, C]); bs = sb("bs", [TT, 2, 2, C]); wj = sb("wj", [TT, 2, C])
        ws0 = sb("ws0", [TT, 2]); wsv = sb("wsv", [TT, 2, 2])
        clsq = sb("clsq", [128, 1]); clso = sb("clso", [1, 2, C]); pdot = sb("pdot", [1, 8]); vdot = sb("vdot", [1, 4])
        clss = sb("clss", [TT, C]); clsr = sb("clsr", [TT, C])

        S = {}
        steps = dict(tensor="q_ps k_ps v_ps sc_ps pv_ps w2_ps tx_ps lin_ps lk_ps tq_ps o2_ps".split(),
                     scalar="qb k_lin sm_e o_t xnt q_cp v_cp k_cp qm_e q_t o2_q s1_d".split(),
                     vector="vb sm_a sm_s sm_p sm_t h_a ln_v v2_d ln_s xn_d qm_s qm_d u_d x2_d w_dn".split(),
                     gpsimd="ln_p or_p r2_p qc_h qc_d xl_d ol_d h2_d bs_d".split())
        for n in sum(steps.values(), []) + ("or_c x_ld0 x_ld1 w_ld ini sm_c ln_c qm_c o2_c st_d0 st_d1 ctx_m ctx_e ctx_t "
                                            "ctx_n ctx_ps ctx_c ctx_x ctx_mp ctx_mw cls_ps cls_c cls_st kc_d "
                                            "bv_d bv_p set_d set_p set_a set_g tbl_d fin_x fin_p fin_ld fin_d fin_a fin_st").split():
            S[n] = ctx.enter_context(nc.semaphore(n))

        def at(eng, name, s):
            eng.wait_ge(S[name], s + (1 + CR))

        x_ld, st_d = (S["x_ld0"], S["x_ld1"]), (S["st_d0"], S["st_d1"])

        def stored(eng, e, s):
            eng.wait_ge(st_d[e], (s - e) * 24 + 48)

        def credit(eng, who):
            for n in steps[who]:
                eng.sem_inc(S[n], CR)

        loads = [(w1T, "w1T"), (b1c, "b1c"), (w2T, "w2T"), (b2r, "b2r"), (posr, "posr"), (tbl, "mask"),
                 (ident, "ident"), (gpre, "gpre"), (wlin, "wlin"), (wout, "wout"), (hmask, "hmask"),
                 (bor, "bor"), (gor, "gor"), (wrr, "wrr"), (brr, "brr"), (clsr, "clsr")]
        W_ALL = 16 * (len(loads) + 3)

        def layer_norm_1(h, par, lnk, done, powered, free):
            for t in range(2):
                ins = nc.vector.bn_stats(bst[:, t, :], h[:, t, :])
            lnk(ins, 1)
            nc.vector.tensor_copy(vdot[:, 1:2], vdot[:, 0:1])
            for t in range(2):
                ins = nc.vector.bn_aggr(mv[:, t, :], bst[:, t, :])
            lnk(ins, 2)
            mean, var = mv[:, :, 0], mv[:, :, 1]
            lnk(nc.vector.tensor_scalar(pwi[:, 0:2], var, EPS, None, ALU.add), 3)
            lnk(nc.vector.reciprocal(rcv[:], pwi[:, 0:2]), 4)
            nc.vector.scalar_tensor_tensor(out=pwi[:, 2:4], in0=var, scalar=TINY2 * EPS, in1=rcv[:],
                                           op0=ALU.max, op1=ALU.mult).then_inc(*done("ln_v"))
            powered()
            nc.vector.tensor_scalar(asc[:, par, :], pwo[:, 0:2], 1.0, None, ALU.add)
            nc.vector.scalar_tensor_tensor(out=nmr[:, par, :], in0=mean, scalar=-1.0, in1=pwo[:, 0:2],
                                           op0=ALU.mult, op1=ALU.mult).then_inc(*done("ln_s"))
            lnk(nc.vector.tensor_tensor(gsc[:], pwo[:, 0:2], pwo[:, 2:4], ALU.mult), 5)
            free()
            for t in range(2):
                ins = nc.vector.tensor_scalar(xn[:, t, :], h[:, t, :], mv[:, t, 0:1], gsc[:, t:t + 1],
                                              ALU.subtract, ALU.mult)
            ins.then_inc(*done("xn_d"))

        def group(ap):
            return ap[:].rearrange("p (g o) -> p g o", o=1).broadcast_to([ap.shape[0], ap.shape[1], 32])

        def transpose_xn(pe):
            for t in range(2):
                for k in range(KC):
                    ins = nc.tensor.transpose(P_T[:, k * STEP + t * TT:k * STEP + (t + 1) * TT],
                                              xn[:, t, k * 128:(k + 1) * 128], ident[0:TT, 0:TT])
            return ins

        def lin_qv(pe):
            for t in range(2):
                for k in range(KC):
                    ins = split_matmul(nc, P_LIN[0:TT, t * 256:(t + 1) * 256],
                                       [x[:, k, t * TT:(t + 1) * TT] for x in (xnh, xnl)],
                                       [w[:, k, :] for w in (wlh, wll)], k == 0, k == KC - 1)
            return ins

        def lin_k(pe):
            for k in range(KC):
                ins = nc.tensor.matmul(P_LK[:, 0:STEP], wlin[:, k, 256:384], xnT[:, k, :],
                                       start=(k == 0), stop=(k == KC - 1))
            return ins

        def transpose_q(pe):
            for t in range(2):
                ins = nc.tensor.transpose(P_T[:, t * TT:(t + 1) * TT],
                                          qs[:, 4 * t:4 * t + 4, :].rearrange("p g d -> p (g d)"), ident[0:TT, 0:TT])
            return ins

        p_lin3 = P_LIN[0:TT, :].rearrange("p (t n) -> p t n", t=2)

        with nc.Block() as block:
            @block.sync
            def _(sp):
                for dst, name in loads:
                    sp.dma_start(dst[:], A[name]).then_inc(S["w_ld"], 16)
                sp.dma_start(kcst[:, 1:1 + NMEM], A["memk"]).then_inc(S["w_ld"], 16)
                sp.dma_start(vst[1:1 + NMEM, 2 * NWR, :], A["memv"]).then_inc(S["w_ld"], 16)
                sp.dma_start(wd, A["wpad"]).then_inc(S["w_ld"], 16)
                sp.wait_ge(S["w_ld"], W_ALL)

            @block.vector
            def _(dve):
                dve.wait_ge(S["w_ld"], W_ALL)
                n = [0]

                def lnk(ins, k=None):
                    n[0] += 1
                    link(dve, ins, S["set_d"], n[0])

                lnk(nc.vector.memset(vdot[:], 0.0))
                for m in range(2):
                    ins = nc.vector.tensor_copy(bvr[:, m, :], b1c[:, 4 + m:5 + m].broadcast_to([128, TT]))
                ins.then_inc(S["bv_d"], 1)
                dve.wait_ge(S["bv_p"], 1)
                lnk(nc.vector.tensor_tensor(b2r[0:TT], b2r[0:TT], P_W2[0:TT, 0:C], ALU.add))
                for v in range(2):
                    nc.vector.tensor_tensor(tbl[:, v, :], tbl[:, v, :], posr[:], ALU.add).then_inc(S["tbl_d"], 1)
                lnk(nc.vector.tensor_scalar(boq[:], bor[:], 1.0 / (HID // 32), None, ALU.mult))
                for k in range(KC):
                    lnk(nc.vector.tensor_scalar(wlin[:, k, :], wlin[:, k, :], gpre[:, k:k + 1], None, ALU.mult))
                lnk(upper_part(nc, wlh[:], wlin[:, :, 0:256]))
                lnk(lower_part(nc, wll[:], wlin[:, :, 0:256], wlh[:]))
                lnk(upper_part(nc, w2h[:], w2T[:]))
                lnk(lower_part(nc, w2l[:], w2T[:], w2h[:]))
                for t in range(2):
                    lnk(nc.vector.tensor_copy(hh[:, 0, t, :], clsr[:]))
                layer_norm_1(hh[:, 0], 0, lnk, lambda name: (S["ini"], 1), lambda: dve.wait_ge(S["set_g"], 5),
                             lambda: None)
                dve.wait_ge(S["ini"], 3)
                lnk(nc.vector.tensor_scalar(clss[:], clsr[:], asc[:, 0, 0:1], nmr[:, 0, 0:1], ALU.mult, ALU.add))
                dve.wait_ge(S["set_p"], 1)
                lnk(nc.vector.tensor_copy(xnT[:].rearrange("p k t -> p (k t)"), P_T[:, 0:KC * STEP]))
                lnk(upper_part(nc, xnh[:], xnT[:]))
                lower_part(nc, xnl[:], xnT[:], xnh[:]).then_inc(S["ini"], 1)
                dve.wait_ge(S["set_p"], 2)
                nc.vector.tensor_copy(vst[0:1, 2 * NWR, :], P_LIN[0:1, 128:256])
                nc.vector.tensor_copy(kcst[:, 0:1], P_LK[:, 0:1])
                lnk(nc.vector.tensor_copy(qraw[:].rearrange("p (t g) d -> p t (g d)", t=2), p_lin3[:, :, 0:128]))
                nc.vector.tensor_copy(kT[:, NTOK - 1:KCOL], kcst[:])
                lnk(nc.vector.tensor_reduce(qmx[:], qraw[:], AX, ALU.max))
                nc.vector.tensor_tensor(qsh[:], qraw[:], group(qmx), ALU.subtract).then_inc(S["ini"], 1)
                dve.wait_ge(S["set_a"], 1)
                lnk(nc.vector.tensor_reduce(qsm[:], qex[:], AX, ALU.add))
                lnk(nc.vector.reciprocal(qrc[:], qsm[:]))
                nc.vector.tensor_tensor(qs[:], qex[:], group(qrc), ALU.mult).then_inc(S["ini"], 1)
                dve.wait_ge(S["set_p"], 3)
                lnk(nc.vector.tensor_copy(clsq[:], P_T[:, 0:1]))
                credit(dve, "vector")

            @block.scalar
            def _(act):
                act.wait_ge(S["ini"], 5)
                nc.scalar.activation(qex[:], qsh[:], ACT.Exp).then_inc(S["set_a"], 1)
                credit(act, "scalar")

            @block.tensor
            def _(pe):
                pe.wait_ge(S["w_ld"], W_ALL)
                pe.wait_ge(S["bv_d"], 1)
                for m in range(2):
                    ins = nc.tensor.matmul(P_W2[0:TT, 0:C], bvr[:, m, :], w2T[:, m, :], start=(m == 0), stop=(m == 1))
                ins.then_inc(S["bv_p"], 1)
                pe.wait_ge(S["ini"], 3)
                transpose_xn(pe).then_inc(S["set_p"], 1)
                pe.wait_ge(S["ini"], 4)
                lin_qv(pe)
                lin_k(pe).then_inc(S["set_p"], 1)
                pe.wait_ge(S["ini"], 6)
                transpose_q(pe).then_inc(S["set_p"], 1)
                credit(pe, "tensor")
                pe.sem_inc(S["ctx_ps"], 2)

            @block.gpsimd
            def _(pool):
                nc.gpsimd.memset(qblk[:], 0.0).then_inc(S["set_g"], 1)
                nc.gpsimd.memset(vblk[:], 0.0).then_inc(S["set_g"], 1)
                nc.gpsimd.memset(pdot[:], 0.0).then_inc(S["set_g"], 1)
                nc.gpsimd.memset(mhalf[:], -0.5).then_inc(S["set_g"], 1)
                pool.wait_ge(S["set_g"], 4)
                pool.wait_ge(S["ini"], 1)
                nc.gpsimd.tensor_tensor(pwo[:], pwi[:], mhalf[:], ALU.pow).then_inc(S["set_g"], 1)
                credit(pool, "gpsimd")

        with nc.Block() as block:
            @block.sync
            def _(sp):
                for e in range(2):
                    sp.sem_inc(st_d[e], 48)
                sp.dma_start(xw[:, 0], A["xw"][0]).then_inc(x_ld[0], 16)
                o3, x3, w1d = A["out_rows"], x2d.rearrange("b n c -> (b n) c"), wd.rearrange("b n -> (b n)")

                def body(F, b, i, e, on):
                    if "fin" in on:
                        s = F - OUTLAG - 1
                        bo = b - 1 if not isinstance(i, int) or i > OUTLAG - NWR else b - 2
                        r0 = s * STEP + bo + 1
                        w0 = s * STEP + bo * (8 * SEG - NWR * STEP) + 1
                    if "proj" in on:
                        at(sp, "v_ps", F - 1)
                        sp.dma_start(xw[:, 1 - e:2 - e], A["xw"][ds(F + 1, 1)].rearrange("s p k t -> p s k t"))\
                            .then_inc(x_ld[1 - e], 16)
                    if "ctx" in on:
                        sp.wait_ge(S["cls_c"], b)
                        sp.dma_start(clsd[ds(b - 1, 1), :], clso[0:1, 0, :]).then_inc(S["cls_st"], 16)
                    if "fin" in on:
                        at(sp, "bs_d", s)
                        sp.dma_start(o3[ds(r0, STEP), :].rearrange("(t p) c -> p t c", p=TT), bs[:, e])\
                            .then_inc(st_d[e], 16)
                        at(sp, "w_dn", s)
                        sp.dma_start(x3[ds(r0, STEP), :].rearrange("(t p) c -> p t c", p=TT), x2[:, e])\
                            .then_inc(st_d[e], 16)
                        sp.dma_start(w1d[ds(w0, STEP)]
                                     .rearrange("(t p) -> p t", p=TT), wsv[:, e, :],
                                     allow_slow_non_contiguous=True).then_inc(st_d[e], 16)
                schedule(sp, body)
                for e in range(2):
                    sp.wait_ge(st_d[e], 48 + 24 * NS)
                sp.wait_ge(S["cls_st"], 16 * NB)
                sp.wait_ge(x_ld[0], 8 * NS + 16)

            @block.gpsimd
            def _(pool):
                def body(F, b, i, e, on):
                    if "fin" in on:
                        s = F - OUTLAG - 1
                        at(pool, "u_d", s)
                        at(pool, "s1_d", s)
                        at(pool, "x2_d", s - 1)
                        at(pool, "bs_d", s - 1)
                        nc.gpsimd.tensor_tensor(h2[:].rearrange("p t c -> p (t c)"), ou[:].rearrange("p t c -> p (t c)"),
                                                s1[:, ds(ring(F, OUTLAG + 1, 2 * C), 2 * C)], ALU.add)\
                            .then_inc(S["h2_d"], 1)
                    if "lin" in on:
                        at(pool, "xnt", F - 3)
                        nc.gpsimd.tensor_tensor(xnl[:], xnT[:], xnh[:].bitcast(F32), ALU.subtract).then_inc(S["xl_d"], 1)
                    if "out" in on:
                        s = F - OUTLAG
                        at(pool, "q_t", s)
                        at(pool, "o2_ps", s - 2)
                        pool_waits(nc, pdot, 1)
                        q = qTs[:, ds(ring(F, OUTLAG, STEP), STEP)]
                        nc.gpsimd.tensor_copy(qch[:, e, :], q).then_inc(S["qc_h"], 1)
                        at(pool, "qc_h", s)
                        pool_waits(nc, pdot, 3)
                        nc.gpsimd.tensor_tensor(qcl[:, e, :], q, qch[:, e, :].bitcast(F32), ALU.subtract)\
                            .then_inc(S["qc_d"], 1)
                    if "fin" in on:
                        at(pool, "v2_d", F - OUTLAG - 1)
                        nc.gpsimd.tensor_tensor(r2[:], v2[:], mhalf[:, 0:2], ALU.pow).then_inc(S["r2_p"], 1)
                    if "mix" in on:
                        at(pool, "o_t", F - 2)
                        nc.gpsimd.tensor_tensor(ol[:], oT[:], oh[:].bitcast(F32), ALU.subtract).then_inc(S["ol_d"], 1)
                    if "out" in on:
                        s = F - OUTLAG
                        at(pool, "o2_q", s)
                        pool_waits(nc, pdot, 2)
                        nc.gpsimd.tensor_scalar(onr[:], oss[:], TINY2, None, ALU.max).then_inc(S["or_c"], 1)
                        pool.wait_ge(S["or_c"], s + 1)
                        nc.gpsimd.tensor_tensor(ors[:], onr[:], mhalf[:, 0:2], ALU.pow).then_inc(S["or_p"], 1)
                    if "mix" in on:
                        at(pool, "ln_v", F - 2)
                        nc.gpsimd.tensor_tensor(pwo[:], pwi[:], mhalf[:], ALU.pow).then_inc(S["ln_p"], 1)
                    if "fin" in on:
                        s = F - OUTLAG - 1
                        at(pool, "x2_d", s)
                        at(pool, "h2_d", s)
                        stored(pool, e, s)
                        nc.gpsimd.tensor_tensor(bs[:, e], h2[:], x2[:, e], ALU.add).then_inc(S["bs_d"], 1)
                schedule(pool, body)

            @block.scalar
            def _(act):
                def body(F, b, i, e, on):
                    if "tq" in on:
                        s = F - 4
                        at(act, "qm_s", s)
                        at(act, "qm_d", s - 1)
                        nc.scalar.activation(qex[:], qsh[:], ACT.Exp).then_inc(S["qm_e"], 1)
                    if "proj" in on:
                        at(act, "q_ps", F)
                        at(act, "sc_ps", F - 2)
                        for h in range(4):
                            r = slice(32 * h, 32 * h + 32)
                            for m in range(2):
                                ins = nc.scalar.activation(
                                    qblk[r, e, m * NJ:(m + 1) * NJ, h, :],
                                    P_QV[r, m * STEP:(m + 1) * STEP].rearrange("p (j q) -> p j q", q=BLK),
                                    ACT.Identity, bias=b1c[r, m:m + 1])
                        ins.then_inc(S["qb"], 1)
                    if "ctx" in on:
                        act.wait_ge(S["ctx_m"], b)
                        nc.scalar.activation(kT[:], kT[:], ACT.Exp, bias=nkmx[:, 0:1], accum_out=ksum[:, 0:1])\
                            .then_inc(S["ctx_e"], 1)
                    if "lin" in on:
                        s = F - 3
                        at(act, "tx_ps", s)
                        at(act, "lk_ps", s - 1)
                        for x in (xnT, xnh):
                            ins = nc.scalar.activation(x[:].rearrange("p k t -> p (k t)"), P_T[:, 0:KC * STEP], ACT.Copy)
                        ins.then_inc(S["xnt"], 1)
                    if "proj" in on:
                        at(act, "k_ps", F)
                        at(act, "sc_ps", F - 2)
                        for m in range(2):
                            ins = nc.scalar.activation(klin[:, e, m, :], P_K[:, m * STEP:(m + 1) * STEP], ACT.Identity,
                                                       bias=b1c[:, 2 + m:3 + m])
                        ins.then_inc(S["k_lin"], 1)
                    if "attn" in on:
                        s = F - 1
                        at(act, "sm_s", s)
                        at(act, "sm_p", s - 1)
                        nc.scalar.activation(pr[:], scs[:], ACT.Exp).then_inc(S["sm_e"], 1)
                    if "mix" in on:
                        s = F - 2
                        at(act, "pv_ps", s)
                        at(act, "w2_ps", s - 1)
                        for o in (oT, oh):
                            for m in range(2):
                                ins = nc.scalar.activation(
                                    o[:, m, :].rearrange("p (r w c) -> p r w c", r=WS, c=WS),
                                    P_PV[:, m * STEP:(m + 1) * STEP].rearrange("p (w r c) -> p r w c", r=WS, c=WS),
                                    ACT.Copy)
                        ins.then_inc(S["o_t"], 1)
                    if "ctx" in on:
                        for g in range(8):
                            act.wait_ge(S["ctx_t"], b * 8 - 8 + g + 1)
                            act.wait_ge(S["ctx_ps"], b * 8 - 8 + g + 1)
                            src = P_LK if g % 2 else P_K
                            if g < 7:
                                ins = nc.scalar.activation(kN[:, g % 2, :], src[0:TT, :], ACT.Copy)
                            else:
                                ins = nc.scalar.activation(kN[0:1 + NMEM, g % 2, 0:128], src[0:1 + NMEM, 0:128], ACT.Copy)
                            ins.then_inc(S["ctx_n"], 1)
                        nc.scalar.activation(kT[:, NTOK - 1:KCOL], kcst[:], ACT.Copy).then_inc(S["kc_d"], 1)
                    if "lin" in on:
                        s = F - 3
                        at(act, "ln_s", s)
                        for t in range(2):
                            ins = nc.scalar.activation(s1[:, ds(ring(F, 3, 2 * C) + t * C, C)], hh[:, 1 - e, t, :],
                                                       ACT.Identity, bias=nmr[:, 1 - e, t:t + 1], scale=asc[:, 1 - e, t:t + 1])
                        ins.then_inc(S["s1_d"], 1)
                    if "lin" in on:
                        s = F - 3
                        at(act, "lin_ps", s)
                        at(act, "qm_s", s - 1)
                        nc.scalar.activation(qraw[:].rearrange("p (t g) d -> p t (g d)", t=2), p_lin3[:, :, 0:128],
                                             ACT.Copy).then_inc(S["q_cp"], 1)
                        i3 = i - 3 if not isinstance(i, int) or i >= 3 else i - 3 + NWR
                        nc.scalar.activation(vst[:, ds(i3 * 2, 2), :], p_lin3[:, :, 128:256], ACT.Copy)\
                            .then_inc(S["v_cp"], 1)
                    if "out" in on:
                        s = F - OUTLAG
                        at(act, "o2_ps", s)
                        at(act, "u_d", s - 1)
                        for t in range(2):
                            ins = nc.scalar.activation(osq[:, t, :], P_K[0:TT, t * C:(t + 1) * C], ACT.Square, scale=float(C) ** -0.5,
                                                       accum_out=oss[:, t:t + 1])
                        ins.then_inc(S["o2_q"], 1)
                    if "lin" in on:
                        s = F - 3
                        at(act, "lk_ps", s)
                        nc.scalar.activation(kT[:, ds(i3 * STEP, STEP)], P_LK[:, 0:STEP], ACT.Copy)\
                            .then_inc(S["k_cp"], 1)
                    if "tq" in on:
                        s = F - 4
                        at(act, "tq_ps", s)
                        nc.scalar.activation(qTs[:, ds(ring(F, 4, STEP), STEP)], P_T[:, 0:STEP], ACT.Copy)\
                            .then_inc(S["q_t"], 1)
                schedule(act, body)

            @block.tensor
            def _(pe):
                def project(e, f, P, name):
                    for m in range(2):
                        for k in range(KC):
                            ins = nc.tensor.matmul(P[:, m * STEP:(m + 1) * STEP], w1T[:, k, f + m, :],
                                                   xw[:, e, k, :],
                                                   start=(k == 0), stop=(k == KC - 1))
                    ins.then_inc(S[name], 1)

                def scores(e, m):
                    for n in range(m * NJ, (m + 1) * NJ):
                        ins = nc.tensor.matmul(P_SC[:, n * BLK:(n + 1) * BLK],
                                               qblk[:, e, n, :, :].rearrange("p h q -> p (h q)"),
                                               klin[:, e, m, (n - m * NJ) * BLK:(n - m * NJ + 1) * BLK],
                                               start=True, stop=True)
                    return ins

                def attend(e, m):
                    for n in range(m * NJ, (m + 1) * NJ):
                        ins = nc.tensor.matmul(P_PV[:, n * BLK:(n + 1) * BLK],
                                               vblk[:, e, n, :, :].rearrange("p h q -> p (h q)"),
                                               pT[:, e, n, :], start=True, stop=True)
                    return ins

                def mix(F, on):
                    if "mix" in on:
                        s = F - 2
                        at(pe, "ol_d", s)
                        at(pe, "h_a", s - 1)
                        for t in range(2):
                            for m in range(2):
                                ins = split_matmul(nc, P_W2[0:TT, t * C:(t + 1) * C],
                                                   [o[:, m, t * TT:(t + 1) * TT] for o in (oh, ol)],
                                                   [w[:, m, :] for w in (w2h, w2l)], m == 0, m == 1)
                        ins.then_inc(S["w2_ps"], 1)

                def body(F, b, i, e, on):
                    if "attn" in on:
                        s = F - 1
                        at(pe, "qb", s)
                        at(pe, "k_lin", s)
                        at(pe, "sm_a", s - 1)
                        scores(1 - e, 0)
                    if "proj" in on:
                        pe.wait_ge(x_ld[e], (F - e) * 8 + 16)
                        at(pe, "vb", F - 1)
                        project(e, 0, P_QV, "q_ps")
                    if "attn" in on:
                        scores(1 - e, 1).then_inc(S["sc_ps"], 1)
                    if "fin" in on:
                        at(pe, "u_d", F - OUTLAG - 1)
                    if "proj" in on:
                        at(pe, "k_lin", F - 1)
                        project(e, 2, P_K, "k_ps")
                    if "lin" in on:
                        s = F - 3
                        at(pe, "xn_d", s)
                        at(pe, "q_t", s - 2)
                        transpose_xn(pe).then_inc(S["tx_ps"], 1)
                    if "mix" in on:
                        s = F - 2
                        at(pe, "sm_t", s)
                        at(pe, "vb", s)
                        at(pe, "o_t", s - 1)
                        attend(e, 0)
                    if "proj" in on:
                        at(pe, "qb", F)
                        project(e, 4, P_QV, "v_ps")
                    if "mix" in on:
                        attend(e, 1).then_inc(S["pv_ps"], 1)
                    if "ctx" in on:
                        pe.wait_ge(S["ctx_e"], b)
                        at(pe, "k_cp", F - 4)
                        at(pe, "v_cp", F - 4)
                        at(pe, "h_a", F - 3 if "proj" in on else F - 4)
                        if "proj" in on:
                            at(pe, "k_lin", F)

                        def turn(g):
                            if g >= 2:
                                pe.wait_ge(S["ctx_n"], b * 8 - 8 + g - 1)
                            P = P_LK if g % 2 else P_K
                            if g < 7:
                                for q in range(4):
                                    c0 = (4 * g + q) * TT
                                    ins = nc.tensor.transpose(P[0:TT, q * 128:(q + 1) * 128], kT[:, c0:c0 + TT], ident[:])
                            else:
                                ins = nc.tensor.transpose(P[0:1 + NMEM, 0:128], kT[:, NTOK - 1:KCOL], ident[:])
                            ins.then_inc(S["ctx_t"], 1)

                        def sum_up(g):
                            pe.wait_ge(S["ctx_n"], b * 8 - 8 + g + 1)
                            for q in range(4 if g < 7 else 1):
                                r = TT if g < 7 else 1 + NMEM
                                ins = nc.tensor.matmul(P_W2[:, 0:128], vst[0:r, 4 * g + q, :],
                                                       kN[0:r, g % 2, q * 128:(q + 1) * 128],
                                                       start=(g == 0 and q == 0), stop=(g == 7))
                            ins.then_inc(S["ctx_ps"], 1)

                        turn(0)
                        turn(1)
                        for g in range(8):
                            sum_up(g)
                            if g + 2 < 8:
                                turn(g + 2)
                    if "lin" in on:
                        s = F - 3
                        at(pe, "xl_d", s)
                        at(pe, "q_cp", s - 1)
                        at(pe, "v_cp", s - 1)
                        lin_qv(pe).then_inc(S["lin_ps"], 1)
                    if "ctx" in on:
                        pe.wait_ge(S["ctx_x"], b)
                        nc.tensor.matmul(P_LK[:, 0:C], ctxT[:], wout[:], start=True, stop=True).then_inc(S["ctx_mp"], 1)
                    if "ctx" in on:
                        mix(F, on)
                        pe.wait_ge(S["ctx_mw"], b)
                        nc.tensor.matmul(P_LK[0:1, 0:C], clsq[:], Mw[:], start=True, stop=True).then_inc(S["cls_ps"], 1)
                    if "out" in on:
                        s = F - OUTLAG
                        at(pe, "qc_d", s)
                        bo = b - 1 if not isinstance(i, int) or i >= OUTLAG - NWR else b - 2
                        pe.wait_ge(S["ctx_mw"], bo + 1)
                        if "proj" in on:
                            at(pe, "k_lin", F)
                        for t in range(2):
                            ins = split_matmul(nc, P_K[0:TT, t * C:(t + 1) * C],
                                               [q[:, e, t * TT:(t + 1) * TT] for q in (qch, qcl)],
                                               [Mh[:], Ml[:]], True, True)
                        ins.then_inc(S["o2_ps"], 1)
                    if "lin" in on:
                        s = F - 3
                        at(pe, "k_cp", s - 1)
                        if "ctx" in on:
                            pe.wait_ge(S["cls_c"], b)
                        lin_k(pe).then_inc(S["lk_ps"], 1)
                    if "ctx" not in on:
                        mix(F, on)
                    if "tq" in on:
                        s = F - 4
                        at(pe, "qm_d", s)
                        at(pe, "xnt", s + 1) if "lin" in on else None
                        transpose_q(pe).then_inc(S["tq_ps"], 1)
                schedule(pe, body)

            @block.vector
            def _(dve):
                def scale_output(F, on):
                    if "out" in on:
                        s = F - OUTLAG
                        at(dve, "or_p", s)
                        at(dve, "h2_d", s - 1)
                        for t in range(2):
                            ins = nc.vector.scalar_tensor_tensor(out=ou[:, t, :], in0=P_K[0:TT, t * C:(t + 1) * C], scalar=ors[:, t:t + 1],
                                                                 in1=gor[0:TT, :], op0=ALU.mult, op1=ALU.mult)
                        ins.then_inc(S["u_d"], 1)

                def finish_rows(F, e, on):
                    if "fin" in on:
                        s, o = F - OUTLAG - 1, e
                        at(dve, "r2_p", s)
                        at(dve, "bs_d", s - 2)
                        stored(dve, o, s)
                        for t in range(2):
                            ins = nc.vector.tensor_scalar(x2[:, o, t, :], h2[:, t, :], mv2[:, t, 0:1], r2[:, t:t + 1],
                                                          ALU.subtract, ALU.mult)
                        ins.then_inc(S["x2_d"], 1)
                        at(dve, "x2_d", s)
                        for t in range(2):
                            ins = nc.vector.tensor_tensor_reduce(wj[:, t, :], x2[:, o, t, :], wrr[0:TT, :], 1.0, 0.0, ALU.mult,
                                                                 ALU.add, ws0[:, t:t + 1])
                        link(dve, ins, S["o2_c"], s * 3 + 3)
                        nc.vector.tensor_scalar(wsv[:, o, :], ws0[:], brr[0:TT, 0:1], None, ALU.add).then_inc(S["w_dn"], 1)

                def body(F, b, i, e, on):
                    if "ctx" in on:
                        at(dve, "k_cp", F - 4)
                        if not isinstance(b, int) or b > 1:
                            dve.wait_ge(S["kc_d"], b - 1)
                        link(dve, nc.vector.tensor_reduce(kmx[:, 1:2], kT[:, (NWR - 1) * STEP:KCOL], AX, ALU.max),
                             S["ctx_c"], b * 6 - 4)
                        nc.vector.tensor_scalar(nkmx[:], kmx[:, 0:1], kmx[:, 1:2], -1.0, ALU.max, ALU.mult)\
                            .then_inc(S["ctx_m"], 1)
                    if "tq" in on:
                        s = F - 4
                        at(dve, "qm_e", s)
                        link(dve, nc.vector.tensor_reduce(qsm[:], qex[:], AX, ALU.add), S["qm_c"], s * 3 + 2)
                        link(dve, nc.vector.reciprocal(qrc[:], qsm[:]), S["qm_c"], s * 3 + 3)
                        at(dve, "tq_ps", s - 1)
                        nc.vector.tensor_tensor(qs[:], qex[:], group(qrc), ALU.mult).then_inc(S["qm_d"], 1)
                    if "attn" in on:
                        s, p = F - 1, 1 - e
                        last_row = isinstance(i, int) and i == 0
                        at(dve, "sc_ps", s)
                        for m in range(2):
                            ins = nc.vector.scalar_tensor_tensor(
                                out=sc[:, m * NJ:(m + 1) * NJ, :].rearrange("p j q -> p (j q)"),
                                in0=P_SC[:, m * STEP:(m + 1) * STEP], scalar=ISC, in1=tbl[:, int(last_row), :],
                                op0=ALU.mult, op1=ALU.add)
                        ins.then_inc(S["sm_a"], 1)
                        at(dve, "sm_a", s)
                        link(dve, nc.vector.tensor_reduce(smx[:], sc[:], AX, ALU.max), S["sm_c"], s * 3 + 1)
                        at(dve, "sm_e", s - 1)
                        nc.vector.tensor_tensor(scs[:], sc[:], group(smx), ALU.subtract).then_inc(S["sm_s"], 1)
                    if "fin" in on:
                        s = F - OUTLAG - 1
                        at(dve, "h2_d", s)
                        for t in range(2):
                            ins = nc.vector.bn_stats(bst2[:, t, :], h2[:, t, :])
                        link(dve, ins, S["o2_c"], s * 3 + 1)
                        nc.vector.tensor_copy(vdot[:, 2:3], vdot[:, 0:1])
                        for t in range(2):
                            ins = nc.vector.bn_aggr(mv2[:, t, :], bst2[:, t, :])
                        link(dve, ins, S["o2_c"], s * 3 + 2)
                        nc.vector.tensor_scalar(v2[:], mv2[:, :, 1], EPS, None, ALU.add).then_inc(S["v2_d"], 1)
                    if "attn" in on:
                        s, p = F - 1, 1 - e
                        at(dve, "sm_e", s)
                        link(dve, nc.vector.tensor_reduce(ssm[:], pr[:], AX, ALU.add), S["sm_c"], s * 3 + 2)
                        link(dve, nc.vector.reciprocal(srec[:], ssm[:]), S["sm_c"], s * 3 + 3)
                        nc.vector.tensor_tensor(prn[:], pr[:], group(srec), ALU.mult).then_inc(S["sm_p"], 1)
                        at(dve, "sm_p", s)
                        at(dve, "pv_ps", s - 2)
                        nc.vector.transpose(pT[:, p].rearrange("p n q -> p (n q)"),
                                            prn[:].rearrange("p n q -> p (n q)")).then_inc(S["sm_t"], 1)
                    if "ctx" in on:
                        dve.wait_ge(S["ctx_e"], b)
                        if not isinstance(b, int) or b > 1:
                            dve.wait_ge(S["ctx_mw"], b - 1)
                        link(dve, nc.vector.reciprocal(krc[:], ksum[:]), S["ctx_c"], b * 6 - 3)
                        dve.wait_ge(S["ctx_ps"], b * 8 + 2)
                        nc.vector.tensor_tensor(ctxT[:], P_W2[:, 0:128], hmask[:], ALU.mult).then_inc(S["ctx_x"], 1)
                    if "proj" in on:
                        at(dve, "v_ps", F)
                        at(dve, "pv_ps", F - 2)
                        for h in range(4):
                            r = slice(32 * h, 32 * h + 32)
                            ins = nc.vector.transpose(vblk[r, e, :, h, :],
                                                      P_QV[r, 0:2 * STEP].rearrange("p (n q) -> p n q", q=BLK))
                        ins.then_inc(S["vb"], 1)
                    if "lin" in on:
                        s = F - 3
                        at(dve, "q_cp", s)
                        link(dve, nc.vector.tensor_reduce(qmx[:], qraw[:], AX, ALU.max), S["qm_c"], s * 3 + 1)
                        at(dve, "qm_e", s - 1)
                        nc.vector.tensor_tensor(qsh[:], qraw[:], group(qmx), ALU.subtract).then_inc(S["qm_s"], 1)
                    if "kmax" in on:
                        at(dve, "k_cp", F - 4)
                        nc.vector.tensor_reduce(kmx[:, 0:1], kT[:, 0:(NWR - 1) * STEP], AX, ALU.max)\
                            .then_inc(S["ctx_c"], 1)
                    if "ctx" in on:
                        dve.wait_ge(S["ctx_mp"], b)
                        if "fin" in on:
                            at(dve, "o2_ps", F - OUTLAG - 1)
                        link(dve, nc.vector.tensor_scalar(Mq[:], P_LK[:, 0:C], krc[:, 0:1], QSC, ALU.mult, ALU.mult),
                             S["ctx_c"], b * 6 - 2)
                        link(dve, nc.vector.tensor_tensor(Mw[:], Mq[:], boq[:], ALU.add), S["ctx_c"], b * 6 - 1)
                        link(dve, upper_part(nc, Mh[:], Mw[:]), S["ctx_c"], b * 6)
                        lower_part(nc, Ml[:], Mw[:], Mh[:]).then_inc(S["ctx_mw"], 1)
                        dve.wait_ge(S["cls_ps"], b)
                        if not isinstance(b, int) or b > 1:
                            dve.wait_ge(S["cls_st"], b * 16 - 16)
                        nc.vector.tensor_copy(clso[0:1, 0, :], P_LK[0:1, 0:C]).then_inc(S["cls_c"], 1)
                    if "mix" in on:
                        s = F - 2
                        at(dve, "w2_ps", s)
                        at(dve, "s1_d", s - 2)
                        ins = nc.vector.tensor_tensor(
                            hh[:, e], P_W2[0:TT, :].rearrange("p (t c) -> p t c", t=2),
                            b2r[0:TT, :].rearrange("p (o c) -> p o c", o=1).broadcast_to([TT, 2, C]), ALU.add)
                        ins.then_inc(S["h_a"], 1)
                        at(dve, "h_a", s)

                        def powered():
                            scale_output(F, on)
                            finish_rows(F, e, on)
                            at(dve, "ln_p", s)
                        layer_norm_1(hh[:, e], e, lambda ins, k: link(dve, ins, S["ln_c"], s * 5 + k),
                                     lambda name: (S[name], 1), powered, lambda: at(dve, "tx_ps", s - 1))
                    else:
                        scale_output(F, on)
                        finish_rows(F, e, on)
                schedule(dve, body)

        G = NB
        with nc.Block() as block:
            @block.sync
            def _(sp):
                sp.dma_start(ob[0:G, 0, :], clsd).then_inc(S["fin_ld"], 16)
                sp.wait_ge(S["fin_d"], 8)
                sp.dma_start(out[:, 0, :], bs[0:G, 0, 0, :]).then_inc(S["fin_st"], 16)
                sp.dma_start(x2d[:, 0, :], x2[0:G, 0, 0, :]).then_inc(S["fin_st"], 16)
                sp.dma_start(wd[:, 0:1], wsv[0:G, 0, 0:1], allow_slow_non_contiguous=True)\
                    .then_inc(S["fin_st"], 16)
                sp.wait_ge(S["fin_st"], 48)

            @block.gpsimd
            def _(pool):
                pool.wait_ge(S["fin_d"], 2)
                nc.gpsimd.tensor_tensor(ors[0:G, 0:1], onr[0:G, 0:1], mhalf[0:G, 0:1], ALU.pow).then_inc(S["fin_p"], 1)
                pool.wait_ge(S["fin_d"], 7)
                nc.gpsimd.tensor_tensor(r2[0:G, 0:1], v2[0:G, 0:1], mhalf[0:G, 0:1], ALU.pow).then_inc(S["fin_p"], 1)

            @block.scalar
            def _(act):
                act.wait_ge(S["fin_d"], 1)
                nc.scalar.activation(osq[0:G, 0, :], ob[0:G, 1, :], ACT.Square, scale=float(C) ** -0.5,
                                     accum_out=oss[0:G, 0:1]).then_inc(S["fin_a"], 1)

            @block.vector
            def _(dve):
                n = [0]

                def lnk(ins):
                    n[0] += 1
                    link(dve, ins, S["fin_d"], n[0])

                dve.wait_ge(S["fin_ld"], 16)
                lnk(nc.vector.tensor_copy(ob[0:G, 1, :], ob[0:G, 0, :]))
                dve.wait_ge(S["fin_a"], 1)
                lnk(nc.vector.tensor_scalar(onr[0:G, 0:1], oss[0:G, 0:1], TINY2, None, ALU.max))
                dve.wait_ge(S["fin_p"], 1)
                lnk(nc.vector.scalar_tensor_tensor(out=ou[0:G, 0, :], in0=ob[0:G, 1, :], scalar=ors[0:G, 0:1],
                                                   in1=gor[0:G], op0=ALU.mult, op1=ALU.mult))
                lnk(nc.vector.tensor_tensor(h2[0:G, 0, :], ou[0:G, 0, :], clss[0:G], ALU.add))
                lnk(nc.vector.bn_stats(bst2[0:G, 0, :], h2[0:G, 0, :]))
                lnk(nc.vector.bn_aggr(mv2[0:G, 0, :], bst2[0:G, 0, :]))
                lnk(nc.vector.tensor_scalar(v2[0:G, 0:1], mv2[0:G, 0, 1:2], EPS, None, ALU.add))
                dve.wait_ge(S["fin_p"], 2)
                nc.vector.tensor_scalar(x2[0:G, 0, 0, :], h2[0:G, 0, :], mv2[0:G, 0, 0:1], r2[0:G, 0:1],
                                        ALU.subtract, ALU.mult).then_inc(S["fin_x"], 1)
                dve.wait_ge(S["fin_x"], 1)
                nc.vector.tensor_tensor(bs[0:G, 0, 0, :], h2[0:G, 0, :], x2[0:G, 0, 0, :], ALU.add)
                nc.vector.tensor_tensor_reduce(wj[0:G, 0, :], x2[0:G, 0, 0, :], wrr[0:G, :], 1.0, 0.0, ALU.mult,
                                               ALU.add, ws0[0:G, 0:1]).then_inc(S["fin_x"], 1)
                dve.wait_ge(S["fin_x"], 2)
                nc.vector.tensor_scalar(wsv[0:G, 0, 0:1], ws0[0:G, 0:1], brr[0:G, 0:1], None, ALU.add)\
                    .then_inc(S["fin_d"], 1)


def select_program(nc, A, ctx):
    wd = A["wd"]

    def sb(name, shape, dt=F32):
        return ctx.enter_context(nc.sbuf_tensor(name, shape, dt))

    ids = sb("ids", [128, SLOTS], I32)
    with ExitStack() as tmp:
        def tb(name, shape, dt=F32):
            return tmp.enter_context(nc.sbuf_tensor(name, shape, dt))

        wt = tb("wt", [128, SEG]); same = tb("same", [128, 128]); before = tb("before", [128, 128])
        allb = tb("allb", [128, 128]); iot = tb("iot", [128, SLOTS])
        idf = tb("idf", [128, SEG])
        bits = tb("bits", [128, 32], I32); u = tb("u", [128, 1], I32); cand = tb("cand", [128, 1], I32)
        msk = tb("msk", [128, 1], I32); thr = tb("thr", [128, 1], I32); okm = tb("okm", [128, 1], I32)
        cnt = tb("cnt", [128, 1]); junk = tb("junk", [128, SEG]); ones = tb("ones", [128, SEG]); zer = tb("zer", [128, SEG])
        gt = tb("gt", [128, SEG]); eq = tb("eq", [128, SEG]); esc = tb("esc", [128, SEG]); seleq = tb("seleq", [128, SEG])
        sel = tb("sel", [128, SEG]); psc = tb("psc", [128, SEG]); pos = tb("pos", [128, SEG]); poi = tb("poi", [128, SEG], I32)
        pdi = tb("pdi", [128, SEG], I32); pmi = tb("pmi", [128, SEG], I32); pdf = tb("pdf", [128, SEG]); pmf = tb("pmf", [128, SEG])
        room = tb("room", [128, 1]); room1 = tb("room1", [128, 1])
        UN = 8
        onL = tb("onL", [128, UN, 128]); onR = tb("onR", [128, UN, SLOTS])
        P_C = tmp.enter_context(nc.psum_tensor("p_cnt", [128, 512], F32))
        P_L = tmp.enter_context(nc.psum_tensor("p_list", [128, 512], F32))
        S = {n: tmp.enter_context(nc.semaphore("sel_" + n)) for n in "ld c cn cp l mm".split()}
        loads = [(wt, wd.rearrange("b (s f) -> (b s) f", s=8)), (same, A["same"]), (before, A["before"]), (allb, A["allb"]),
                 (iot, A["iota"]), (idf, A["idf"]), (bits, A["bits"])]
        thf = thr[:].bitcast(F32)
        with nc.Block() as block:
            @block.sync
            def _(sp):
                for dst, src in loads:
                    sp.dma_start(dst[:], src).then_inc(S["ld"], 16)
                sp.wait_ge(S["ld"], 16 * len(loads))

            @block.vector
            def _(dve):
                dve.wait_ge(S["ld"], 16 * len(loads))
                PER = 5

                def lnk(ins, v):
                    link(dve, ins, S["c"], v)

                def threshold(key, v):
                    lnk(nc.vector.tensor_scalar(msk[:], key[:], 31, -1, ALU.arith_shift_right, ALU.bitwise_xor), v + 1)
                    lnk(nc.vector.scalar_tensor_tensor(out=thr[:], in0=msk[:], scalar=-2147483648, in1=key[:],
                                                       op0=ALU.bitwise_or, op1=ALU.bitwise_xor), v + 2)

                nc.vector.memset(u[:], 0)
                nc.vector.memset(ones[:], 1.0)
                lnk(nc.vector.memset(zer[:], 0.0), 1)
                with dve.Fori(0, 31, 2) as r2:
                    for k in range(2):
                        r = r2 + k
                        v = r * PER + 1
                        bit = bits[:, ds(r, 1)]
                        lnk(nc.vector.tensor_tensor(cand[:], u[:], bit, ALU.bitwise_or), v + 1)
                        threshold(cand, v + 1)
                        nc.vector.scalar_tensor_tensor(out=junk[:], in0=wt[:], scalar=thf[:, 0:1], in1=ones[:],
                                                       op0=ALU.is_ge, op1=ALU.mult, accum_out=cnt[:])\
                            .then_inc(S["cn"], 1)
                        dve.wait_ge(S["cp"], r + 1)
                        lnk(nc.vector.tensor_scalar(okm[:], P_C[:, 0:1], float(KK), -1.0, ALU.is_ge, ALU.mult), v + 4)
                        lnk(nc.vector.scalar_tensor_tensor(out=u[:], in0=okm[:], scalar=bit, in1=u[:],
                                                           op0=ALU.bitwise_and, op1=ALU.bitwise_or), v + 5)
                v = 32 * PER + 1
                threshold(u, v)
                nc.vector.scalar_tensor_tensor(out=gt[:], in0=wt[:], scalar=thf[:, 0:1], in1=ones[:], op0=ALU.is_gt,
                                               op1=ALU.mult, accum_out=cnt[:]).then_inc(S["cn"], 1)
                lnk(nc.vector.tensor_scalar(eq[:], wt[:], thf[:, 0:1], None, ALU.is_equal), v + 3)
                nc.vector.tensor_tensor_scan(esc[:], eq[:], zer[:], 0.0, ALU.add, ALU.add).then_inc(S["cn"], 1)
                dve.wait_ge(S["cp"], 34)
                lnk(nc.vector.tensor_scalar(room[:], P_C[:, 0:1], -1.0, float(KK), ALU.mult, ALU.add), v + 4)
                lnk(nc.vector.tensor_tensor(room1[:], room[:], P_C[:, 1:2], ALU.subtract), v + 5)
                lnk(nc.vector.scalar_tensor_tensor(out=seleq[:], in0=esc[:], scalar=room1[:, 0:1], in1=eq[:],
                                                   op0=ALU.is_le, op1=ALU.mult), v + 6)
                lnk(nc.vector.tensor_tensor(sel[:], gt[:], seleq[:], ALU.add), v + 7)
                nc.vector.tensor_tensor_scan(psc[:], sel[:], zer[:], 0.0, ALU.add, ALU.add).then_inc(S["cn"], 1)
                dve.wait_ge(S["cp"], 35)
                lnk(nc.vector.tensor_copy(room[:], P_C[:, 2:3]), v + 8)
                lnk(nc.vector.scalar_tensor_tensor(out=pos[:], in0=psc[:], scalar=room[:, 0:1], in1=sel[:],
                                                   op0=ALU.add, op1=ALU.mult), v + 9)
                lnk(nc.vector.tensor_scalar(poi[:], pos[:], -1.0, None, ALU.add), v + 10)
                nc.vector.tensor_scalar(pdi[:], poi[:], 7, None, ALU.arith_shift_right)
                lnk(nc.vector.tensor_scalar(pmi[:], poi[:], 127, None, ALU.bitwise_and), v + 11)
                nc.vector.tensor_copy(pdf[:], pdi[:])
                lnk(nc.vector.tensor_copy(pmf[:], pmi[:]), v + 12)
                with dve.Fori(0, SEG - UN + 1, UN) as f:
                    for q in range(UN):
                        dve.wait_ge(S["mm"], f + q + 1)
                        nc.vector.tensor_scalar(onL[:, q, :], iot[:, 0:128], pmf[:, ds(f + q, 1)], idf[:, ds(f + q, 1)],
                                                ALU.is_equal, ALU.mult)
                        nc.vector.tensor_scalar(onR[:, q, :], iot[:], pdf[:, ds(f + q, 1)], None, ALU.is_equal)\
                            .then_inc(S["l"], 1)
                dve.wait_ge(S["mm"], SEG + UN)
                lnk(nc.vector.tensor_copy(ids[:], P_L[:, 0:SLOTS]), v + 13)

            @block.tensor
            def _(pe):
                pe.wait_ge(S["ld"], 16 * len(loads))
                pe.sem_inc(S["mm"], UN)
                with pe.Fori(0, 32) as r:
                    pe.wait_ge(S["cn"], r + 1)
                    nc.tensor.matmul(P_C[:, 0:1], same[:], cnt[:], start=True, stop=True).then_inc(S["cp"], 1)
                pe.wait_ge(S["cn"], 33)
                nc.tensor.matmul(P_C[:, 0:1], same[:], cnt[:], start=True, stop=True).then_inc(S["cp"], 1)
                pe.wait_ge(S["cn"], 34)
                nc.tensor.matmul(P_C[:, 1:2], before[:], esc[:, SEG - 1:SEG], start=True, stop=True).then_inc(S["cp"], 1)
                pe.wait_ge(S["cn"], 35)
                nc.tensor.matmul(P_C[:, 2:3], allb[:], psc[:, SEG - 1:SEG], start=True, stop=True).then_inc(S["cp"], 1)

                def add(q, v, start, stop):
                    pe.wait_ge(S["l"], v)
                    return nc.tensor.matmul(P_L[:, 0:SLOTS], onL[:, q, :], onR[:, q, :],
                                            start=start, stop=stop).then_inc(S["mm"], 1)
                add(0, 1, True, False)
                for q in range(1, UN):
                    add(q, q + 1, False, False)
                with pe.Fori(UN, SEG - 2 * UN + 1, UN) as f:
                    for q in range(UN):
                        add(q, f + q + 1, False, False)
                for q in range(UN):
                    add(q, SEG - UN + q + 1, False, q == UN - 1)
    return ids


def feed_forward_program(nc, A, ids):
    with ExitStack() as ctx:
        def sb(name, shape, dt=F32):
            return ctx.enter_context(nc.sbuf_tensor(name, shape, dt))

        w1 = sb("w1", [128, KC, FF]); b1 = sb("b1", [128, NHB]); w2 = sb("w2", [128, NHB, C])
        b2 = sb("b2", [128, C]); wr = sb("wr", [128, C]); br = sb("br", [128, 1]); idn = sb("idn", [128, 128])
        ix = sb("ix", [128, 4, 2], I32); pdot = sb("pdot3", [1, 16])
        xg = sb("xg", [128, 2, 2, C]); xh = sb("xh", [128, 2, KC, 256], F32R); xl = sb("xl", [128, 2, KC, 256], F32R)
        w1h = sb("w1h", [128, KC, FF], F32R); w1l = sb("w1l", [128, KC, FF], F32R)
        w2h = sb("w2h", [128, NHB, C], F32R); w2l = sb("w2l", [128, NHB, C], F32R)
        wsj = sb("wsj", [128, 2, C]); wg = sb("wg", [128, 2]); wgb = sb("wgb", [128, 2, 2])
        hT = sb("hT", [128, NHB, 256])
        hh = sb("hth", [128, 2, NHB, 256], F32R); hl = sb("htl", [128, 2, NHB, 256], F32R); yb = sb("yb", [128, 2, 2, C]); ym = sb("ym", [128, 2, 2, C])
        P_X = ctx.enter_context(nc.psum_tensor("p_x", [128, 512], F32))
        P_H = [ctx.enter_context(nc.psum_tensor(f"p_h{n}", [128, 512], F32)) for n in range(4)]
        P_Y = [ctx.enter_context(nc.psum_tensor(f"p_y{n}", [128, 512], F32)) for n in range(2)]
        S = {n: ctx.enter_context(nc.semaphore("ff_" + n)) for n in
             "dot ld ix g0 g1 xt xu xc h0 h1 h2 h3 e hu hs y ya ym wc w ws s0 s1".split()}
        g, st = (S["g0"], S["g1"]), (S["s0"], S["s1"])
        loads = [(w1, "fw1"), (b1, "fb1"), (w2, "fw2"), (b2, "fb2"), (wr, "wrr"), (br, "brr"), (idn, "ident")]
        LAST = NSEL - (NPAIR * 256 - 128)
        out_rows, x2_rows = A["out_rows"], A["x2d"].rearrange("b n c -> (b n) c")

        def pairs(eng, body):
            for p in range(2):
                body(p, p, False)
            with eng.Fori(2, NPAIR - 3, 2) as p:
                body(p, 0, False)
                body(p + 1, 1, False)
            body(NPAIR - 2, 0, False)
            body(NPAIR - 1, 1, True)

        with nc.Block() as block:
            @block.sync
            def _(sp):
                for dst, name in loads:
                    sp.dma_start(dst[:], A[name]).then_inc(S["ld"], 16)
                sp.wait_ge(S["ld"], 16 * len(loads))

            @block.gpsimd
            def _(pool):
                def index(p, q):
                    pool_waits(nc, pdot, 4)
                    nc.gpsimd.tensor_copy(ix[:, q, :], ids[:, ds(p * 2, 2)]).then_inc(S["ix"], 1)

                def rows(last, t):
                    return LAST if last and t == 1 else 128

                def gather(p, e, q, last):
                    pool.wait_ge(S["ix"], p + 1)
                    pool.wait_ge(S["xt"], p + 1)
                    pool.wait_ge(S["w"], p + 1)
                    pool_waits(nc, pdot, 5)
                    for t in range(2):
                        r = rows(last, t)
                        nc.gpsimd.indirect_dma_start(
                            out=xg[0:r, e, t, :], out_offset=None, in_=x2_rows,
                            in_offset=bass.IndirectOffsetOnAxis(ap=ix[0:r, q, t:t + 1], axis=0)).then_inc(g[e], 16)

                def scatter(p, e, q, last):
                    pool.wait_ge(S["ym"], p + 1)
                    pool_waits(nc, pdot, 6 + q)
                    for t in range(2):
                        r = rows(last, t)
                        nc.gpsimd.indirect_dma_start(
                            out=out_rows, out_offset=bass.IndirectOffsetOnAxis(ap=ix[0:r, q, t:t + 1], axis=0),
                            in_=ym[0:r, e, t, :], in_offset=None, compute_op=ALU.add).then_inc(st[e], 16)

                nc.gpsimd.memset(pdot[:], 0.0).then_inc(S["dot"], 1)
                pool.wait_ge(S["dot"], 1)
                def step(p, e, q, last):
                    index(p, q)
                    gather(p, e, q, last)
                    scatter(p - 3, 1 - e, (q + 1) % 4, False)

                for p in range(3):
                    index(p, p)
                    gather(p, p % 2, p, False)
                step(3, 1, 3, False)
                with pool.Fori(4, NPAIR - 5, 4) as p:
                    for k in range(4):
                        pool.wait_ge(st[k % 2], (p + (k - k % 2)) * 16 - 32)
                        step(p + k, k % 2, k, False)
                for p in range(NPAIR - NPAIR % 4, NPAIR):
                    pool.wait_ge(st[p % 2], (p - p % 2) * 16 - 32)
                    step(p, p % 2, p % 4, p == NPAIR - 1)
                for p in range(NPAIR - 3, NPAIR):
                    scatter(p, p % 2, p % 4, p == NPAIR - 1)
                for e in range(2):
                    pool.wait_ge(st[e], 32 * (NPAIR // 2))

            @block.tensor
            def _(pe):
                def turn(p, e):
                    pe.wait_ge(g[e], (p - e) * 16 + 32)
                    pe.wait_ge(S["xc"], p + 2)
                    for t in range(2):
                        for k in range(KC):
                            ins = nc.tensor.transpose(P_X[:, k * 256 + t * 128:k * 256 + (t + 1) * 128],
                                                      xg[:, e, t, k * 128:(k + 1) * 128], idn[:])
                    ins.then_inc(S["xt"], 1)

                def up(p, e):
                    pe.wait_ge(S["xc"], p + 3)
                    for n in range(4):
                        pe.wait_ge(S["e"], (p + 1) * 4 + n + 1)
                        for m in range(2):
                            for k in range(KC):
                                hb = 2 * n + m
                                ins = split_matmul(nc, P_H[n][:, m * 256:(m + 1) * 256],
                                                   [w[:, k, hb * 128:(hb + 1) * 128] for w in (w1h, w1l)],
                                                   [x[:, e, k, :] for x in (xh, xl)], k == 0, k == KC - 1)
                        ins.then_inc(S[f"h{n}"], 1)

                def down(p, e):
                    pe.wait_ge(S["ya"], p + 1)
                    pe.wait_ge(S["hs"], (p + 2) * 4 + 4)
                    for t in range(2):
                        for hb in range(NHB):
                            ins = split_matmul(nc, P_Y[e][:, t * C:(t + 1) * C],
                                               [h[:, e, hb, t * 128:(t + 1) * 128] for h in (hh, hl)],
                                               [w[:, hb, :] for w in (w2h, w2l)], hb == 0, hb == NHB - 1)
                    ins.then_inc(S["y"], 1)

                pe.wait_ge(S["ld"], 16 * len(loads))
                pe.wait_ge(S["ws"], 4)
                pe.sem_inc(S["xt"], 2)
                pe.sem_inc(S["y"], 2)
                turn(0, 0)
                up(0, 0)
                turn(1, 1)
                up(1, 1)
                turn(2, 0)
                down(0, 0)
                with pe.Fori(2, NPAIR - 3, 2) as p:
                    for e in range(2):
                        up(p + e, e)
                        turn(p + e + 1, 1 - e)
                        down(p + e - 1, 1 - e)
                up(NPAIR - 2, 0)
                turn(NPAIR - 1, 1)
                down(NPAIR - 3, 1)
                up(NPAIR - 1, 1)
                down(NPAIR - 2, 0)
                down(NPAIR - 1, 1)

            @block.scalar
            def _(act):
                act.wait_ge(S["ld"], 16 * len(loads))
                act.sem_inc(S["e"], 8)

                def body(p, e, last):
                    for n in range(4):
                        act.wait_ge(S["hs"], (p + 1) * 4 + n + 1)
                        act.wait_ge(S[f"h{n}"], p + 1)
                        for m in range(2):
                            hb = 2 * n + m
                            ins = nc.scalar.activation(hT[:, hb, :], P_H[n][:, m * 256:(m + 1) * 256],
                                                       ACT.Gelu_apprx_tanh, bias=b1[:, hb:hb + 1])
                        ins.then_inc(S["e"], 1)
                pairs(act, body)

            @block.vector
            def _(dve):
                dve.wait_ge(S["ld"], 16 * len(loads))
                dve.sem_inc(S["xc"], 2)
                dve.sem_inc(S["ya"], 2)
                dve.sem_inc(S["w"], 2)
                dve.sem_inc(S["wc"], 2)
                dve.sem_inc(S["hs"], 8)
                for n, (high, low, w) in enumerate(((w1h, w1l, w1), (w2h, w2l, w2))):
                    high, low, w = (x[:].rearrange("p k f -> p (k f)") for x in (high, low, w))
                    upper_part(nc, high, w).then_inc(S["ws"], 1)
                    dve.wait_ge(S["ws"], 2 * n + 1)
                    lower_part(nc, low, w, high).then_inc(S["ws"], 1)

                def turned(p, e):
                    dve.wait_ge(S["xt"], p + 3)
                    dve.wait_ge(S["h3"], p - 1) if not isinstance(p, int) or p >= 2 else None
                    high, low = (x[:, e].rearrange("p k t -> p (k t)") for x in (xh, xl))
                    upper_part(nc, high, P_X[:]).then_inc(S["xu"], 1)
                    dve.wait_ge(S["xu"], p + 1)
                    lower_part(nc, low, P_X[:], high).then_inc(S["xc"], 1)

                def hidden(p, e):
                    dve.wait_ge(S["y"], p + 1)
                    for n in range(4):
                        high, low, x = (h[:, 2 * n:2 * n + 2, :].rearrange("p h t -> p (h t)")
                                        for h in (hh[:, e], hl[:, e], hT))
                        dve.wait_ge(S["e"], (p + 2) * 4 + n + 1)
                        upper_part(nc, high, x).then_inc(S["hu"], 1)
                        dve.wait_ge(S["hu"], p * 4 + n + 1)
                        lower_part(nc, low, x, high).then_inc(S["hs"], 1)

                def weigh(p, e):
                    dve.wait_ge(g[e], (p - e) * 16 + 32)
                    dve.wait_ge(S["wc"], p + 2)
                    for t in range(2):
                        ins = nc.vector.tensor_tensor_reduce(wsj[:, t, :], xg[:, e, t, :], wr[:], 1.0, 0.0, ALU.mult,
                                                             ALU.add, wg[:, t:t + 1])
                    ins.then_inc(S["w"], 1)
                    dve.wait_ge(S["w"], p + 3)
                    nc.vector.tensor_scalar(wgb[:, e, :], wg[:], br[:, 0:1], None, ALU.add).then_inc(S["wc"], 1)

                def second(p, e):
                    dve.wait_ge(S["y"], p + 3)
                    nc.vector.tensor_tensor(yb[:, e], P_Y[e][:].rearrange("p (t c) -> p t c", t=2),
                                            b2[:].rearrange("p (o c) -> p o c", o=1).broadcast_to([128, 2, C]), ALU.add)\
                        .then_inc(S["ya"], 1)
                    dve.wait_ge(S["ya"], p + 3)
                    dve.wait_ge(S["wc"], p + 3)
                    dve.wait_ge(st[e], (p - e) * 16 + 0) if not isinstance(p, int) or p >= 2 else None
                    for t in range(2):
                        ins = nc.vector.tensor_scalar(ym[:, e, t, :], yb[:, e, t, :], wgb[:, e, t:t + 1], None, ALU.mult)
                    ins.then_inc(S["ym"], 1)

                turned(0, 0)
                weigh(0, 0)
                hidden(0, 0)
                turned(1, 1)
                weigh(1, 1)
                hidden(1, 1)
                turned(2, 0)
                second(0, 0)
                weigh(2, 0)
                with dve.Fori(2, NPAIR - 3, 2) as p:
                    for e in range(2):
                        hidden(p + e, e)
                        turned(p + e + 1, 1 - e)
                        second(p + e - 1, 1 - e)
                        weigh(p + e + 1, 1 - e)
                hidden(NPAIR - 2, 0)
                turned(NPAIR - 1, 1)
                second(NPAIR - 3, 1)
                weigh(NPAIR - 1, 1)
                hidden(NPAIR - 1, 1)
                second(NPAIR - 2, 0)
                second(NPAIR - 1, 1)


def lay_out(inputs):
    import numpy as np
    f = {n: np.asarray(a) for n, a in inputs.items()}
    x = np.concatenate([f["x"][:, :, WS // 2:], f["x"][:, :, :WS // 2]], axis=2)
    x = np.concatenate([x[:, :, :, WS // 2:], x[:, :, :, :WS // 2]], axis=3)
    x = x.reshape(NB, KC, 128, NWR, WS, NWR, WS).transpose(0, 3, 2, 1, 5, 4, 6).reshape(NS, 128, KC, STEP)
    xw = np.concatenate([x, x[:1]], axis=0)
    w1 = f["L0_tok_w1"].reshape(E, NH, 3, C).transpose(2, 1, 0, 3).reshape(6, 128, C)
    b1 = f["L0_tok_b1"].reshape(E, NH, 3).transpose(2, 1, 0).reshape(6, 128)
    tok = np.arange(BLK)
    win, row, col = tok // 16, tok % 16 // WS, tok % WS
    pos = f["L0_tok_pos_emb"][row[None, :] - row[:, None] + WS - 1, col[None, :] - col[:, None] + WS - 1]
    other = win[:, None] != win[None, :]
    half = WS // 2
    rows = (row[:, None] >= half) != (row[None, :] >= half)
    cols = (col[:, None] >= half) != (col[None, :] >= half)
    mask = np.zeros((2, NJ, BLK, BLK), np.float32)
    mask[:, :, other] = NEG
    mask[1, :, rows] = NEG
    edge = cols & (win[:, None] == 1) & (win[None, :] == 1)
    mask[:, NJ - 1, edge] = NEG
    mask = np.broadcast_to(mask.transpose(2, 0, 1, 3)[None], (4, BLK, 2, NJ, BLK)).reshape(128, 2, STEP)
    posr = np.broadcast_to(pos[None, :, None, :], (4, BLK, NJ, BLK)).reshape(128, STEP)
    q, k, v = np.split(f["L0_attn_w_qkv"], 3, axis=1)
    wlin = np.concatenate([q, v, k], axis=1).reshape(KC, 128, 3 * HID).transpose(1, 0, 2)

    def rep(a, n=128):
        return np.broadcast_to(a.reshape(1, -1), (n, a.size))
    part = np.arange(128)
    mk, mvv = f["L0_attn_mem_kv"]
    tokid = (part // 8 * NTOK + part % 8 * SEG)[:, None] + np.arange(SEG)[None, :]
    tokid = np.where(np.arange(SEG)[None, :] + (part % 8 * SEG)[:, None] < NTOK, tokid, 0)
    return {
        "xw": xw, "w1T": w1.transpose(2, 0, 1).reshape(KC, 128, 6, 128).transpose(1, 0, 2, 3), "b1c": b1.T,
        "w2T": f["L0_tok_w2"].T.reshape(KC, 128, C).transpose(1, 0, 2), "b2r": rep(f["L0_tok_b2"]),
        "posr": posr, "mask": mask, "ident": np.eye(128, dtype=np.float32),
        "gpre": f["L0_attn_g_pre"].reshape(KC, 128).T, "wlin": wlin, "wout": f["L0_attn_w_out"],
        "hmask": (part[:, None] // 32 == part[None, :] // 32).astype(np.float32),
        "bor": rep(f["L0_attn_b_out"]), "gor": rep(f["L0_attn_g_out"]), "wrr": rep(f["L0_ffn_wr"]),
        "brr": rep(f["L0_ffn_br"]), "clsr": rep(f["cls_tok"], TT),
        "memk": mk.reshape(HID, NMEM), "memv": mvv.reshape(HID, NMEM).T,
        "wpad": np.full((NB, 8 * SEG), -3e38, np.float32),
        "same": (part[:, None] // 8 == part[None, :] // 8).astype(np.float32),
        "before": ((part[:, None] // 8 == part[None, :] // 8) & (part[:, None] < part[None, :])).astype(np.float32),
        "allb": (part[:, None] < part[None, :]).astype(np.float32),
        "iota": rep(np.arange(SLOTS, dtype=np.float32)),
        "idf": tokid.astype(np.float32),
        "bits": np.broadcast_to((np.uint32(1) << np.arange(31, -1, -1, dtype=np.uint32)).view(np.int32), (128, 32)),
        "fw1": f["L0_ffn_w1"].reshape(KC, 128, FF).transpose(1, 0, 2), "fb1": f["L0_ffn_b1"].reshape(NHB, 128).T,
        "fw2": f["L0_ffn_w2"].reshape(NHB, 128, C).transpose(1, 0, 2), "fb2": rep(f["L0_ffn_b2"]),
    }


def kernel(**inputs):
    import numpy as np
    import concourse.bacc as bacc
    from concourse.bass_utils import run_bass_kernel_spmd

    nc = bacc.Bacc("TRN2", target_bir_lowering=False, num_devices=1)
    arrays, A = {}, {}
    for name, a in lay_out(inputs).items():
        a = np.ascontiguousarray(a)
        arrays[f"in_{name}"] = a
        A[name] = nc.dram_tensor(f"in_{name}", a.shape, mybir.dt.from_np(a.dtype), kind="ExternalInput").ap()
    A["out"] = nc.dram_tensor("out_h", (NB, NTOK, C), F32, kind="ExternalOutput").ap()
    A["out_rows"] = A["out"].rearrange("b n c -> (b n) c")
    A["x2d"] = nc.dram_tensor("x2_scratch", (NB, NTOK, C), F32).ap()
    A["wd"] = nc.dram_tensor("w_scratch", (NB, 8 * SEG), F32).ap()
    A["clsd"] = nc.dram_tensor("cls_scratch", (NB, C), F32).ap()
    attention_program(nc, A)
    with ExitStack() as ctx:
        ids = select_program(nc, A, ctx)
        feed_forward_program(nc, A, ids)
    r = run_bass_kernel_spmd(nc, [arrays], core_ids=[0])
    return r.results[0]["out_h"]
```
